# Optimizing a Trainium2 kernel written in Bass

```python
import numpy as np
import jax
import jax.numpy as jnp

def _softmax(x, axis=-1):
    return jax.nn.softmax(x, axis=axis)

def _gelu(x):
    return jax.nn.gelu(x, approximate=True)

def _silu(x):
    return jax.nn.silu(x)

def _sigmoid(x):
    return jax.nn.sigmoid(x)

def _layernorm(x, axis=-1, eps=1e-05):
    m = jnp.mean(x, axis=axis, keepdims=True)
    v = jnp.var(x, axis=axis, keepdims=True)
    return (x - m) / jnp.sqrt(v + eps)

def _scatter_add(tgt, idx, src, axis=0):
    return tgt.at[idx].add(src)

def _segment_sum(src, seg, n):
    return jax.ops.segment_sum(src, seg, n)
kernel_name = 'mk_xattn_ffn_d4_seqx_r4_92bfa8'

def setup_inputs(seed: int=0):
    np.random.seed(seed)
    _w = jnp.asarray

    def _rec_inputs():
        import jax
        import jax.numpy as jnp
        _rk = jax.random.key(seed)
        x = -0.0002928 + 1 * jax.random.normal(jax.random.fold_in(_rk, 1), (16, 128, 256), jnp.float32)
        _lenS = 128 - jax.random.randint(jax.random.fold_in(_rk, 7), (16,), 0, max(1, 128 // 4) + 1, jnp.int32)
        _lenS2 = 128 - jax.random.randint(jax.random.fold_in(_rk, 8), (16,), 0, max(1, 128 // 4) + 1, jnp.int32)
        _ctx_1024P = jax.random.normal(jax.random.fold_in(_rk, 11), (16, 16, 256), jnp.float32)
        _ctx_1024c = jax.random.dirichlet(jax.random.fold_in(_rk, 511), 0.3 * jnp.ones((16,), jnp.float32), (16, 128))
        _ctx_1024t = jnp.einsum('bsk,bkd->bsd', _ctx_1024c, _ctx_1024P)
        _ctx_1024t = _ctx_1024t * jax.lax.rsqrt(jnp.mean(jnp.square(_ctx_1024t)) + 1e-12) * 0.953939
        ctx_1024 = -1.39393e-06 + 0.999914 * (_ctx_1024t + 0.3 * jax.random.normal(jax.random.fold_in(_rk, 611), (16, 128, 256), jnp.float32))
        _validS = jnp.arange(128)[None, :] < _lenS[:, None]
        _validS2 = jnp.arange(128)[None, :] < _lenS2[:, None]
        _causal = jnp.tril(jnp.ones((128, 128), dtype=bool))
        mask_1x1xSxS2_bk0 = jnp.logical_not(jnp.broadcast_to(_validS2[0:1, None, None, :], (1, 1, 128, 128)))
        return (x, ctx_1024, mask_1x1xSxS2_bk0)
    x, ctx_1024, mask_1x1xSxS2_bk0 = _rec_inputs()

    def _L0_xattn_setup():
        import jax, jax.numpy as jnp
        import numpy as np
        D_MODEL = 256
        N_HEADS = 16
        HEAD_DIM = D_MODEL // N_HEADS
        key = jax.random.key(seed)
        ks = jax.random.split(key, 11)
        B, S, D = (2, 512, D_MODEL)
        scale = 1.0 / np.sqrt(D)
        return {'q': jax.random.normal(ks[0], (B, S, D), jnp.float32), 'k': jax.random.normal(ks[1], (B, S, D), jnp.float32), 'v': jax.random.normal(ks[2], (B, S, D), jnp.float32), 'Wq': jax.random.normal(ks[3], (D, D), jnp.float32) * scale, 'bq': jnp.zeros((D,), jnp.float32), 'Wk': jax.random.normal(ks[4], (D, D), jnp.float32) * scale, 'bk': jnp.zeros((D,), jnp.float32), 'Wv': jax.random.normal(ks[5], (D, D), jnp.float32) * scale, 'bv': jnp.zeros((D,), jnp.float32), 'Wo': jax.random.normal(ks[6], (D, D), jnp.float32) * scale, 'bo': jnp.zeros((D,), jnp.float32)}
    _L0_xattn_all = _L0_xattn_setup()
    _L0_xattn_in = {k: v for k, v in _L0_xattn_all.items() if k in ('Wq', 'bq', 'Wk', 'bk', 'Wv', 'bv', 'Wo', 'bo')}
    del _L0_xattn_all

    def _L0_ffn_setup():
        import jax, jax.numpy as jnp
        import numpy as np
        QMAX = 127.0

        def _ste_round(v):
            return v + jax.lax.stop_gradient(jnp.round(v) - v)

        def _act_fake_quant(x, clip_factor):
            scale = jax.nn.sigmoid(clip_factor) * jnp.max(jnp.abs(x)) / QMAX
            return jnp.clip(_ste_round(x / scale), -QMAX - 1.0, QMAX) * scale

        def _weight_fake_quant(w):
            scale = jnp.max(jnp.abs(w), axis=1, keepdims=True) / QMAX
            return jnp.clip(_ste_round(w / scale), -QMAX - 1.0, QMAX) * scale
        key = jax.random.key(seed)
        k1, k2, k3, k4 = jax.random.split(key, 4)
        B, S, H, I = (8, 2048, 256, 704)
        return {'x': jax.random.normal(k1, (B, S, H), dtype=jnp.float32), 'clip_x': jnp.full((1,), 4.0, dtype=jnp.float32), 'clip_down': jnp.full((1,), 4.0, dtype=jnp.float32), 'w_gate': jax.random.normal(k2, (I, H), dtype=jnp.float32) * 0.02, 'w_up': jax.random.normal(k3, (I, H), dtype=jnp.float32) * 0.02, 'w_down': jax.random.normal(k4, (H, I), dtype=jnp.float32) * 0.02}
    _L0_ffn_all = _L0_ffn_setup()
    _L0_ffn_in = {k: v for k, v in _L0_ffn_all.items() if k in ('clip_x', 'clip_down', 'w_gate', 'w_up', 'w_down')}
    del _L0_ffn_all

    def _L1_xattn_setup():
        import jax, jax.numpy as jnp
        import numpy as np
        import math
        HEADS = 16
        D_MODEL = 256
        D_K = D_MODEL // HEADS
        PRUNE_KEEP = 0.9

        def _split_heads(x, B):
            return x.reshape(B, -1, HEADS, D_K).transpose(0, 2, 1, 3)

        def _pruned_attention(q, k, v):
            B, H, S, _ = q.shape
            scores = jnp.einsum('bhqd,bhkd->bhqk', q, k) / math.sqrt(D_K)
            scores = jax.nn.softmax(scores, axis=-1)
            keep = int(S * PRUNE_KEEP)
            col_sum = jnp.sum(scores, axis=2)
            _, idx = jax.lax.top_k(col_sum, keep)
            mask = jnp.zeros((B, H, S), scores.dtype).at[jnp.arange(B)[:, None, None], jnp.arange(H)[None, :, None], idx].set(1.0)
            pruned = scores * mask[:, :, None, :]
            return jnp.einsum('bhqk,bhkd->bhqd', pruned, v)
        key = jax.random.key(seed)
        ks = jax.random.split(key, 12)
        B, S = (2, 512)
        sc = 0.02
        return {'q': jax.random.normal(ks[0], (B, S, D_MODEL), jnp.float32), 'k': jax.random.normal(ks[1], (B, S, D_MODEL), jnp.float32), 'v': jax.random.normal(ks[2], (B, S, D_MODEL), jnp.float32), 'Wq': jax.random.normal(ks[3], (D_MODEL, D_MODEL), jnp.float32) * sc, 'bq': jnp.zeros((D_MODEL,), jnp.float32), 'Wk': jax.random.normal(ks[4], (D_MODEL, D_MODEL), jnp.float32) * sc, 'bk': jnp.zeros((D_MODEL,), jnp.float32), 'Wv': jax.random.normal(ks[5], (D_MODEL, D_MODEL), jnp.float32) * sc, 'bv': jnp.zeros((D_MODEL,), jnp.float32), 'Wo': jax.random.normal(ks[6], (D_MODEL, D_MODEL), jnp.float32) * sc, 'bo': jnp.zeros((D_MODEL,), jnp.float32)}
    _L1_xattn_all = _L1_xattn_setup()
    _L1_xattn_in = {k: v for k, v in _L1_xattn_all.items() if k in ('Wq', 'bq', 'Wk', 'bk', 'Wv', 'bv', 'Wo', 'bo')}
    del _L1_xattn_all

    def _L1_ffn_setup():
        import jax, jax.numpy as jnp
        import numpy as np
        EPS = 1e-05

        def rmsnorm(x):
            return x * jax.lax.rsqrt(jnp.mean(x * x, axis=-1, keepdims=True) + EPS)

        def act_quant(x):
            scale = 127.0 / jnp.clip(jnp.max(jnp.abs(x), axis=-1, keepdims=True), 1e-05)
            q = jnp.clip(jnp.round(x * scale), -128.0, 127.0) / scale
            return x + jax.lax.stop_gradient(q - x)

        def weight_quant(w):
            scale = 1.0 / jnp.clip(jnp.mean(jnp.abs(w)), 1e-05)
            q = jnp.clip(jnp.round(w * scale), -1.0, 1.0) / scale
            return w + jax.lax.stop_gradient(q - w)

        def bitlinear(x, w, b):
            xq = act_quant(rmsnorm(x))
            wq = weight_quant(w)
            return jnp.einsum('bsd,fd->bsf', xq, wq) + b
        key = jax.random.key(seed)
        k0, k1, k2 = jax.random.split(key, 3)
        B, S, D, F = (2, 2048, 256, 1024)
        x = jax.random.normal(k0, (B, S, D), dtype=jnp.float32)
        w1 = jax.random.normal(k1, (F, D), dtype=jnp.float32) * (1.0 / np.sqrt(D))
        b1 = jnp.zeros((F,), dtype=jnp.float32)
        w2 = jax.random.normal(k2, (D, F), dtype=jnp.float32) * (1.0 / np.sqrt(F))
        b2 = jnp.zeros((D,), dtype=jnp.float32)
        return {'x': x, 'w1': w1, 'b1': b1, 'w2': w2, 'b2': b2}
    _L1_ffn_all = _L1_ffn_setup()
    _L1_ffn_in = {k: v for k, v in _L1_ffn_all.items() if k in ('w1', 'b1', 'w2', 'b2')}
    del _L1_ffn_all

    def _L2_xattn_setup():
        import jax, jax.numpy as jnp
        import numpy as np
        import math
        D_MODEL = 256
        NUM_HEADS = 16
        D_K = D_MODEL // NUM_HEADS
        key = jax.random.key(seed)
        ks = jax.random.split(key, 12)
        B, S = (2, 512)
        s = 1.0 / math.sqrt(D_MODEL)
        inp = {'q': jax.random.normal(ks[0], (B, S, D_MODEL), jnp.float32), 'k': jax.random.normal(ks[1], (B, S, D_MODEL), jnp.float32), 'v': jax.random.normal(ks[2], (B, S, D_MODEL), jnp.float32), 'mask': jnp.tril(jnp.ones((S, S), dtype=bool))[None, None, :, :], 'Wq': jax.random.normal(ks[3], (D_MODEL, D_MODEL), jnp.float32) * s, 'bq': jax.random.normal(ks[4], (D_MODEL,), jnp.float32) * s, 'Wk': jax.random.normal(ks[5], (D_MODEL, D_MODEL), jnp.float32) * s, 'bk': jax.random.normal(ks[6], (D_MODEL,), jnp.float32) * s, 'Wv': jax.random.normal(ks[7], (D_MODEL, D_MODEL), jnp.float32) * s, 'bv': jax.random.normal(ks[8], (D_MODEL,), jnp.float32) * s, 'Wo': jax.random.normal(ks[9], (D_MODEL, D_MODEL), jnp.float32) * s, 'bo': jax.random.normal(ks[10], (D_MODEL,), jnp.float32) * s}
        return inp
    _L2_xattn_all = _L2_xattn_setup()
    _L2_xattn_in = {k: v for k, v in _L2_xattn_all.items() if k in ('Wq', 'bq', 'Wk', 'bk', 'Wv', 'bv', 'Wo', 'bo')}
    del _L2_xattn_all

    def _L2_ffn_setup():
        import jax, jax.numpy as jnp
        import numpy as np
        B, S, D_MODEL, D_FF, E, R, TOP_K = (4, 512, 256, 1024, 8, 16, 2)
        key = jax.random.key(seed)
        ks = jax.random.split(key, 9)
        sd = 1.0 / np.sqrt(D_MODEL)
        return {'hidden_states': jax.random.normal(ks[0], (B, S, D_MODEL), jnp.float32), 'wi': jax.random.normal(ks[1], (D_FF, D_MODEL), jnp.float32) * sd, 'bi': jax.random.normal(ks[2], (D_FF,), jnp.float32) * 0.01, 'wo': jax.random.normal(ks[3], (D_MODEL, D_FF), jnp.float32) * (1.0 / np.sqrt(D_FF)), 'bo': jax.random.normal(ks[4], (D_MODEL,), jnp.float32) * 0.01, 'lora_A': jax.random.normal(ks[5], (E, R, D_MODEL), jnp.float32) * sd, 'lora_B': jax.random.normal(ks[6], (E, D_FF, R), jnp.float32) * 0.02, 'gate_w': jax.random.normal(ks[7], (E, D_MODEL), jnp.float32) * sd, 'gate_b': jax.random.normal(ks[8], (E,), jnp.float32) * 0.01}
    _L2_ffn_all = _L2_ffn_setup()
    _L2_ffn_in = {k: v for k, v in _L2_ffn_all.items() if k in ('wi', 'bi', 'wo', 'bo', 'lora_A', 'lora_B', 'gate_w', 'gate_b')}
    del _L2_ffn_all

    def _L3_xattn_setup():
        import jax, jax.numpy as jnp
        import numpy as np
        EPS = 1e-06

        def _rmsnorm(x, w, eps=EPS):
            x32 = x.astype(jnp.float32)
            var = jnp.mean(x32 * x32, axis=-1, keepdims=True)
            return (x32 * jax.lax.rsqrt(var + eps)).astype(x.dtype) * w
        key = jax.random.key(seed)
        ks = jax.random.split(key, 6)
        B, S, K, H = (4, 512, 64, 256)
        return {'hidden_states': jax.random.normal(ks[0], (B, S, H), jnp.float32), 'memory_state': jax.random.normal(ks[1], (B, K, H), jnp.float32), 'q_w': jax.random.normal(ks[2], (H, H), jnp.float32) * (1.0 / np.sqrt(H)), 'k_w': jax.random.normal(ks[3], (H, H), jnp.float32) * (1.0 / np.sqrt(H)), 'norm_w': jnp.ones((H,), jnp.float32), 'gate_w': jax.random.normal(ks[4], (H, H), jnp.float32) * 0.02, 'gate_b': jnp.zeros((H,), jnp.float32)}
    _L3_xattn_all = _L3_xattn_setup()
    _L3_xattn_in = {k: v for k, v in _L3_xattn_all.items() if k in ('q_w', 'k_w', 'norm_w', 'gate_w', 'gate_b')}
    del _L3_xattn_all

    def _L3_ffn_setup():
        import jax, jax.numpy as jnp
        import numpy as np
        N_HEADS = 16
        NUM_EXPERTS = 4
        TOP_K = 2
        D_MODEL = 256
        GATE_HID = 128
        key = jax.random.key(seed)
        ks = jax.random.split(key, 12)
        B, T, C, E = (2, 256, D_MODEL, NUM_EXPERTS)
        s = 1.0 / np.sqrt(C)
        return {'hidden_states': jax.random.normal(ks[0], (B, T, C), jnp.float32), 'Wq': jax.random.normal(ks[1], (E, C, C), jnp.float32) * s, 'bq': jnp.zeros((E, C), jnp.float32), 'Wk': jax.random.normal(ks[2], (E, C, C), jnp.float32) * s, 'bk': jnp.zeros((E, C), jnp.float32), 'Wv': jax.random.normal(ks[3], (E, C, C), jnp.float32) * s, 'bv': jnp.zeros((E, C), jnp.float32), 'Wg1': jax.random.normal(ks[4], (C, GATE_HID), jnp.float32) * s, 'bg1': jnp.zeros((GATE_HID,), jnp.float32), 'Wg2': jax.random.normal(ks[5], (GATE_HID, E), jnp.float32) / np.sqrt(GATE_HID), 'bg2': jnp.zeros((E,), jnp.float32), 'Wo': jax.random.normal(ks[6], (C, C), jnp.float32) * s, 'bo': jnp.zeros((C,), jnp.float32)}
    _L3_ffn_all = _L3_ffn_setup()
    _L3_ffn_in = {k: v for k, v in _L3_ffn_all.items() if k in ('Wq', 'bq', 'Wk', 'bk', 'Wv', 'bv', 'Wg1', 'bg1', 'Wg2', 'bg2', 'Wo', 'bo')}
    del _L3_ffn_all
    return {'x': x, 'ctx_1024': ctx_1024, 'mask_1x1xSxS2_bk0': mask_1x1xSxS2_bk0, 'L0_xattn_Wq': _L0_xattn_in['Wq'], 'L0_xattn_bq': _L0_xattn_in['bq'], 'L0_xattn_Wk': _L0_xattn_in['Wk'], 'L0_xattn_bk': _L0_xattn_in['bk'], 'L0_xattn_Wv': _L0_xattn_in['Wv'], 'L0_xattn_bv': _L0_xattn_in['bv'], 'L0_xattn_Wo': _L0_xattn_in['Wo'], 'L0_xattn_bo': _L0_xattn_in['bo'], 'L0_ffn_clip_x': _L0_ffn_in['clip_x'], 'L0_ffn_clip_down': _L0_ffn_in['clip_down'], 'L0_ffn_w_gate': _L0_ffn_in['w_gate'], 'L0_ffn_w_up': _L0_ffn_in['w_up'], 'L0_ffn_w_down': _L0_ffn_in['w_down'], 'L1_xattn_Wq': _L1_xattn_in['Wq'], 'L1_xattn_bq': _L1_xattn_in['bq'], 'L1_xattn_Wk': _L1_xattn_in['Wk'], 'L1_xattn_bk': _L1_xattn_in['bk'], 'L1_xattn_Wv': _L1_xattn_in['Wv'], 'L1_xattn_bv': _L1_xattn_in['bv'], 'L1_xattn_Wo': _L1_xattn_in['Wo'], 'L1_xattn_bo': _L1_xattn_in['bo'], 'L1_ffn_w1': _L1_ffn_in['w1'], 'L1_ffn_b1': _L1_ffn_in['b1'], 'L1_ffn_w2': _L1_ffn_in['w2'], 'L1_ffn_b2': _L1_ffn_in['b2'], 'L2_xattn_Wq': _L2_xattn_in['Wq'], 'L2_xattn_bq': _L2_xattn_in['bq'], 'L2_xattn_Wk': _L2_xattn_in['Wk'], 'L2_xattn_bk': _L2_xattn_in['bk'], 'L2_xattn_Wv': _L2_xattn_in['Wv'], 'L2_xattn_bv': _L2_xattn_in['bv'], 'L2_xattn_Wo': _L2_xattn_in['Wo'], 'L2_xattn_bo': _L2_xattn_in['bo'], 'L2_ffn_wi': _L2_ffn_in['wi'], 'L2_ffn_bi': _L2_ffn_in['bi'], 'L2_ffn_wo': _L2_ffn_in['wo'], 'L2_ffn_bo': _L2_ffn_in['bo'], 'L2_ffn_lora_A': _L2_ffn_in['lora_A'], 'L2_ffn_lora_B': _L2_ffn_in['lora_B'], 'L2_ffn_gate_w': _L2_ffn_in['gate_w'], 'L2_ffn_gate_b': _L2_ffn_in['gate_b'], 'L3_xattn_q_w': _L3_xattn_in['q_w'], 'L3_xattn_k_w': _L3_xattn_in['k_w'], 'L3_xattn_norm_w': _L3_xattn_in['norm_w'], 'L3_xattn_gate_w': _L3_xattn_in['gate_w'], 'L3_xattn_gate_b': _L3_xattn_in['gate_b'], 'L3_ffn_Wq': _L3_ffn_in['Wq'], 'L3_ffn_bq': _L3_ffn_in['bq'], 'L3_ffn_Wk': _L3_ffn_in['Wk'], 'L3_ffn_bk': _L3_ffn_in['bk'], 'L3_ffn_Wv': _L3_ffn_in['Wv'], 'L3_ffn_bv': _L3_ffn_in['bv'], 'L3_ffn_Wg1': _L3_ffn_in['Wg1'], 'L3_ffn_bg1': _L3_ffn_in['bg1'], 'L3_ffn_Wg2': _L3_ffn_in['Wg2'], 'L3_ffn_bg2': _L3_ffn_in['bg2'], 'L3_ffn_Wo': _L3_ffn_in['Wo'], 'L3_ffn_bo': _L3_ffn_in['bo']}

def reference(x, ctx_1024, mask_1x1xSxS2_bk0, L0_xattn_Wq, L0_xattn_bq, L0_xattn_Wk, L0_xattn_bk, L0_xattn_Wv, L0_xattn_bv, L0_xattn_Wo, L0_xattn_bo, L0_ffn_clip_x, L0_ffn_clip_down, L0_ffn_w_gate, L0_ffn_w_up, L0_ffn_w_down, L1_xattn_Wq, L1_xattn_bq, L1_xattn_Wk, L1_xattn_bk, L1_xattn_Wv, L1_xattn_bv, L1_xattn_Wo, L1_xattn_bo, L1_ffn_w1, L1_ffn_b1, L1_ffn_w2, L1_ffn_b2, L2_xattn_Wq, L2_xattn_bq, L2_xattn_Wk, L2_xattn_bk, L2_xattn_Wv, L2_xattn_bv, L2_xattn_Wo, L2_xattn_bo, L2_ffn_wi, L2_ffn_bi, L2_ffn_wo, L2_ffn_bo, L2_ffn_lora_A, L2_ffn_lora_B, L2_ffn_gate_w, L2_ffn_gate_b, L3_xattn_q_w, L3_xattn_k_w, L3_xattn_norm_w, L3_xattn_gate_w, L3_xattn_gate_b, L3_ffn_Wq, L3_ffn_bq, L3_ffn_Wk, L3_ffn_bk, L3_ffn_Wv, L3_ffn_bv, L3_ffn_Wg1, L3_ffn_bg1, L3_ffn_Wg2, L3_ffn_bg2, L3_ffn_Wo, L3_ffn_bo):
    import jax
    import jax.numpy as jnp

    def _L0_xattn_ref(q, k, v, Wq, bq, Wk, bk, Wv, bv, Wo, bo):
        import jax, jax.numpy as jnp
        import numpy as np
        D_MODEL = 256
        N_HEADS = 16
        HEAD_DIM = D_MODEL // N_HEADS
        B, S, D = q.shape
        H, Hd = (N_HEADS, HEAD_DIM)

        def split_heads(x):
            return x.reshape(B, S, H, Hd).transpose(0, 2, 1, 3)
        qh = split_heads(q @ Wq + bq)
        kh = split_heads(k @ Wk + bk)
        vh = split_heads(v @ Wv + bv)
        scores = jnp.einsum('bhqd,bhkd->bhqk', qh, kh) / jnp.sqrt(jnp.float32(Hd))
        probs = jax.nn.softmax(scores, axis=-1)
        ctx = jnp.einsum('bhqk,bhkd->bhqd', probs, vh)
        out = ctx.transpose(0, 2, 1, 3).reshape(B, S, D)
        return out @ Wo + bo

    def _L0_ffn_ref(x, clip_x, clip_down, w_gate, w_up, w_down):
        import jax, jax.numpy as jnp
        import numpy as np
        QMAX = 127.0

        def _ste_round(v):
            return v + jax.lax.stop_gradient(jnp.round(v) - v)

        def _act_fake_quant(x, clip_factor):
            scale = jax.nn.sigmoid(clip_factor) * jnp.max(jnp.abs(x)) / QMAX
            return jnp.clip(_ste_round(x / scale), -QMAX - 1.0, QMAX) * scale

        def _weight_fake_quant(w):
            scale = jnp.max(jnp.abs(w), axis=1, keepdims=True) / QMAX
            return jnp.clip(_ste_round(w / scale), -QMAX - 1.0, QMAX) * scale
        xq = _act_fake_quant(x, clip_x[0])
        gate = jnp.einsum('bsh,ih->bsi', xq, _weight_fake_quant(w_gate))
        up = jnp.einsum('bsh,ih->bsi', xq, _weight_fake_quant(w_up))
        h = _act_fake_quant(jax.nn.silu(gate) * up, clip_down[0])
        return jnp.einsum('bsi,hi->bsh', h, _weight_fake_quant(w_down))

    def _L1_xattn_ref(q, k, v, Wq, bq, Wk, bk, Wv, bv, Wo, bo):
        import jax, jax.numpy as jnp
        import numpy as np
        import math
        HEADS = 16
        D_MODEL = 256
        D_K = D_MODEL // HEADS
        PRUNE_KEEP = 0.9

        def _split_heads(x, B):
            return x.reshape(B, -1, HEADS, D_K).transpose(0, 2, 1, 3)

        def _pruned_attention(q, k, v):
            B, H, S, _ = q.shape
            scores = jnp.einsum('bhqd,bhkd->bhqk', q, k) / math.sqrt(D_K)
            scores = jax.nn.softmax(scores, axis=-1)
            keep = int(S * PRUNE_KEEP)
            col_sum = jnp.sum(scores, axis=2)
            _, idx = jax.lax.top_k(col_sum, keep)
            mask = jnp.zeros((B, H, S), scores.dtype).at[jnp.arange(B)[:, None, None], jnp.arange(H)[None, :, None], idx].set(1.0)
            pruned = scores * mask[:, :, None, :]
            return jnp.einsum('bhqk,bhkd->bhqd', pruned, v)
        B = q.shape[0]
        qh = _split_heads(q @ Wq.T + bq, B)
        kh = _split_heads(k @ Wk.T + bk, B)
        vh = _split_heads(v @ Wv.T + bv, B)
        out = _pruned_attention(qh, kh, vh)
        concat = out.transpose(0, 2, 1, 3).reshape(B, -1, D_MODEL)
        return concat @ Wo.T + bo

    def _L1_ffn_ref(x, w1, b1, w2, b2):
        import jax, jax.numpy as jnp
        import numpy as np
        EPS = 1e-05

        def rmsnorm(x):
            return x * jax.lax.rsqrt(jnp.mean(x * x, axis=-1, keepdims=True) + EPS)

        def act_quant(x):
            scale = 127.0 / jnp.clip(jnp.max(jnp.abs(x), axis=-1, keepdims=True), 1e-05)
            q = jnp.clip(jnp.round(x * scale), -128.0, 127.0) / scale
            return x + jax.lax.stop_gradient(q - x)

        def weight_quant(w):
            scale = 1.0 / jnp.clip(jnp.mean(jnp.abs(w)), 1e-05)
            q = jnp.clip(jnp.round(w * scale), -1.0, 1.0) / scale
            return w + jax.lax.stop_gradient(q - w)

        def bitlinear(x, w, b):
            xq = act_quant(rmsnorm(x))
            wq = weight_quant(w)
            return jnp.einsum('bsd,fd->bsf', xq, wq) + b
        h = bitlinear(x, w1, b1)
        h = jax.nn.gelu(h, approximate=False)
        return bitlinear(h, w2, b2)

    def _L2_xattn_ref(q, k, v, mask, Wq, bq, Wk, bk, Wv, bv, Wo, bo):
        import jax, jax.numpy as jnp
        import numpy as np
        import math
        D_MODEL = 256
        NUM_HEADS = 16
        D_K = D_MODEL // NUM_HEADS
        B, S, _ = q.shape

        def proj(x, W, b):
            y = x @ W.T + b
            return y.reshape(B, -1, NUM_HEADS, D_K).transpose(0, 2, 1, 3)
        Q = proj(q, Wq, bq)
        K = proj(k, Wk, bk)
        V = proj(v, Wv, bv)
        scores = jnp.einsum('bhqd,bhkd->bhqk', Q, K) / math.sqrt(D_K)
        scores = jnp.where(mask, scores, jnp.float32(-1000000000.0))
        probs = jax.nn.softmax(scores, axis=-1)
        attn = jnp.einsum('bhqk,bhkd->bhqd', probs, V)
        attn = attn.transpose(0, 2, 1, 3).reshape(B, S, D_MODEL)
        return attn @ Wo.T + bo

    def _L2_ffn_ref(hidden_states, wi, bi, wo, bo, lora_A, lora_B, gate_w, gate_b):
        import jax, jax.numpy as jnp
        import numpy as np
        B, S, D_MODEL, D_FF, E, R, TOP_K = (4, 512, 256, 1024, 8, 16, 2)
        logits = jnp.einsum('bsd,ed->bse', hidden_states, gate_w) + gate_b
        scores = jax.nn.softmax(logits, axis=-1)
        top_v, top_i = jax.lax.top_k(scores, TOP_K)
        val_sum = top_v.sum(axis=-1)
        out = jnp.zeros_like(hidden_states)
        for e in range(E):
            count = (top_i == e).sum(axis=-1).astype(hidden_states.dtype)
            gate = count * val_sum
            inter = jnp.einsum('bsd,fd->bsf', hidden_states, wi) + bi + jnp.einsum('bsr,fr->bsf', jnp.einsum('bsd,rd->bsr', hidden_states, lora_A[e]), lora_B[e])
            h = jax.nn.relu(inter)
            expert_out = jnp.einsum('bsf,df->bsd', h, wo) + bo
            out = out + gate[..., None] * expert_out
        return out

    def _L3_xattn_ref(hidden_states, memory_state, q_w, k_w, norm_w, gate_w, gate_b):
        import jax, jax.numpy as jnp
        import numpy as np
        EPS = 1e-06

        def _rmsnorm(x, w, eps=EPS):
            x32 = x.astype(jnp.float32)
            var = jnp.mean(x32 * x32, axis=-1, keepdims=True)
            return (x32 * jax.lax.rsqrt(var + eps)).astype(x.dtype) * w
        B, S, H = hidden_states.shape
        K = memory_state.shape[1]
        scale = 1.0 / np.sqrt(H)
        normed = _rmsnorm(hidden_states, norm_w)
        v_pool = jnp.concatenate([normed, memory_state], axis=1)
        q = jnp.einsum('bsh,oh->bso', normed, q_w)
        k = jnp.einsum('bth,oh->bto', v_pool, k_w)
        logits = jnp.einsum('bsd,btd->bst', q, k) * scale
        local = jnp.tril(jnp.ones((S, S), bool))
        mask = jnp.concatenate([local, jnp.ones((S, K), bool)], axis=1)
        logits = jnp.where(mask[None], logits, -jnp.inf)
        attn = jax.nn.softmax(logits, axis=-1)
        h_tilde = jnp.einsum('bst,bth->bsh', attn, v_pool)
        alpha = jax.nn.sigmoid(jnp.einsum('bsh,oh->bso', hidden_states, gate_w) + gate_b)
        return (1.0 - alpha) * hidden_states + alpha * h_tilde

    def _L3_ffn_ref(hidden_states, Wq, bq, Wk, bk, Wv, bv, Wg1, bg1, Wg2, bg2, Wo, bo):
        import jax, jax.numpy as jnp
        import numpy as np
        N_HEADS = 16
        NUM_EXPERTS = 4
        TOP_K = 2
        D_MODEL = 256
        GATE_HID = 128
        B, T, C = hidden_states.shape
        H = N_HEADS
        D = C // H
        pooled = hidden_states.mean(axis=1)
        logits = jax.nn.relu(pooled @ Wg1 + bg1) @ Wg2 + bg2
        vals, idx = jax.lax.top_k(logits, TOP_K)
        sm = jax.nn.softmax(vals, axis=-1)
        weights = jnp.zeros_like(logits).at[jnp.arange(B)[:, None], idx].set(sm)

        def moe_proj(W, b):
            Wc = jnp.einsum('be,ecd->bcd', weights, W)
            bc = weights @ b
            return jnp.einsum('btc,bcd->btd', hidden_states, Wc) + bc[:, None, :]
        q = moe_proj(Wq, bq).reshape(B, T, H, D)
        k = moe_proj(Wk, bk).reshape(B, T, H, D)
        v = moe_proj(Wv, bv).reshape(B, T, H, D)
        scores = jnp.einsum('bthd,bshd->bhts', q, k) / np.sqrt(D).astype(np.float32)
        attn = jax.nn.softmax(scores, axis=-1)
        out = jnp.einsum('bhts,bshd->bthd', attn, v).reshape(B, T, C)
        return out @ Wo + bo
    x = x + _L0_xattn_ref(_layernorm(x, axis=-1), ctx_1024, ctx_1024, L0_xattn_Wq, L0_xattn_bq, L0_xattn_Wk, L0_xattn_bk, L0_xattn_Wv, L0_xattn_bv, L0_xattn_Wo, L0_xattn_bo)
    x = x + _L0_ffn_ref(_layernorm(x, axis=-1), L0_ffn_clip_x, L0_ffn_clip_down, L0_ffn_w_gate, L0_ffn_w_up, L0_ffn_w_down)
    x = x + _L1_xattn_ref(_layernorm(x, axis=-1), ctx_1024, ctx_1024, L1_xattn_Wq, L1_xattn_bq, L1_xattn_Wk, L1_xattn_bk, L1_xattn_Wv, L1_xattn_bv, L1_xattn_Wo, L1_xattn_bo)
    x = x + _L1_ffn_ref(_layernorm(x, axis=-1), L1_ffn_w1, L1_ffn_b1, L1_ffn_w2, L1_ffn_b2)
    x = x + _L2_xattn_ref(_layernorm(x, axis=-1), ctx_1024, ctx_1024, mask_1x1xSxS2_bk0, L2_xattn_Wq, L2_xattn_bq, L2_xattn_Wk, L2_xattn_bk, L2_xattn_Wv, L2_xattn_bv, L2_xattn_Wo, L2_xattn_bo)
    x = x + _L2_ffn_ref(_layernorm(x, axis=-1), L2_ffn_wi, L2_ffn_bi, L2_ffn_wo, L2_ffn_bo, L2_ffn_lora_A, L2_ffn_lora_B, L2_ffn_gate_w, L2_ffn_gate_b)
    x = x + _L3_xattn_ref(_layernorm(x, axis=-1), ctx_1024, L3_xattn_q_w, L3_xattn_k_w, L3_xattn_norm_w, L3_xattn_gate_w, L3_xattn_gate_b)
    x = x + _L3_ffn_ref(_layernorm(x, axis=-1), L3_ffn_Wq, L3_ffn_bq, L3_ffn_Wk, L3_ffn_bk, L3_ffn_Wv, L3_ffn_bv, L3_ffn_Wg1, L3_ffn_bg1, L3_ffn_Wg2, L3_ffn_bg2, L3_ffn_Wo, L3_ffn_bo)
    return x

_drawn_inputs = setup_inputs


def setup_inputs(seed=0):
    import zlib

    import numpy as np

    out = dict(_drawn_inputs(seed))
    spreads = {'L0_xattn_bq': (0.0, 0.34),
     'L0_xattn_bk': (0.0, 0.8),
     'L0_xattn_bv': (0.0, 0.1),
     'L0_xattn_bo': (0.0, 0.1),
     'L1_xattn_bq': (0.0, 0.8),
     'L1_xattn_bk': (0.0, 0.8),
     'L1_xattn_bv': (0.0, 0.1),
     'L1_xattn_bo': (0.0, 0.1),
     'L1_ffn_b1': (0.0, 0.1),
     'L1_ffn_b2': (0.0, 0.1),
     'L3_xattn_norm_w': (1.0, 0.6),
     'L3_xattn_gate_b': (0.0, 0.711),
     'L3_ffn_bq': (0.0, 0.8),
     'L3_ffn_bk': (0.0, 0.8),
     'L3_ffn_bv': (0.0, 0.1),
     'L3_ffn_bg1': (0.0, 0.1),
     'L3_ffn_bg2': (0.0, 0.8),
     'L3_ffn_bo': (0.0, 0.1)}
    factors = {'L1_xattn_Wq': 6.699,
     'L1_xattn_Wk': 6.396,
     'L2_ffn_bi': 8.0,
     'L2_ffn_bo': 7.859,
     'L2_ffn_gate_b': 8.0,
     'L3_ffn_Wq': 4.436,
     'L3_ffn_Wk': 4.341}
    for name, (base, spread) in spreads.items():
        noise = np.random.default_rng([zlib.crc32(name.encode()), seed]).standard_normal(out[name].shape)
        drawn = base * np.exp(spread * noise) if base else spread * noise
        out[name] = jnp.asarray(drawn.astype(out[name].dtype))
    for name, factor in factors.items():
        out[name] = (out[name] * factor).astype(out[name].dtype)
    return out
```

```python
from contextlib import ExitStack

import concourse.bass as bass
from concourse import mybir

F32 = mybir.dt.float32
BF16 = mybir.dt.bfloat16
U8 = mybir.dt.uint8
I32 = mybir.dt.int32
ALU = mybir.AluOpType
ACT = mybir.ActivationFunctionType
AX = mybir.AxisListType

P = 128
NB = 16
D = 256
DC = D // P
NH = 16
DH = D // NH
HC = NH // DC
NQ = 4
HQ = NH // NQ
NS = 2
TURNS = NB // NS
BANK = 512
LN_EPS = 1e-5
BIG = 3.0e38
MAGIC = 1.5 * 2.0 ** 23
KEEP = int(P * 0.9)
NDROP = P - KEEP
PADS = 64


class Section:

    def __init__(self, nc, name):
        self.nc, self.name, self.ctx, self.sems = nc, name, ExitStack(), []

    def __enter__(self):
        return self

    def sb(self, name, shape, dt=F32):
        return self.ctx.enter_context(self.nc.sbuf_tensor(f"{self.name}_{name}", shape, dt))

    def ps(self, name, shape, dt=F32):
        return self.ctx.enter_context(self.nc.psum_tensor(f"{self.name}_{name}", shape, dt))

    def sem(self, name):
        s = self.nc.alloc_semaphore(f"{self.name}_{name}")
        self.sems.append(s)
        return s

    def per_stream(self, name):
        return [self.sem(f"{name}{s}") for s in range(NS)]

    def block(self):
        return self.nc.Block()

    def __exit__(self, *exc):
        self.ctx.__exit__(*exc)
        if exc[0] is None and self.sems:
            self.nc.clear_and_free_semaphores(self.sems)
            self.nc.all_engine_barrier()
        return False


def arrived(eng, g, *groups):
    for what in groups:
        eng.wait_ge(g.loaded[what], 16 * g.counts[what])


def apart(dve, g):
    g.pads += 1
    n = g.pads % PADS
    dve.memset(g.pad[0:1, n:n + 1], 0.0)


class Turned:

    def __init__(self, sec, banks, jobs):
        self.banks, self.ps, self.sb = banks, sec.sem("turned_ps"), sec.sem("turned_sb")
        self.lots = [jobs[n:n + 4] for n in range(0, len(jobs), 4)]

    def tensor(self, pe, ident):
        for n, lot in enumerate(self.lots):
            if n >= 2:
                pe.wait_ge(self.sb, n - 1)
            for m, (src, _) in enumerate(lot):
                rows, cols = src.shape[0], src.shape[1]
                mm = pe.transpose(self.banks[n % 2][0:cols, m * P:m * P + rows], src, ident[0:rows, 0:rows])
            mm.then_inc(self.ps, 1)

    def scalar(self, act):
        for n, lot in enumerate(self.lots):
            act.wait_ge(self.ps, n + 1)
            for m, (src, dst) in enumerate(lot):
                rows, cols = src.shape[0], src.shape[1]
                cp = act.copy(dst, self.banks[n % 2][0:cols, m * P:m * P + rows])
            cp.then_inc(self.sb, 1)

    def wait(self, eng):
        eng.wait_ge(self.sb, len(self.lots))


class LayerNorm:

    def __init__(self, sec, g):
        self.g = g
        self.std, self.t1, self.t2 = sec.sb("ln_std", [P, NB]), sec.sb("ln_t1", [P, NB]), sec.sb("ln_t2", [P, NB])
        self.r0, self.rstd = sec.sb("ln_r0", [P, NB]), sec.sb("ln_rstd", [P, NB, 1])
        self.mv = sec.sb("ln_mv", [P, NB, 2])
        self.xn = [sec.sb(f"xn{s}", [P, D]) for s in range(NS)]
        self.s_aggr, self.s_std, self.s_step = sec.sem("ln_aggr"), sec.sem("ln_std"), sec.sem("ln_step")
        self.s_xn = sec.per_stream("xn")

    def vector_start(self, dve):
        for b in range(NB):
            ins = dve.bn_aggr(self.mv[:, b, :], self.g.stats[:, b, :])
        ins.then_inc(self.s_aggr, 1)
        var = self.mv[:, :, 1]
        dve.wait_ge(self.s_std, 1)
        dve.reciprocal(self.r0[:, :], self.std[:, :]).then_inc(self.s_step, 1)
        dve.wait_ge(self.s_step, 1)
        dve.scalar_tensor_tensor(out=self.t1[:, :], in0=var, scalar=LN_EPS, in1=self.r0[:, :], op0=ALU.add,
                                 op1=ALU.mult).then_inc(self.s_step, 1)
        dve.wait_ge(self.s_step, 2)
        dve.scalar_tensor_tensor(out=self.t2[:, :], in0=self.t1[:, :], scalar=-0.5, in1=self.r0[:, :],
                                 op0=ALU.mult, op1=ALU.mult).then_inc(self.s_step, 1)
        dve.wait_ge(self.s_step, 3)
        dve.scalar_tensor_tensor(out=self.rstd[:, :, 0], in0=self.t2[:, :], scalar=1.5, in1=self.r0[:, :],
                                 op0=ALU.add, op1=ALU.mult).then_inc(self.s_step, 1)
        dve.wait_ge(self.s_step, 4)

    def scalar_start(self, act):
        act.wait_ge(self.s_aggr, 1)
        act.activation(self.std[:, :], self.mv[:, :, 1], ACT.Sqrt, bias=self.g.eps[:, 0:1]).then_inc(self.s_std, 1)

    def vector_apply(self, dve, s, i):
        b = NS * (i - 1) + s
        dve.tensor_scalar(self.xn[s][:, :], self.g.x[:, b, :], self.mv[:, b, 0:1], self.rstd[:, b, :],
                          ALU.subtract, ALU.mult).then_inc(self.s_xn[s], 1)

    def vector_stats(self, dve, s, i, s_x):
        dve.wait_ge(s_x[s], i)
        apart(dve, self.g)
        dve.bn_stats(self.g.stats[:, NS * (i - 1) + s, :], tile_of(self.g, i, s))


class Rsqrt:
    STEPS = 12

    def __init__(self, sec, name, width):
        self.v, self.t, self.y = (sec.sb(f"{name}_{n}", [P, width]) for n in ("v", "t", "y"))
        self.u = sec.sb(f"{name}_u", [P, width])
        self.j = sec.sb(f"{name}_j", [P, width], I32)
        self.s = sec.sem(f"{name}_step")

    def vector(self, dve, src, scale, eps, i):
        n = Rsqrt.STEPS * (i - 1)

        def link(k, ins):
            ins.then_inc(self.s, 1)
            dve.wait_ge(self.s, n + k)
        v, t, u, y, j = self.v[:, :], self.t[:, :], self.u[:, :], self.y[:, :], self.j[:, :]
        link(1, dve.tensor_scalar(v, src, scale, eps, ALU.mult, ALU.add))
        link(2, dve.tensor_scalar(j, v.bitcast(I32), 1, None, ALU.arith_shift_right))
        link(3, dve.tensor_scalar(y.bitcast(I32), j, -1.0, float(0x5F3759DF), ALU.mult, ALU.add))
        for k in (4, 7, 10):
            link(k, dve.tensor_tensor(t, v, y, ALU.mult))
            link(k + 1, dve.scalar_tensor_tensor(out=u, in0=t, scalar=-0.5, in1=y, op0=ALU.mult, op1=ALU.mult))
            link(k + 2, dve.scalar_tensor_tensor(out=y, in0=u, scalar=1.5, in1=y, op0=ALU.add, op1=ALU.mult))
        return y


def tile_of(g, i, s):
    return g.x[:, NS * (i - 1) + s, :]


def banks_of(sec):
    return [[sec.ps(f"bank{s}_{n}", [P, BANK]) for n in range(4)] for s in range(NS)]


class Globals:
    pass


def setup(nc, g, a):
    sec = Section(nc, "setup")
    with sec:
        ctx_nat = sec.sb("ctx_nat", [P, NB, D])
        banks = banks_of(sec)
        s_const, s_zero = sec.sem("const"), sec.sem("zero")
        s_ps, s_sb = sec.sem("ctx_ps"), sec.sem("ctx_sb")
        s_ctx = sec.sem("ctx_in")
        flat = [banks[s][n] for n in range(4) for s in range(NS)]
        with sec.block() as block:
            @block.sync
            def _(sp):
                for q in range(4):
                    sp.dma_start(ctx_nat[:, 4 * q:4 * q + 4, :],
                                 a["ctx_1024"][4 * q:4 * q + 4].rearrange("b p d -> p b d")).then_inc(s_ctx, 16)
                sp.dma_start(g.x[:, :, :], a["x"].rearrange("b p d -> p b d")).then_inc(g.loaded["x"], 16)
                for dst, src, what in g.loads:
                    sp.dma_start(dst, src, allow_slow_non_contiguous=True).then_inc(g.loaded[what], 16)
                sp.wait_ge(g.loaded["x"], 16)

            @block.gpsimd
            def _(pool):
                pool.memset(g.ident[:, :], 0.0).then_inc(s_zero, 1)
                pool.memset(g.hmask[:, :], 1.0).then_inc(s_zero, 1)
                pool.memset(g.causal[:, :, :], 0.0).then_inc(s_zero, 1)
                pool.wait_ge(s_zero, 3)
                pool.affine_select(out=g.ident[:, :], in_=g.ident[:, :], compare_op=ALU.not_equal, fill=1.0,
                                   base=0, pattern=[[-1, P]], channel_multiplier=1).then_inc(s_const, 1)
                pool.affine_select(out=g.hmask[:, :], in_=g.hmask[:, :], compare_op=ALU.is_ge, fill=0.0,
                                   base=0, pattern=[[-DH, HC]], channel_multiplier=1).then_inc(s_zero, 1)
                pool.wait_ge(s_zero, 4)
                pool.affine_select(out=g.hmask[:, :], in_=g.hmask[:, :], compare_op=ALU.is_ge, fill=0.0,
                                   base=DH - 1, pattern=[[DH, HC]], channel_multiplier=-1).then_inc(s_const, 1)
                pool.affine_select(out=g.causal[:, 0, :], in_=g.causal[:, 0, :], compare_op=ALU.is_ge, fill=-BIG,
                                   base=0, pattern=[[-1, P]], channel_multiplier=1).then_inc(s_const, 1)

            @block.vector
            def _(dve):
                dve.memset(g.eps[:, :], LN_EPS).then_inc(s_const, 1)
                dve.memset(g.onesP[:, :], 1.0).then_inc(s_const, 1)
                dve.memset(g.magic[:, :], MAGIC).then_inc(s_const, 1)
                dve.wait_ge(g.loaded["x"], 16)
                for b in range(NB):
                    dve.bn_stats(g.stats[:, b, :], g.x[:, b, :])
                for e in range(8):
                    dve.memset(g.order[:, e:e + 1], 8.0 - e)
                dve.memset(g.far[:, :], -1e9 * DH ** 0.5)
                arrived(dve, g, "mask")
                dve.tensor_scalar(g.hidden[:, :], g.mask, 0.0, None, ALU.is_equal)
                for n in range(1, NB, 2):
                    dve.wait_ge(s_ps, n + 1)
                    dve.tensor_copy(g.ctxT[:, n, :, :], flat[n % 8][:, 0:D]
                                    .rearrange("p (c t) -> p c t", c=DC)).then_inc(s_sb, 1)

            @block.scalar
            def _(act):
                for n in range(0, NB, 2):
                    act.wait_ge(s_ps, n + 1)
                    act.copy(g.ctxT[:, n, :, :], flat[n % 8][:, 0:D]
                             .rearrange("p (c t) -> p c t", c=DC)).then_inc(s_sb, 1)

            @block.tensor
            def _(pe):
                pe.wait_ge(s_const, 6)
                for n in range(NB):
                    if n % 4 == 0:
                        pe.wait_ge(s_ctx, 16 * NB // 4)
                    if n == 8:
                        pe.wait_ge(s_sb, 8)
                    for c in range(DC):
                        mm = pe.transpose(flat[n % 8][:, c * P:c * P + P], ctx_nat[:, n, c * P:c * P + P],
                                          g.ident[:, :])
                    mm.then_inc(s_ps, 1)


PLAIN, PRUNED, MASKED, MIXED = range(4)


def attention(nc, g, name, kind, w, turned, needs):
    sec = Section(nc, name)
    with sec:
        ln = LayerNorm(sec, g)
        bank = banks_of(sec)
        sbs = lambda nm, shape, dt=F32: [sec.sb(f"{nm}{s}", shape, dt) for s in range(NS)]
        xT, ctxT, qT, kT = (sbs(n, [P, DC, P]) for n in ("xT", "ctxT", "qT", "kT"))
        v = sbs("v", [P, NH, DH + 1])
        kbd = sbs("kbd", [P, DC, HC, P])
        pr = sbs("pr", [P, 2, HQ, P])
        prT = sbs("prT", [P, NQ, HQ, P])
        mx = sbs("mx", [P, NH])
        rl = sbs("rl", [P, NH])
        on, oT = sbs("on", [P, NH, DH]), sbs("oT", [P, DC, P])
        S = [bank[s][0:2] for s in range(NS)]
        T = [bank[s][2] for s in range(NS)]
        M = [bank[s][3] for s in range(NS)]
        (s_ctx, s_xT_ps, s_xT, s_q_ps, s_k_ps, s_v_ps, s_q, s_k, s_v, s_kbd, s_sc, s_mx, s_sh, s_ex, s_tp,
         s_pt, s_av, s_rl, s_on, s_oT_ps, s_oT, s_y, s_bo, s_x) = (sec.per_stream(n) for n in (
             "ctx_loaded", "xT_ps", "xT", "q_ps", "k_ps", "v_ps", "q", "k", "v", "kbd", "scores", "max",
             "shifted", "exp", "probsT_ps", "probsT", "av", "recip", "out", "outT_ps", "outT", "y",
             "bo_added", "x_done"))
        s_one = sec.sem("ones_set")
        turn_w = Turned(sec, [bank[0][0], bank[1][0]], turned) if turned else None
        O = [M[s][:, 0:NH * (DH + 1)].rearrange("p (h e) -> p h e", h=NH) for s in range(NS)]
        if kind == PRUNED:
            ls, rls = sbs("ls", [P, NH]), sbs("rls", [P, NH])
            cs, keepT = sbs("cs", [P, NH]), sbs("keepT", [P, NH])
            cst, cst2 = sbs("cst", [NH, P]), sbs("cst2", [NH, P])
            m8 = sbs("m8", [NH, 2, 8])
            s_ls, s_rls, s_cs_ps, s_cs, s_csT, s_ct, s_m1, s_r1, s_m2, s_fill, s_r2, s_keep, s_kT, s_kTs, s_vm = (
                sec.per_stream(n) for n in ("rowsum", "rowrecip", "colsum_ps", "colsum", "colsumT_ps", "colsumT",
                                            "least8", "drop8", "least16", "fill", "drop13", "keep", "keepT_ps",
                                            "keepT", "v_pruned"))
            colsum = [M[s][:, 320:320 + NH] for s in range(NS)]
            CT = [T[s][0:NH, 0:P] for s in range(NS)]
            KT = [T[s][:, 256:256 + NH] for s in range(NS)]
        if kind == MASKED:
            s_mk = sec.per_stream("masked")
        if kind == MIXED:
            mix = sbs("mix", [P, g.mixw])
            s_mixp = sec.per_stream("mix_partial")
            s_mix = sec.per_stream("mix")
            s_mixc = sec.per_stream("mix_chain")

        def weights(s):
            if kind != MIXED:
                return w
            m = mix[s]
            q = {n: m[:, DC * D * c:DC * D * (c + 1)].rearrange("p (c n) -> p c n", c=DC)
                 for c, n in enumerate(("Wq", "Wk", "Wv"))}
            o = 3 * DC * D
            q.update(bq=m[:, o:o + DC], bk=m[:, o + DC:o + 2 * DC], bv=m[:, o + 2 * DC:o + 2 * DC + D])
            q.update(Wo=w["Wo"], bo=w["bo"])
            return q

        kv = xT if kind == MIXED else ctxT
        with sec.block() as block:
            @block.sync
            def _(sp):
                if kind != MIXED:
                    for s in range(NS):
                        sp.dma_start(ctxT[s][:, :, :], g.ctxT[:, s, :, :]).then_inc(s_ctx[s], 16)
                    with sp.Fori(1, TURNS) as i:
                        for s in range(NS):
                            sp.wait_ge(s_v_ps[s], i)
                            sp.dma_start(ctxT[s][:, :, :], g.ctxT[:, NS * i + s, :, :]).then_inc(s_ctx[s], 16)

            @block.gpsimd
            def _(pool):
                arrived(pool, g, *needs)
                for s in range(NS):
                    pool.memset(v[s][:, :, :], 1.0).then_inc(s_one, 1)
                with pool.Fori(1, TURNS + 1) as i:
                    for s in range(NS):
                        for c in range(DC):
                            if c == 0:
                                pool.wait_ge(s_k[s], i)
                            pool.tensor_tensor(
                                kbd[s][:, c, :, :], kT[s][:, c, :].unsqueeze(1).to_broadcast([P, HC, P]),
                                g.hmask[:, :].unsqueeze(2).to_broadcast([P, HC, P]), ALU.mult).then_inc(s_kbd[s], 1)
                    for s in range(NS):
                        pool.wait_ge(ln.s_xn[s], i)
                        pool.tensor_tensor(tile_of(g, i, s), tile_of(g, i, s), w["bo"], ALU.add).then_inc(s_bo[s], 1)

            @block.tensor
            def _(pe):
                arrived(pe, g, *needs)
                if turn_w:
                    turn_w.tensor(pe, g.ident)
                    turn_w.wait(pe)
                pe.wait_ge(s_one, NS)
                with pe.Fori(1, TURNS + 1) as i:
                    nth = [pe.snap(NQ * i - NQ + 1 + t) for t in range(NQ)]
                    half = [pe.snap(DC * i - DC + 1 + c) for c in range(DC)]
                    for s in range(NS):
                        pe.wait_ge(ln.s_xn[s], i)
                        for c in range(DC):
                            mm = pe.transpose(M[s][:, c * P:c * P + P], ln.xn[s][:, c * P:c * P + P], g.ident[:, :])
                        mm.then_inc(s_xT_ps[s], 1)

                    def project(out, W, inp):
                        for m in range(DC):
                            for c in range(DC):
                                mm = pe.matmul(out[:, m * P:m * P + P], W[:, c, m * P:m * P + P], inp[:, c, :],
                                               start=(c == 0), stop=(c == DC - 1))
                        return mm

                    for s in range(NS):
                        W = weights(s)
                        if kind == MIXED:
                            pe.wait_ge(s_mix[s], i)
                        else:
                            pe.wait_ge(s_ctx[s], 16 * i)
                        if kind == MIXED:
                            pe.wait_ge(s_xT[s], i)
                        project(S[s][1], W["Wk"], kv[s]).then_inc(s_k_ps[s], 1)
                        pe.wait_ge(s_xT[s], i)
                        project(S[s][0], W["Wq"], xT[s]).then_inc(s_q_ps[s], 1)
                        for c in range(DC):
                            mm = pe.matmul(T[s][:, 0:D], kv[s][:, c, :], W["Wv"][:, c, :], start=(c == 0),
                                           stop=(c == DC - 1))
                        mm.then_inc(s_v_ps[s], 1)

                    def scores(s, t):
                        c = t * HQ // HC
                        if t < 2:
                            pe.wait_ge(s_q[s], i)
                        else:
                            pe.wait_ge(s_sh[s], nth[t - 2])
                        pe.wait_ge(s_kbd[s], half[c])
                        h = t * HQ % HC
                        pe.matmul(S[s][t % 2][:, :], qT[s][:, c, :], kbd[s][:, c, h:h + HQ, :], start=True,
                                  stop=True).then_inc(s_sc[s], 1)

                    def turn_probs(s, t):
                        pe.wait_ge(s_ex[s], nth[t])
                        if t == 0:
                            pe.wait_ge(s_v[s], i)
                        else:
                            pe.wait_ge(s_pt[s], nth[t - 1])
                        if kind == PRUNED:
                            pe.wait_ge(s_rls[s], nth[t])
                            for h in range(HQ):
                                n = t * HQ + h
                                pe.matmul(colsum[s][:, n:n + 1], pr[s][:, t % 2, h, :], rls[s][:, n:n + 1],
                                          start=True, stop=True)
                        for h in range(HQ):
                            mm = pe.transpose(T[s][:, h * P:h * P + P], pr[s][:, t % 2, h, :], g.ident[:, :])
                        mm.then_inc(s_tp[s], 1)

                    def values(s, t):
                        pe.wait_ge(s_pt[s], nth[t])
                        for h in range(t * HQ, t * HQ + HQ):
                            mm = pe.matmul(O[s][:, h, :], prT[s][:, t, h % HQ, :], v[s][:, h, :], start=True,
                                           stop=True)
                        if t == NQ - 1:
                            mm.then_inc(s_av[s], 1)

                    late = 2 if kind != PRUNED else NQ + 2
                    for t in range(NQ + 1 if kind == PRUNED else NQ + 2):
                        for s in range(NS):
                            if t < NQ:
                                scores(s, t)
                            if 1 <= t <= NQ:
                                turn_probs(s, t - 1)
                            if t >= late:
                                values(s, t - late)
                    if kind == PRUNED:
                        for s in range(NS):
                            pe.wait_ge(s_cs[s], i)
                            pe.wait_ge(s_pt[s], nth[NQ - 1])
                            pe.transpose(CT[s], cs[s][:, :], g.ident[:, :]).then_inc(s_csT[s], 1)
                        for s in range(NS):
                            pe.wait_ge(s_keep[s], i)
                            pe.matmul(KT[s], cst2[s][:, :], g.ident[0:NH, 0:NH], start=True, stop=True).then_inc(s_kT[s], 1)
                        for s in range(NS):
                            pe.wait_ge(s_vm[s], i)
                            for t in range(NQ):
                                values(s, t)
                    for s in range(NS):
                        pe.wait_ge(s_on[s], i)
                        for c in range(DC):
                            mm = pe.transpose(T[s][:, c * P:c * P + P],
                                              on[s][:, c * HC:(c + 1) * HC, :].rearrange("p h e -> p (h e)"),
                                              g.ident[:, :])
                        mm.then_inc(s_oT_ps[s], 1)
                    for s in range(NS):
                        pe.wait_ge(s_oT[s], i)
                        for c in range(DC):
                            mm = pe.matmul(S[s][0][:, 0:D], oT[s][:, c, :], w["Wo"][:, c, :], start=(c == 0),
                                           stop=(c == DC - 1))
                        mm.then_inc(s_y[s], 1)

            @block.scalar
            def _(act):
                if turn_w:
                    turn_w.scalar(act)
                ln.scalar_start(act)
                with act.Fori(1, TURNS + 1) as i:
                    nth = [act.snap(NQ * i - NQ + 1 + t) for t in range(NQ)]
                    if kind == MIXED:
                        for s in range(NS):
                            act.activation(mix[s][:, :], g.experts[:, 0, :], ACT.Copy,
                                           scale=g.gates[:, NS * (i - 1) + s, 0, :]).then_inc(s_mixp[s], 1)
                    for s in range(NS):
                        act.wait_ge(s_xT_ps[s], i)
                        act.copy(xT[s][:, :, :], M[s][:, 0:D].rearrange("p (c t) -> p c t", c=DC)).then_inc(s_xT[s], 1)
                    for t in range(NQ + 1):
                        for s in range(NS):
                            if t < NQ:
                                act.wait_ge(s_sh[s], nth[t])
                                act.activation(pr[s][:, t % 2, :, :], pr[s][:, t % 2, :, :], ACT.Exp,
                                               scale=DH ** -0.5).then_inc(s_ex[s], 1)
                            if t >= 1:
                                act.wait_ge(s_tp[s], nth[t - 1])
                                act.copy(prT[s][:, t - 1, :, :], T[s][:, :].rearrange("p (h k) -> p h k", h=HQ)
                                         ).then_inc(s_pt[s], 1)
                    for s in range(NS):
                        act.wait_ge(s_oT_ps[s], i)
                        act.copy(oT[s][:, :, :], T[s][:, 0:D].rearrange("p (c t) -> p c t", c=DC)).then_inc(s_oT[s], 1)

            @block.vector
            def _(dve):
                arrived(dve, g, *needs)
                dve.wait_ge(s_one, NS)
                ln.vector_start(dve)
                with dve.Fori(1, TURNS + 1) as i:
                    nth = [dve.snap(NQ * i - NQ + 1 + t) for t in range(NQ)]
                    for s in range(NS):
                        ln.vector_apply(dve, s, i)
                    if kind == MIXED:
                        for s in range(NS):
                            for e in range(1, 4):
                                if e == 1:
                                    dve.wait_ge(s_mixp[s], i)
                                else:
                                    dve.wait_ge(s_mixc[s], 2 * i - 3 + e)
                                mixed = dve.scalar_tensor_tensor(
                                    out=mix[s][:, :], in0=g.experts[:, e, :], scalar=g.gates[:, NS * (i - 1) + s, e, :],
                                    in1=mix[s][:, :], op0=ALU.mult, op1=ALU.add)
                                mixed.then_inc(s_mixc[s] if e < 3 else s_mix[s], 1)
                            dve.wait_ge(s_mix[s], i)
                    for s in range(NS):
                        W = weights(s)
                        col = lambda b: W[b].unsqueeze(2).to_broadcast([P, DC, P])
                        two = lambda ps: ps[:, 0:D].rearrange("p (c t) -> p c t", c=DC)
                        dve.wait_ge(s_k_ps[s], i)
                        dve.tensor_tensor(kT[s][:, :, :], two(S[s][1]), col("bk"), ALU.add).then_inc(s_k[s], 1)
                        dve.wait_ge(s_q_ps[s], i)
                        dve.tensor_tensor(qT[s][:, :, :], two(S[s][0]), col("bq"), ALU.add).then_inc(s_q[s], 1)
                        dve.wait_ge(s_v_ps[s], i)
                        dve.tensor_tensor(v[s][:, :, 0:DH], T[s][:, 0:D].rearrange("p (h e) -> p h e", h=NH),
                                          W["bv"].rearrange("p (h e) -> p h e", h=NH), ALU.add).then_inc(s_v[s], 1)
                    for t in range(NQ):
                        for s in range(NS):
                            sc = S[s][t % 2][:, :].rearrange("p (h k) -> p h k", h=HQ)
                            m4 = mx[s][:, t * HQ:t * HQ + HQ]
                            dve.wait_ge(s_sc[s], nth[t])
                            if kind == MASKED:
                                apart(dve, g)
                                dve.copy_predicated(sc, g.hidden[:, :].unsqueeze(1).to_broadcast([P, HQ, P]),
                                                    g.far[:, 0:1].unsqueeze(2).to_broadcast([P, HQ, P])
                                                    ).then_inc(s_mk[s], 1)
                                dve.wait_ge(s_mk[s], nth[t])
                            dve.tensor_reduce(m4, sc, AX.X, ALU.max).then_inc(s_mx[s], 1)
                            if t >= 2:
                                dve.wait_ge(s_tp[s], nth[t - 2])
                            dve.wait_ge(s_mx[s], nth[t])
                            dve.tensor_tensor(pr[s][:, t % 2, :, :], sc, m4.unsqueeze(2).to_broadcast([P, HQ, P]),
                                              ALU.subtract).then_inc(s_sh[s], 1)
                        if kind == PRUNED:
                            for s in range(NS):
                                l4 = slice(t * HQ, t * HQ + HQ)
                                dve.wait_ge(s_ex[s], nth[t])
                                dve.tensor_reduce(ls[s][:, l4], pr[s][:, t % 2, :, :], AX.X, ALU.add).then_inc(s_ls[s], 1)
                                dve.wait_ge(s_ls[s], nth[t])
                                dve.reciprocal(rls[s][:, l4], ls[s][:, l4]).then_inc(s_rls[s], 1)
                    if kind == PRUNED:
                        for s in range(NS):
                            dve.wait_ge(s_tp[s], nth[NQ - 1])
                            dve.tensor_copy(cs[s][:, :], colsum[s]).then_inc(s_cs[s], 1)
                        for s in range(NS):
                            dve.wait_ge(s_csT[s], i)
                            dve.tensor_scalar(cst[s][:, ::-1], CT[s], -1.0, None, ALU.mult).then_inc(s_ct[s], 1)
                        for s in range(NS):
                            dve.wait_ge(s_ct[s], i)
                            apart(dve, g)
                            dve.max(m8[s][:, 0, :], cst[s][:, :]).then_inc(s_m1[s], 1)
                            dve.wait_ge(s_m1[s], i)
                            apart(dve, g)
                            dve.match_replace(cst2[s][:, :], m8[s][:, 0, :], cst[s][:, :], -BIG).then_inc(s_r1[s], 1)
                            dve.wait_ge(s_r1[s], i)
                            apart(dve, g)
                            dve.max(m8[s][:, 1, :], cst2[s][:, :]).then_inc(s_m2[s], 1)
                            dve.wait_ge(s_m2[s], i)
                            apart(dve, g)
                            dve.tensor_scalar(m8[s][:, 1, NDROP - 8:8], m8[s][:, 1, NDROP - 8:8], 0.0, -BIG,
                                              ALU.mult, ALU.add).then_inc(s_fill[s], 1)
                            dve.wait_ge(s_fill[s], i)
                            apart(dve, g)
                            dve.match_replace(cst[s][:, :], m8[s][:, 1, :], cst2[s][:, :], -BIG).then_inc(s_r2[s], 1)
                            dve.wait_ge(s_r2[s], i)
                            dve.tensor_scalar(cst2[s][:, ::-1], cst[s][:, :], -0.5 * BIG, None, ALU.is_gt
                                              ).then_inc(s_keep[s], 1)
                        for s in range(NS):
                            dve.wait_ge(s_kT[s], i)
                            dve.tensor_copy(keepT[s][:, :], KT[s]).then_inc(s_kTs[s], 1)
                            dve.wait_ge(s_kTs[s], i)
                            dve.tensor_tensor(v[s][:, :, 0:DH], v[s][:, :, 0:DH],
                                              keepT[s][:, :].unsqueeze(2).to_broadcast([P, NH, DH]), ALU.mult
                                              ).then_inc(s_vm[s], 1)
                    for s in range(NS):
                        dve.wait_ge(s_av[s], i)
                        dve.reciprocal(rl[s][:, :], O[s][:, :, DH]).then_inc(s_rl[s], 1)
                        dve.wait_ge(s_rl[s], i)
                        dve.tensor_tensor(on[s][:, :, :], O[s][:, :, 0:DH],
                                          rl[s][:, :].unsqueeze(2).to_broadcast([P, NH, DH]), ALU.mult
                                          ).then_inc(s_on[s], 1)
                    for s in range(NS):
                        dve.wait_ge(s_y[s], i)
                        dve.wait_ge(s_bo[s], i)
                        dve.tensor_tensor(tile_of(g, i, s), S[s][0][:, 0:D], tile_of(g, i, s), ALU.add
                                          ).then_inc(s_x[s], 1)
                    for s in range(NS):
                        ln.vector_stats(dve, s, i, s_x)


QMAX = 127.0
F0 = 704
FC0 = -(-F0 // P)
TG = 4
NG = NB // TG


def rounded(eng, out, tmp, src, scalar, sem, n, clip=None):
    lo, hi = clip or (-128.0, 127.0)
    eng.tensor_scalar(tmp, src, scalar, MAGIC, ALU.mult, ALU.add).then_inc(sem, 1)
    eng.wait_ge(sem, n + 1)
    eng.tensor_scalar(tmp, tmp, MAGIC + hi, MAGIC + lo, ALU.min, ALU.max).then_inc(sem, 1)
    eng.wait_ge(sem, n + 2)
    eng.tensor_scalar(out, tmp, MAGIC, None, ALU.subtract).then_inc(sem, 1)
    eng.wait_ge(sem, n + 3)


class GlobalMax:

    def __init__(self, sec, name, bank):
        self.ps, self.one = bank, sec.sb(f"{name}_one", [1, 1])
        self.s_row, self.s_one, self.s_all = sec.sem(f"{name}_row"), sec.sem(f"{name}_one"), sec.sem(f"{name}_all")

    def tensor(self, pe, g, col, s_col, n):
        pe.wait_ge(s_col, n)
        pe.transpose(self.ps[0:1, 0:P], col, g.ident[:, :]).then_inc(self.s_row, 1)
        pe.wait_ge(self.s_one, 1)
        pe.matmul(self.ps[:, P:P + 1], g.onesP[0:1, :], self.one[:, :], start=True, stop=True
                  ).then_inc(self.s_all, 1)

    def vector(self, dve):
        dve.wait_ge(self.s_row, 1)
        dve.tensor_reduce(self.one[:, :], self.ps[0:1, 0:P], AX.X, ALU.max).then_inc(self.s_one, 1)
        dve.wait_ge(self.s_all, 1)
        return self.ps[:, P:P + 1]


def fake_quant_ffn(nc, g, w):
    sec = Section(nc, "L0f")
    with sec:
        ln = LayerNorm(sec, g)
        banks = [sec.ps(f"bank{n}", [P, BANK]) for n in range(8)]
        act_scale = sec.sb("act_scale", [P, 8])
        sg, su, iw = (sec.sb(n, [P, FC0]) for n in ("gate_scale", "up_scale", "inv_w"))
        sd, sd_row = sec.sb("down_scale", [P, DC]), sec.sb("down_row", [P, D])
        xqT = sec.sb("xqT", [P, DC, NB * P], BF16)
        wT = {n: sec.sb(f"{n}T", [P, DC, FC0 * P], BF16) for n in ("gate", "up")}
        wdT = sec.sb("downT", [P, FC0, D], BF16)
        amax, hmax = sec.sb("amax", [P, NB, 1]), sec.sb("hmax", [P, NG * FC0])
        gm1, gm2 = GlobalMax(sec, "xmax", banks[7]), GlobalMax(sec, "hmax", banks[7])
        s_sc, s_w, s_w2, s_amax, s_col, s_q, s_xq = (sec.sem(n) for n in (
            "scales", "w_steps", "w_rounded", "tile_amax", "amax_col", "q_steps", "xq_ready"))
        s_dr, s_t_ps, s_t_sb, s_row_ps = sec.sem("x_steps"), sec.sem("turned_ps"), sec.sem("turned_sb"), sec.sem("row_ps")
        half_col = sec.sb("amax_cols", [P, 2])
        s_idb = sec.sem("identb")
        with ExitStack() as early:
            xn_all = early.enter_context(nc.sbuf_tensor("L0f_xn_all", [P, NB, D], F32))
            xq = early.enter_context(nc.sbuf_tensor("L0f_xq", [P, NB, D], BF16))
            wq = {n: early.enter_context(nc.sbuf_tensor(f"L0f_{n}q", [P, FC0, D], BF16)) for n in ("gate", "up")}
            wdq = early.enter_context(nc.sbuf_tensor("L0f_downq", [P, DC, FC0 * P], BF16))
            wtmp = early.enter_context(nc.sbuf_tensor("L0f_wtmp", [P, FC0, D], F32))
            identb = early.enter_context(nc.sbuf_tensor("L0f_identb", [P, P], BF16))
            blocks = [(wq[n][:, f, c * P:c * P + P], wT[n][:, c, f * P:f * P + P])
                      for n in ("gate", "up") for f in range(FC0) for c in range(DC)]
            blocks += [(wdq[:, c, f * P:f * P + P], wdT[:, f, c * P:c * P + P]) for f in range(FC0) for c in range(DC)]
            with sec.block() as block:
                @block.tensor
                def _(pe):
                    pe.wait_ge(s_idb, 1)
                    pe.wait_ge(s_w2, 3)
                    for n in range(0, len(blocks), 4):
                        k = n // 4
                        if k >= 6:
                            pe.wait_ge(s_t_sb, k - 5)
                        for m, (src, _) in enumerate(blocks[n:n + 4]):
                            mm = pe.transpose(banks[k % 6][:, :].bitcast(BF16)[:, m * P:m * P + P], src, identb[:, :])
                        mm.then_inc(s_t_ps, 1)
                    for c in range(DC):
                        mm = pe.matmul(banks[6][:, c * P:c * P + P], sd[:, c:c + 1].to_broadcast([P, P]),
                                       g.ident[:, :], start=True, stop=True)
                    mm.then_inc(s_row_ps, 1)
                    gm1.tensor(pe, g, half_col[:, 0:1], s_col, 1)
                    nw = len(blocks) // 4
                    for t in range(NB // 2):
                        k = nw + t
                        pe.wait_ge(s_xq, t // 2 + 1)
                        pe.wait_ge(s_t_sb, k - 5)
                        for m in range(4):
                            b, c = 2 * t + m // 2, m % 2
                            mm = pe.transpose(banks[k % 6][:, :].bitcast(BF16)[:, m * P:m * P + P],
                                              xq[:, b, c * P:c * P + P], identb[:, :])
                        mm.then_inc(s_t_ps, 1)

                @block.scalar
                def _(act):
                    arrived(act, g, "L0_ffn")
                    act.copy(identb[:, :], g.ident[:, :]).then_inc(s_idb, 1)
                    ln.scalar_start(act)
                    act.activation(act_scale[:, 0:1], w["clip_x"], ACT.Exp, scale=-1.0).then_inc(s_sc, 1)
                    act.activation(act_scale[:, 1:2], w["clip_down"], ACT.Exp, scale=-1.0).then_inc(s_sc, 1)
                    for k in range(len(blocks) // 4):
                        act.wait_ge(s_t_ps, k + 1)
                        for m in range(4):
                            dst = blocks[4 * k + m][1]
                            cp = act.copy(dst, banks[k % 6][:, :].bitcast(BF16)[:, m * P:m * P + P])
                        cp.then_inc(s_t_sb, 1)
                    for t in range(NB // 2):
                        k = len(blocks) // 4 + t
                        act.wait_ge(s_t_ps, k + 1)
                        act.copy(xqT[:, :, 2 * t * P:(2 * t + 2) * P].rearrange("p c (b n) -> p b c n", b=2),
                                 banks[k % 6][:, :].bitcast(BF16)[:, 0:4 * P].rearrange("p (b c n) -> p b c n", b=2, c=2)
                                 ).then_inc(s_t_sb, 1)

                @block.vector
                def _(dve):
                    arrived(dve, g, "L0_ffn")
                    n = 0
                    dve.memset(w["gate"][F0 % P:P, FC0 - 1, :], 0.0)
                    dve.memset(w["up"][F0 % P:P, FC0 - 1, :], 0.0)
                    dve.memset(w["down"][:, :, F0:FC0 * P], 0.0).then_inc(s_w, 1)
                    n += 1
                    dve.wait_ge(s_w, n)

                    def scales(src, out):
                        k = src.shape[1]
                        dve.tensor_reduce(iw[:, 0:k], src, AX.X, ALU.max, apply_absolute_value=True).then_inc(s_w, 1)
                        dve.wait_ge(s_w, n + 1)
                        dve.tensor_scalar(out, iw[:, 0:k], 1.0 / QMAX, 1e-37, ALU.mult, ALU.max).then_inc(s_w, 1)
                        dve.wait_ge(s_w, n + 2)
                        dve.reciprocal(iw[:, 0:k], out).then_inc(s_w, 1)
                        dve.wait_ge(s_w, n + 3)

                    for src, out, q in (("gate", sg, wq["gate"]), ("up", su, wq["up"]), ("down", sd, wdq)):
                        k = w[src].shape[1]
                        tmp = wtmp[:, :, :] if src != "down" else wtmp[:, :, :].rearrange("p f n -> p (f n)")[
                            :, 0:DC * FC0 * P].rearrange("p (c n) -> p c n", c=DC)
                        scales(w[src], out[:, :])
                        n += 3
                        dve.tensor_tensor(tmp, w[src], iw[:, 0:k].unsqueeze(2).to_broadcast(list(w[src].shape)),
                                          ALU.mult).then_inc(s_w, 1)
                        dve.wait_ge(s_w, n + 1)
                        dve.tensor_scalar(tmp, tmp, MAGIC, None, ALU.add).then_inc(s_w, 1)
                        dve.wait_ge(s_w, n + 2)
                        dve.tensor_scalar(q[:, :, :], tmp, MAGIC, None, ALU.subtract).then_inc(s_w2, 1)
                        n += 2
                        dve.wait_ge(s_w2, {"gate": 1, "up": 2, "down": 3}[src])
                    ln.vector_start(dve)
                    with dve.Fori(1, NB + 1) as i:
                        dve.tensor_scalar(xn_all[:, i - 1, :], g.x[:, i - 1, :], ln.mv[:, i - 1, 0:1],
                                          ln.rstd[:, i - 1, :], ALU.subtract, ALU.mult).then_inc(ln.s_xn[0], 1)
                        dve.wait_ge(ln.s_xn[0], i)
                        dve.tensor_reduce(amax[:, i - 1, :], xn_all[:, i - 1, :], AX.X, ALU.max, apply_absolute_value=True).then_inc(s_amax, 1)
                    dve.wait_ge(s_amax, NB)
                    dve.tensor_reduce(half_col[:, 0:1], amax[:, :, 0], AX.X, ALU.max).then_inc(s_col, 1)
                    dve.wait_ge(s_sc, 2)
                    dve.tensor_scalar(act_scale[:, 2:4], act_scale[:, 0:2], 1.0, QMAX, ALU.add, ALU.mult).then_inc(s_sc, 1)
                    dve.wait_ge(s_sc, 3)
                    dve.reciprocal(act_scale[:, 2:4], act_scale[:, 2:4]).then_inc(s_sc, 1)
                    dve.wait_ge(s_row_ps, 1)
                    dve.tensor_copy(sd_row[:, :], banks[6][:, 0:D]).then_inc(s_sc, 1)
                    top = gm1.vector(dve)
                    dve.wait_ge(s_sc, 5)
                    dve.tensor_tensor(act_scale[:, 4:5], top, act_scale[:, 2:3], ALU.mult).then_inc(s_sc, 1)
                    dve.wait_ge(s_sc, 6)
                    dve.reciprocal(act_scale[:, 5:6], act_scale[:, 4:5]).then_inc(s_sc, 1)
                    dve.tensor_scalar(sg[:, :], sg[:, :], act_scale[:, 4:5], None, ALU.mult)
                    dve.tensor_scalar(su[:, :], su[:, :], act_scale[:, 4:5], None, ALU.mult)
                    dve.wait_ge(s_sc, 7)
                    for q in range(4):
                        part = xn_all[:, 4 * q:4 * q + 4, :]
                        rounded(dve, xq[:, 4 * q:4 * q + 4, :], part, part, act_scale[:, 5:6], s_dr, 3 * q)
                        dve.memset(g.pad[0:1, q:q + 1], 0.0).then_inc(s_xq, 1)

        h = sec.sb("h", [P, FC0, NB * P])
        ga = sec.sb("silu_gate", [P, 3, BANK])
        s_gu_ps, s_silu, s_h, s_free, s_mx = (sec.sem(n) for n in ("gate_up_ps", "silu", "h", "banks_free", "h_amax"))
        with sec.block() as block:
            @block.tensor
            def _(pe):
                with pe.Fori(1, NG + 1) as i:
                    for f in range(FC0):
                        k = f % 3
                        pe.wait_ge(s_free, FC0 * i - FC0 + f + 1)
                        for m, n in enumerate(("gate", "up")):
                            for c in range(DC):
                                mm = pe.matmul(banks[2 * k + m][:, :], wT[n][:, c, f * P:f * P + P],
                                               xqT[:, c, bass.ts(i - 1, BANK)], start=(c == 0), stop=(c == DC - 1))
                        mm.then_inc(s_gu_ps, 1)
                gm2.tensor(pe, g, half_col[:, 1:2], s_col, 2)

            @block.scalar
            def _(act):
                with act.Fori(1, NG + 1) as i:
                    for f in range(FC0):
                        act.wait_ge(s_free, FC0 * i - FC0 + f + 1)
                        act.wait_ge(s_gu_ps, FC0 * i - FC0 + f + 1)
                        act.activation(ga[:, f % 3, :], banks[2 * (f % 3)][:, :], ACT.Silu,
                                       scale=sg[:, f:f + 1]).then_inc(s_silu, 1)

            @block.vector
            def _(dve):
                dve.memset(g.pad[0:1, 0:1], 0.0).then_inc(s_free, 3)
                with dve.Fori(1, NG + 1) as i:
                    for f in range(FC0):
                        dve.wait_ge(s_silu, FC0 * i - FC0 + f + 1)
                        dve.scalar_tensor_tensor(out=h[:, f, bass.ts(i - 1, BANK)], in0=banks[2 * (f % 3) + 1][:, :],
                                                 scalar=su[:, f:f + 1], in1=ga[:, f % 3, :], op0=ALU.mult,
                                                 op1=ALU.mult).then_inc(s_free, 1)
                dve.wait_ge(s_free, NG * FC0 + 3)
                for f in range(FC0):
                    dve.tensor_reduce(hmax[:, f:f + 1], h[:, f, :], AX.X, ALU.max, apply_absolute_value=True).then_inc(s_mx, 1)
                dve.wait_ge(s_mx, FC0)
                dve.tensor_reduce(half_col[:, 1:2], hmax[:, 0:FC0], AX.X, ALU.max).then_inc(s_col, 1)
                top = gm2.vector(dve)
                dve.tensor_tensor(act_scale[:, 6:7], top, act_scale[:, 3:4], ALU.mult).then_inc(s_sc, 1)
                dve.wait_ge(s_sc, 8)
                dve.reciprocal(act_scale[:, 7:8], act_scale[:, 6:7])
                dve.tensor_scalar(sd_row[:, :], sd_row[:, :], act_scale[:, 6:7], None, ALU.mult)

        hq = sec.sb("hq", [P, 2, FC0, P], BF16)
        yt = sec.sb("yt", [P, 2, D])
        s_hr, s_hc, s_hq, s_y, s_yt, s_x = (sec.sem(n) for n in ("h_scaled", "h_clipped", "hq", "y", "y_scaled", "x_done"))
        with sec.block() as block:
            @block.scalar
            def _(act):
                with act.Fori(1, NB + 1) as i:
                    hb = h[:, :, bass.ts(i - 1, P)]
                    act.activation(hb, hb, ACT.Identity, bias=g.magic[:, 0:1], scale=act_scale[:, 7:8]).then_inc(s_hr, 1)

            @block.vector
            def _(dve):
                with dve.Fori(1, NB // 2 + 1) as i:
                    for s in range(2):
                        b = 2 * i - 2 + s
                        hb = h[:, :, bass.ts(b, P)]
                        dve.wait_ge(s_hr, 2 * i - 1 + s)
                        dve.tensor_scalar(hb, hb, MAGIC + QMAX, MAGIC - QMAX - 1.0, ALU.min, ALU.max).then_inc(s_hc, 1)
                        dve.wait_ge(s_hc, 2 * i - 1 + s)
                        dve.tensor_scalar(hq[:, s, :, :], hb, MAGIC, None, ALU.subtract).then_inc(s_hq, 1)
                    for s in range(2):
                        b = 2 * i - 2 + s
                        dve.wait_ge(s_y, 2 * i - 1 + s)
                        dve.tensor_tensor(yt[:, s, :], banks[s][:, 0:D], sd_row[:, :], ALU.mult).then_inc(s_yt, 1)
                        dve.wait_ge(s_yt, 2 * i - 1 + s)
                        dve.tensor_tensor(g.x[:, b, :], yt[:, s, :], g.x[:, b, :], ALU.add).then_inc(s_x, 1)
                    dve.wait_ge(s_x, 2 * i)
                    apart(dve, g)
                    for s in range(2):
                        dve.bn_stats(g.stats[:, 2 * i - 2 + s, :], g.x[:, 2 * i - 2 + s, :])

            @block.tensor
            def _(pe):
                with pe.Fori(1, NB // 2 + 1) as i:
                    for s in range(2):
                        pe.wait_ge(s_hq, 2 * i - 1 + s)
                        for f in range(FC0):
                            mm = pe.matmul(banks[s][:, 0:D], hq[:, s, f, :], wdT[:, f, :], start=(f == 0),
                                           stop=(f == FC0 - 1))
                        mm.then_inc(s_y, 1)


def bitlinear_ffn(nc, g, w):
    sec = Section(nc, "L1f")
    F = 1024
    FC = F // P
    with sec:
        ln = LayerNorm(sec, g)
        bank = banks_of(sec)
        sbs = lambda nm, shape, dt=F32: [sec.sb(f"{nm}{s}", shape, dt) for s in range(NS)]
        identb = sec.sb("identb", [P, P], BF16)
        w1T, w2T = sec.sb("w1T", [P, DC, F], BF16), sec.sb("w2T", [P, FC, D], BF16)
        xs, xq, xqT = sbs("xs", [P, D]), sbs("xq", [P, D], BF16), sbs("xqT", [P, DC, P], BF16)
        hh, hs = sbs("h", [P, F]), sbs("hs", [P, F])
        hq, hqT = sbs("hq", [P, F], BF16), sbs("hqT", [P, FC, P], BF16)
        ss, am, fac, deq, tmp = (sec.sb(n, [P, 2, NS]) for n in ("ss", "am", "factor", "dequant", "tmp"))
        rs = [Rsqrt(sec, f"rs{n}", NS) for n in range(2)]
        wsum, wmean, winv = sec.sb("wsum", [P, 2]), sec.sb("wmean", [P, 2]), sec.sb("winv", [P, 2])
        s_sq, s_am, s_ch, s_scaled, s_q, s_qT_ps, s_qT = (
            [sec.sem(f"{n}{k}") for k in range(2)] for n in ("squares", "amax", "factor_steps", "scaled", "rounded",
                                                             "qT_ps", "qT"))
        s_h_ps, s_h, s_gelu, s_y, s_bo, s_x = (sec.per_stream(n) for n in (
            "h_ps", "h_pre", "gelu", "y", "b2_added", "x_done"))
        s_ws, s_wps, s_wst, s_wq = sec.sem("w_sums"), sec.sem("w_mean_ps"), sec.sem("w_steps"), sec.sem("w_rounded")
        with ExitStack() as early:
            wq = [early.enter_context(nc.sbuf_tensor(f"L1f_w{n}q", [P, 8, D] if n == 0 else [P, DC, F], BF16))
                  for n in range(2)]
            flat = [bank[s][n] for n in range(3) for s in range(NS)]
            blocks = [(wq[0][:, f, c * P:c * P + P], w1T[:, c, f * P:f * P + P]) for c in range(DC) for f in range(FC)]
            blocks += [(wq[1][:, c, f * P:f * P + P], w2T[:, f, c * P:c * P + P]) for f in range(FC) for c in range(DC)]
            s_t_ps, s_t_sb = sec.sem("turned_ps"), sec.sem("turned_sb")
            with sec.block() as block:
                @block.tensor
                def _(pe):
                    pe.wait_ge(s_ws, 2)
                    pe.matmul(bank[0][3][:, 0:2], g.onesP[:, :], wsum[:, :], start=True, stop=True).then_inc(s_wps, 1)
                    pe.wait_ge(s_wq, 3)
                    for k in range(len(blocks) // 4):
                        if k >= 6:
                            pe.wait_ge(s_t_sb, k - 5)
                        for m in range(4):
                            mm = pe.transpose(flat[k % 6][:, :].bitcast(BF16)[:, m * P:m * P + P],
                                              blocks[4 * k + m][0], identb[:, :])
                        mm.then_inc(s_t_ps, 1)

                @block.scalar
                def _(act):
                    act.copy(identb[:, :], g.ident[:, :]).then_inc(s_wq, 1)
                    for k in range(len(blocks) // 4):
                        act.wait_ge(s_t_ps, k + 1)
                        for m in range(4):
                            cp = act.copy(blocks[4 * k + m][1], flat[k % 6][:, :].bitcast(BF16)[:, m * P:m * P + P])
                        cp.then_inc(s_t_sb, 1)

                @block.vector
                def _(dve):
                    arrived(dve, g, "L1_ffn")
                    for n in range(2):
                        dve.tensor_reduce(wsum[:, n:n + 1], w[f"w{n + 1}"], AX.XY, ALU.add,
                                          apply_absolute_value=True).then_inc(s_ws, 1)
                    dve.wait_ge(s_wps, 1)
                    dve.tensor_scalar(wmean[:, :], bank[0][3][:, 0:2], 1.0 / (F * D), 1e-5, ALU.mult,
                                      ALU.max).then_inc(s_wst, 1)
                    dve.wait_ge(s_wst, 1)
                    dve.reciprocal(winv[:, :], wmean[:, :]).then_inc(s_wst, 1)
                    dve.wait_ge(s_wst, 2)
                    for n in range(2):
                        src = w[f"w{n + 1}"]
                        rounded(dve, wq[n][:, :, :], src, src, winv[:, n:n + 1], s_wst, 2 + 3 * n, (-1.0, 1.0))
                        dve.memset(g.pad[0:1, n:n + 1], 0.0).then_inc(s_wq, 1)

        with sec.block() as block:
            @block.gpsimd
            def _(pool):
                arrived(pool, g, "L1_ffn")
                with pool.Fori(1, TURNS + 1) as i:
                    for s in range(NS):
                        pool.wait_ge(ln.s_xn[s], i)
                        pool.tensor_tensor(tile_of(g, i, s), tile_of(g, i, s), w["b2"], ALU.add).then_inc(s_bo[s], 1)

            @block.scalar
            def _(act):
                ln.scalar_start(act)
                with act.Fori(1, TURNS + 1) as i:
                    both = [act.snap(NS * i - NS + 1 + s) for s in range(NS)]
                    for s in range(NS):
                        act.wait_ge(ln.s_xn[s], i)
                        act.activation(xs[s][:, :], ln.xn[s][:, :], ACT.Square, accum_out=ss[:, 0, s:s + 1]
                                       ).then_inc(s_sq[0], 1)
                    for s in range(NS):
                        act.wait_ge(s_ch[0], 5 * i)
                        act.wait_ge(s_sq[0], both[s])
                        act.activation(xs[s][:, :], ln.xn[s][:, :], ACT.Identity, bias=g.magic[:, 0:1],
                                       scale=fac[:, 0, s:s + 1]).then_inc(s_scaled[0], 1)
                    for s in range(NS):
                        act.wait_ge(s_qT_ps[0], both[s])
                        act.copy(xqT[s][:, :, :], bank[s][3][:, :].bitcast(BF16)[:, 0:D]
                                 .rearrange("p (c t) -> p c t", c=DC)).then_inc(s_qT[0], 1)
                    for s in range(NS):
                        act.wait_ge(s_h[s], 2 * i)
                        act.activation(hh[s][:, :], hh[s][:, :], ACT.Gelu).then_inc(s_gelu[s], 1)
                    for s in range(NS):
                        act.wait_ge(s_gelu[s], i)
                        act.activation(hs[s][:, :], hh[s][:, :], ACT.Square, accum_out=ss[:, 1, s:s + 1]
                                       ).then_inc(s_sq[1], 1)
                    for s in range(NS):
                        act.wait_ge(s_ch[1], 5 * i)
                        act.wait_ge(s_sq[1], both[s])
                        act.activation(hs[s][:, :], hh[s][:, :], ACT.Identity, bias=g.magic[:, 0:1],
                                       scale=fac[:, 1, s:s + 1]).then_inc(s_scaled[1], 1)
                    for s in range(NS):
                        act.wait_ge(s_qT_ps[1], both[s])
                        act.copy(hqT[s][:, :, :], bank[s][2][:, :].bitcast(BF16).rearrange("p (c t) -> p c t", c=FC)
                                 ).then_inc(s_qT[1], 1)

            @block.vector
            def _(dve):
                arrived(dve, g, "L1_ffn")
                ln.vector_start(dve)
                with dve.Fori(1, TURNS + 1) as i:
                    both = [dve.snap(NS * i - NS + 1 + s) for s in range(NS)]

                    def factors(k):
                        dve.wait_ge(s_sq[k], NS * i)
                        dve.wait_ge(s_am[k], NS * i)
                        width = D if k == 0 else F
                        r = rs[k].vector(dve, ss[:, k, :], 1.0 / width, 1e-5, i)
                        n = 5 * i - 5
                        dve.tensor_tensor(tmp[:, k, :], r, am[:, k, :], ALU.mult).then_inc(s_ch[k], 1)
                        dve.wait_ge(s_ch[k], n + 1)
                        dve.tensor_scalar(tmp[:, k, :], tmp[:, k, :], 1e-5, 1.0 / QMAX, ALU.max,
                                          ALU.mult).then_inc(s_ch[k], 1)
                        dve.wait_ge(s_ch[k], n + 2)
                        dve.tensor_scalar(deq[:, k, :], tmp[:, k, :], wmean[:, k:k + 1], None, ALU.mult
                                          ).then_inc(s_ch[k], 1)
                        dve.reciprocal(fac[:, k, :], tmp[:, k, :]).then_inc(s_ch[k], 1)
                        dve.wait_ge(s_ch[k], n + 4)
                        dve.tensor_tensor(fac[:, k, :], fac[:, k, :], r, ALU.mult).then_inc(s_ch[k], 1)

                    for s in range(NS):
                        ln.vector_apply(dve, s, i)
                    for s in range(NS):
                        dve.wait_ge(ln.s_xn[s], i)
                        dve.tensor_reduce(am[:, 0, s:s + 1], ln.xn[s][:, :], AX.X, ALU.max, apply_absolute_value=True).then_inc(s_am[0], 1)
                    factors(0)
                    for s in range(NS):
                        dve.wait_ge(s_scaled[0], both[s])
                        dve.tensor_scalar(xq[s][:, :], xs[s][:, :], MAGIC, None, ALU.subtract).then_inc(s_q[0], 1)
                    for s in range(NS):
                        for m in range(2):
                            dve.wait_ge(s_h_ps[s], 2 * i - 1 + m)
                            dve.scalar_tensor_tensor(out=hh[s][:, m * BANK:(m + 1) * BANK], in0=bank[s][m][:, :],
                                                     scalar=deq[:, 0, s:s + 1], in1=w["b1"][:, m * BANK:(m + 1) * BANK],
                                                     op0=ALU.mult, op1=ALU.add).then_inc(s_h[s], 1)
                    for s in range(NS):
                        dve.wait_ge(s_gelu[s], i)
                        dve.tensor_reduce(am[:, 1, s:s + 1], hh[s][:, :], AX.X, ALU.max, apply_absolute_value=True).then_inc(s_am[1], 1)
                    factors(1)
                    for s in range(NS):
                        dve.wait_ge(s_scaled[1], both[s])
                        dve.tensor_scalar(hq[s][:, :], hs[s][:, :], MAGIC, None, ALU.subtract).then_inc(s_q[1], 1)
                    for s in range(NS):
                        dve.wait_ge(s_y[s], i)
                        dve.wait_ge(s_bo[s], i)
                        dve.scalar_tensor_tensor(out=tile_of(g, i, s), in0=bank[s][3][:, 256:256 + D],
                                                 scalar=deq[:, 1, s:s + 1], in1=tile_of(g, i, s), op0=ALU.mult,
                                                 op1=ALU.add).then_inc(s_x[s], 1)
                    for s in range(NS):
                        ln.vector_stats(dve, s, i, s_x)

            @block.tensor
            def _(pe):
                with pe.Fori(1, TURNS + 1) as i:
                    both = [pe.snap(NS * i - NS + 1 + s) for s in range(NS)]
                    for s in range(NS):
                        pe.wait_ge(s_q[0], both[s])
                        for c in range(DC):
                            mm = pe.transpose(bank[s][3][:, :].bitcast(BF16)[:, c * P:c * P + P],
                                              xq[s][:, c * P:c * P + P], identb[:, :])
                        mm.then_inc(s_qT_ps[0], 1)
                    for s in range(NS):
                        pe.wait_ge(s_qT[0], both[s])
                        for m in range(2):
                            for c in range(DC):
                                mm = pe.matmul(bank[s][m][:, :], xqT[s][:, c, :], w1T[:, c, m * BANK:(m + 1) * BANK],
                                               start=(c == 0), stop=(c == DC - 1))
                            mm.then_inc(s_h_ps[s], 1)
                    for s in range(NS):
                        pe.wait_ge(s_q[1], both[s])
                        for f in range(FC):
                            mm = pe.transpose(bank[s][2][:, :].bitcast(BF16)[:, f * P:f * P + P],
                                              hq[s][:, f * P:f * P + P], identb[:, :])
                        mm.then_inc(s_qT_ps[1], 1)
                    for s in range(NS):
                        pe.wait_ge(s_qT[1], both[s])
                        for f in range(FC):
                            mm = pe.matmul(bank[s][3][:, 256:256 + D], hqT[s][:, f, :], w2T[:, f, :], start=(f == 0),
                                           stop=(f == FC - 1))
                        mm.then_inc(s_y[s], 1)


class TopTwo:
    STEPS = 9

    def __init__(self, sec, name, rows, n):
        self.rows, self.n = rows, n
        self.m, self.c, self.f = sec.sb(f"{name}_m", [rows, 2]), sec.sb(f"{name}_c", [rows, 2, n]), sec.sb(f"{name}_f", [rows, 2])
        self.one, self.rest = sec.sb(f"{name}_one", [rows, 2, n]), sec.sb(f"{name}_rest", [rows, n])
        self.s = sec.sem(f"{name}_step")

    def vector(self, dve, g, lg, i):
        n = TopTwo.STEPS * (i - 1)

        def link(k, ins):
            ins.then_inc(self.s, 1)
            dve.wait_ge(self.s, n + k)
        order = g.order[0:self.rows, 0:self.n]
        src = lg
        for k in range(2):
            m, c, f, one = self.m[:, k:k + 1], self.c[:, k, :], self.f[:, k:k + 1], self.one[:, k, :]
            link(5 * k + 1, dve.tensor_reduce(m, src, AX.X, ALU.max))
            link(5 * k + 2, dve.scalar_tensor_tensor(out=c, in0=src, scalar=m, in1=order, op0=ALU.is_equal, op1=ALU.mult))
            link(5 * k + 3, dve.tensor_reduce(f, c, AX.X, ALU.max))
            link(5 * k + 4, dve.tensor_scalar(one, c, f, None, ALU.is_equal))
            if k == 0:
                link(5, dve.scalar_tensor_tensor(out=self.rest[:, :], in0=one, scalar=-BIG, in1=lg, op0=ALU.mult,
                                                 op1=ALU.add))
                src = self.rest[:, :]


def lora_ffn(nc, g, w):
    sec = Section(nc, "L2f")
    E, R, F = 8, 16, 1024
    FC = F // P
    with sec:
        ln = LayerNorm(sec, g)
        bank = banks_of(sec)
        sbs = lambda nm, shape, dt=F32: [sec.sb(f"{nm}{s}", shape, dt) for s in range(NS)]
        wiT, woT, bT = sec.sb("wiT", [P, DC, F]), sec.sb("woT", [P, FC, D]), sec.sb("loraBT", [P, F])
        agT = sec.sb("loraA_gateT", [P, DC, P + E])
        bo2 = sec.sb("bo2", [P, D])
        xT, lg, dl = sbs("xT", [P, DC, P]), sbs("logits", [P, E]), sbs("dl", [P, E + 1])
        tk = [TopTwo(sec, f"top{s}", P, E) for s in range(NS)]
        den, vs = sbs("den", [P, 2]), sbs("vs", [P, 1])
        diff = sbs("diff", [P, E])
        ta, tb = sbs("ta", [P, 2, P]), sbs("taT", [P, 2, P])
        u1, u2, hs = sbs("u1", [P, 4, P]), sbs("u2", [P, 4, P]), sbs("hs", [P, FC, P])
        y = sbs("y", [P, D])
        jobs = [(w["wi"][:, f, c * P:c * P + P], wiT[:, c, f * P:f * P + P]) for c in range(DC) for f in range(FC)]
        jobs += [(w["wo"][:, c, f * P:f * P + P], woT[:, f, c * P:c * P + P]) for f in range(FC) for c in range(DC)]
        jobs += [(w["lora_B"][:, f, :], bT[:, f * P:f * P + P]) for f in range(FC)]
        jobs += [(w["lora_A"][:, c * P:c * P + P], agT[:, c, 0:P]) for c in range(DC)]
        jobs += [(w["gate_w"][:, c * P:c * P + P], agT[:, c, P:P + E]) for c in range(DC)]
        turn_w = Turned(sec, [bank[0][0], bank[1][0]], jobs)
        (s_xT_ps, s_xT, s_t_ps, s_lg, s_dl, s_e, s_vs, s_diff, s_ta, s_taT_ps, s_taT, s_u_ps, s_v_ps, s_u1, s_r1,
         s_u2, s_hs, s_y_ps, s_y, s_x, s_den) = (sec.per_stream(n) for n in (
             "xT_ps", "xT", "lora_ps", "logits", "shifted", "exp", "val_sum", "mask_diff", "masked", "maskedT_ps",
             "maskedT", "first_ps", "second_ps", "first", "first_relu", "second", "hidden", "y_ps", "y", "x_done",
             "den"))
        s_bo2 = sec.sem("bo2")
        with sec.block() as block:
            @block.tensor
            def _(pe):
                arrived(pe, g, "L2_ffn")
                turn_w.tensor(pe, g.ident)
                turn_w.wait(pe)
                with pe.Fori(1, TURNS + 1) as i:
                    nth = [pe.snap(2 * i - 1 + t) for t in range(2)]
                    for s in range(NS):
                        pe.wait_ge(ln.s_xn[s], i)
                        for c in range(DC):
                            mm = pe.transpose(bank[s][3][:, c * P:c * P + P], ln.xn[s][:, c * P:c * P + P], g.ident[:, :])
                        mm.then_inc(s_xT_ps[s], 1)
                    for s in range(NS):
                        pe.wait_ge(s_xT[s], i)
                        for c in range(DC):
                            mm = pe.matmul(bank[s][2][:, 0:P + E], xT[s][:, c, :], agT[:, c, :], start=(c == 0),
                                           stop=(c == DC - 1))
                        mm.then_inc(s_t_ps[s], 1)

                    def first(s, t):
                        for m in range(4):
                            f = 4 * t + m
                            for c in range(DC):
                                pe.matmul(bank[s][t][:, m * P:m * P + P], wiT[:, c, f * P:f * P + P], xT[s][:, c, :],
                                          start=(m == 0 and c == 0), stop=False, skip_group_check=True)

                    def expert(s, t, k, s_done):
                        for m in range(4):
                            f = 4 * t + m
                            mm = pe.matmul(bank[s][t][:, m * P:m * P + P], bT[:, f * P:f * P + P], tb[s][:, k, :],
                                           start=False, stop=(k == 1), skip_group_check=True)
                        mm.then_inc(s_done[s], 1)

                    for s in range(NS):
                        for t in range(2):
                            first(s, t)
                    for s in range(NS):
                        pe.wait_ge(s_ta[s], i)
                        for k in range(2):
                            mm = pe.transpose(bank[s][2][:, 256 + k * P:256 + (k + 1) * P], ta[s][:, k, :], g.ident[:, :])
                        mm.then_inc(s_taT_ps[s], 1)
                    for s in range(NS):
                        pe.wait_ge(s_taT[s], i)
                        for t in range(2):
                            expert(s, t, 0, s_u_ps)
                    for s in range(NS):
                        for t in range(2):
                            pe.wait_ge(s_u1[s], nth[t])
                            expert(s, t, 1, s_v_ps)
                    for s in range(NS):
                        for t in range(2):
                            pe.wait_ge(s_hs[s], nth[t])
                            for f in range(4 * t, 4 * t + 4):
                                mm = pe.matmul(bank[s][3][:, 0:D], hs[s][:, f, :], woT[:, f, :], start=(f == 0),
                                               stop=(f == FC - 1))
                        mm.then_inc(s_y_ps[s], 1)

            @block.scalar
            def _(act):
                turn_w.scalar(act)
                ln.scalar_start(act)
                with act.Fori(1, TURNS + 1) as i:
                    nth = [act.snap(2 * i - 1 + t) for t in range(2)]
                    for s in range(NS):
                        act.wait_ge(s_xT_ps[s], i)
                        act.copy(xT[s][:, :, :], bank[s][3][:, 0:D].rearrange("p (c t) -> p c t", c=DC)).then_inc(s_xT[s], 1)
                    for s in range(NS):
                        act.wait_ge(s_dl[s], 2 * i)
                        act.activation(dl[s][:, :], dl[s][:, :], ACT.Exp).then_inc(s_e[s], 1)
                    for s in range(NS):
                        act.wait_ge(s_taT_ps[s], i)
                        act.copy(tb[s][:, :, :], bank[s][2][:, 256:512].rearrange("p (k t) -> p k t", k=2)).then_inc(s_taT[s], 1)
                    for s in range(NS):
                        for t in range(2):
                            act.wait_ge(s_u1[s], nth[t])
                            act.activation(hs[s][:, 4 * t:4 * t + 4, :], hs[s][:, 4 * t:4 * t + 4, :], ACT.Relu
                                           ).then_inc(s_r1[s], 1)

            @block.gpsimd
            def _(pool):
                arrived(pool, g, "L2_ffn")
                pool.tensor_tensor(bo2[:, :], w["bo"], w["bo"], ALU.add).then_inc(s_bo2, 1)

            @block.vector
            def _(dve):
                arrived(dve, g, "L2_ffn")
                dve.wait_ge(s_bo2, 1)
                ln.vector_start(dve)
                with dve.Fori(1, TURNS + 1) as i:
                    nth = [dve.snap(2 * i - 1 + t) for t in range(2)]
                    for s in range(NS):
                        ln.vector_apply(dve, s, i)
                    for s in range(NS):
                        t_ps = bank[s][2]
                        dve.wait_ge(s_t_ps[s], i)
                        dve.tensor_tensor(lg[s][:, :], t_ps[:, P:P + E], w["gate_b"], ALU.add).then_inc(s_lg[s], 1)
                        dve.wait_ge(s_lg[s], i)
                        tk[s].vector(dve, g, lg[s][:, :], i)
                        one = tk[s].one
                        dve.tensor_scalar(dl[s][:, 0:E], lg[s][:, :], tk[s].m[:, 0:1], None, ALU.subtract).then_inc(s_dl[s], 1)
                        dve.tensor_scalar(dl[s][:, E:E + 1], tk[s].m[:, 1:2], tk[s].m[:, 0:1], None, ALU.subtract
                                          ).then_inc(s_dl[s], 1)
                        dve.tensor_tensor(diff[s][:, :], one[:, 1, :], one[:, 0, :], ALU.subtract).then_inc(s_diff[s], 1)
                        er = lambda ap: ap.rearrange("p (e r) -> p e r", e=E)
                        dve.tensor_tensor(er(ta[s][:, 0, :]), er(t_ps[:, 0:P]),
                                          one[:, 0, :].unsqueeze(2).to_broadcast([P, E, R]), ALU.mult)
                        dve.wait_ge(s_diff[s], i)
                        dve.tensor_tensor(er(ta[s][:, 1, :]), er(t_ps[:, 0:P]),
                                          diff[s][:, :].unsqueeze(2).to_broadcast([P, E, R]), ALU.mult).then_inc(s_ta[s], 1)
                    for s in range(NS):
                        dve.wait_ge(s_e[s], i)
                        dve.tensor_reduce(den[s][:, 0:1], dl[s][:, 0:E], AX.X, ALU.add).then_inc(s_den[s], 1)
                        dve.wait_ge(s_den[s], 2 * i - 1)
                        dve.reciprocal(den[s][:, 1:2], den[s][:, 0:1]).then_inc(s_den[s], 1)
                        dve.wait_ge(s_den[s], 2 * i)
                        dve.scalar_tensor_tensor(out=vs[s][:, :], in0=dl[s][:, E:E + 1], scalar=1.0, in1=den[s][:, 1:2],
                                                 op0=ALU.add, op1=ALU.mult).then_inc(s_vs[s], 1)
                    bi = lambda t: w["bi"][:, 4 * t:4 * t + 4].unsqueeze(2).to_broadcast([P, 4, P])
                    ps = lambda s, t: bank[s][t][:, :].rearrange("p (m t) -> p m t", m=4)
                    for s in range(NS):
                        for t in range(2):
                            dve.wait_ge(s_u_ps[s], nth[t])
                            dve.tensor_tensor(hs[s][:, 4 * t:4 * t + 4, :], ps(s, t), bi(t), ALU.add).then_inc(s_u1[s], 1)
                    for s in range(NS):
                        for t in range(2):
                            u = (u1, u2)[t][s]
                            dve.wait_ge(s_v_ps[s], nth[t])
                            dve.tensor_tensor(u[:, :, :], ps(s, t), bi(t), ALU.add).then_inc(s_u2[s], 1)
                            dve.wait_ge(s_u2[s], nth[t])
                            dve.wait_ge(s_r1[s], nth[t])
                            dve.scalar_tensor_tensor(out=hs[s][:, 4 * t:4 * t + 4, :], in0=u[:, :, :], scalar=0.0,
                                                     in1=hs[s][:, 4 * t:4 * t + 4, :], op0=ALU.max, op1=ALU.add
                                                     ).then_inc(s_hs[s], 1)
                    for s in range(NS):
                        dve.wait_ge(s_y_ps[s], i)
                        dve.tensor_tensor(y[s][:, :], bank[s][3][:, 0:D], bo2[:, :], ALU.add).then_inc(s_y[s], 1)
                        dve.wait_ge(s_y[s], i)
                        dve.wait_ge(s_vs[s], i)
                        dve.scalar_tensor_tensor(out=tile_of(g, i, s), in0=y[s][:, :], scalar=vs[s][:, 0:1],
                                                 in1=tile_of(g, i, s), op0=ALU.mult, op1=ALU.add).then_inc(s_x[s], 1)
                    for s in range(NS):
                        ln.vector_stats(dve, s, i, s_x)


def gated_attention(nc, g, w, ctx_dram):
    sec = Section(nc, "L3a")
    SCALE = D ** -0.5
    with sec:
        ln = LayerNorm(sec, g)
        bank = banks_of(sec)
        sbs = lambda nm, shape, dt=F32: [sec.sb(f"{nm}{s}", shape, dt) for s in range(NS)]
        qk, gwT = sec.sb("qk", [P, DC, D]), sec.sb("gate_wT", [P, DC, D])
        mem, memT = sbs("mem", [P, D]), sbs("memT", [P, DC, P])
        ss, rs = sec.sb("ss", [P, NS]), Rsqrt(sec, "rs", NS)
        sq, nm = sbs("squares", [P, D]), sbs("nm", [P, D])
        xT, nmT, qT = sbs("xT", [P, DC, P]), sbs("nmT", [P, DC, P]), sbs("qT", [P, DC, P])
        lgt, pT = sbs("logits", [P, 2, P]), sbs("probsT", [P, 2, P])
        mx, den = sbs("mx", [P, 2]), sbs("den", [P, 2])
        z, d = sbs("z", [P, D]), sbs("d", [P, D])
        jobs = [(w["gate_w"][:, m, c * P:c * P + P], gwT[:, c, m * P:m * P + P]) for m in range(DC) for c in range(DC)]
        turn_w = Turned(sec, [bank[0][0], bank[1][0]], jobs)
        s_qk_ps, s_qk, s_sq = sec.sem("qk_ps"), sec.sem("qk"), sec.sem("sumsq")
        (s_mem, s_memT, s_nm, s_xT_ps, s_xT, s_q_ps, s_q, s_z_ps, s_z, s_ez, s_ap1, s_al, s_l_ps, s_lg, s_mx, s_nb,
         s_p, s_pT_ps, s_pT, s_h, s_rd, s_d1, s_d2, s_d3, s_x, s_nmT_ps, s_nmT) = (sec.per_stream(n) for n in (
             "mem", "memT", "normed", "xT_ps", "xT", "q_ps", "q", "z_ps", "z", "exp_z", "alpha1", "alpha", "logits_ps",
             "logits", "max", "neg_max", "probs", "probsT_ps", "probsT", "h_tilde", "recip", "d1", "d2", "d3",
             "x_done", "nmT_ps", "nmT"))
        with sec.block() as block:
            @block.sync
            def _(sp):
                for s in range(NS):
                    sp.dma_start(mem[s][:, :], ctx_dram[s, :, :]).then_inc(s_mem[s], 16)
                    sp.dma_start(memT[s][:, :, :], g.ctxT[:, s, :, :]).then_inc(s_memT[s], 16)
                with sp.Fori(1, TURNS) as i:
                    for s in range(NS):
                        sp.wait_ge(s_h[s], i)
                        sp.dma_start(mem[s][:, :], ctx_dram[NS * i + s, :, :]).then_inc(s_mem[s], 16)
                        sp.dma_start(memT[s][:, :, :], g.ctxT[:, NS * i + s, :, :]).then_inc(s_memT[s], 16)

            @block.tensor
            def _(pe):
                arrived(pe, g, "L3_xattn")
                turn_w.tensor(pe, g.ident)
                for m in range(DC):
                    for c in range(DC):
                        mm = pe.matmul(bank[0][2][:, m * D:m * D + D], w["q_w"][:, c, m * P:m * P + P], w["k_w"][:, c, :],
                                       start=(c == 0), stop=(c == DC - 1))
                mm.then_inc(s_qk_ps, 1)
                turn_w.wait(pe)
                pe.wait_ge(s_qk, 1)
                with pe.Fori(1, TURNS + 1) as i:
                    def turn(s, src, out, s_done):
                        for c in range(DC):
                            mm = pe.transpose(out[:, c * P:c * P + P], src[s][:, c * P:c * P + P], g.ident[:, :])
                        mm.then_inc(s_done[s], 1)
                    for s in range(NS):
                        pe.wait_ge(ln.s_xn[s], i)
                        turn(s, ln.xn, bank[s][3], s_xT_ps)
                    for s in range(NS):
                        pe.wait_ge(s_xT[s], i)
                        for c in range(DC):
                            mm = pe.matmul(bank[s][2][:, 0:D], xT[s][:, c, :], gwT[:, c, :], start=(c == 0),
                                           stop=(c == DC - 1))
                        mm.then_inc(s_z_ps[s], 1)
                    for s in range(NS):
                        pe.wait_ge(s_nm[s], i)
                        turn(s, nm, bank[s][3], s_nmT_ps)
                    for s in range(NS):
                        pe.wait_ge(s_nmT[s], i)
                        for m in range(DC):
                            for c in range(DC):
                                mm = pe.matmul(bank[s][0][:, m * P:m * P + P], qk[:, c, m * P:m * P + P], nmT[s][:, c, :],
                                               start=(c == 0), stop=(c == DC - 1))
                        mm.then_inc(s_q_ps[s], 1)
                    for s in range(NS):
                        pe.wait_ge(s_q[s], i)
                        pe.wait_ge(s_memT[s], 16 * i)
                        for k, keys in enumerate((nmT, memT)):
                            for c in range(DC):
                                mm = pe.matmul(bank[s][1][:, k * P:k * P + P], qT[s][:, c, :], keys[s][:, c, :],
                                               start=(c == 0), stop=(c == DC - 1))
                        mm.then_inc(s_l_ps[s], 1)
                    for s in range(NS):
                        pe.wait_ge(s_p[s], i)
                        for k in range(2):
                            mm = pe.transpose(bank[s][3][:, k * P:k * P + P], lgt[s][:, k, :], g.ident[:, :])
                        mm.then_inc(s_pT_ps[s], 1)
                    for s in range(NS):
                        pe.wait_ge(s_pT[s], i)
                        pe.wait_ge(s_mem[s], 16 * i)
                        pe.matmul(bank[s][0][:, 0:D], pT[s][:, 0, :], nm[s][:, :], start=True, stop=False)
                        pe.matmul(bank[s][0][:, 0:D], pT[s][:, 1, :], mem[s][:, :], start=False, stop=True
                                  ).then_inc(s_h[s], 1)

            @block.scalar
            def _(act):
                turn_w.scalar(act)
                act.wait_ge(s_qk_ps, 1)
                act.copy(qk[:, :, :], bank[0][2][:, :].rearrange("p (c n) -> p c n", c=DC)).then_inc(s_qk, 1)
                ln.scalar_start(act)
                two = lambda ap: ap[:, 0:D].rearrange("p (c t) -> p c t", c=DC)
                with act.Fori(1, TURNS + 1) as i:
                    for s in range(NS):
                        act.wait_ge(ln.s_xn[s], i)
                        act.activation(sq[s][:, :], ln.xn[s][:, :], ACT.Square, accum_out=ss[:, s:s + 1]).then_inc(s_sq, 1)
                    for s in range(NS):
                        act.wait_ge(s_xT_ps[s], i)
                        act.copy(xT[s][:, :, :], two(bank[s][3])).then_inc(s_xT[s], 1)
                    for s in range(NS):
                        act.wait_ge(s_nmT_ps[s], i)
                        act.copy(nmT[s][:, :, :], two(bank[s][3])).then_inc(s_nmT[s], 1)
                    for s in range(NS):
                        act.wait_ge(s_q_ps[s], i)
                        act.copy(qT[s][:, :, :], two(bank[s][0])).then_inc(s_q[s], 1)
                    for s in range(NS):
                        act.wait_ge(s_z[s], i)
                        act.activation(z[s][:, :], z[s][:, :], ACT.Exp, scale=-1.0).then_inc(s_ez[s], 1)
                    for s in range(NS):
                        act.wait_ge(s_nb[s], i)
                        act.activation(lgt[s][:, :, :], lgt[s][:, :, :], ACT.Exp, bias=mx[s][:, 1:2], scale=SCALE,
                                       accum_out=den[s][:, 0:1]).then_inc(s_p[s], 1)
                    for s in range(NS):
                        act.wait_ge(s_pT_ps[s], i)
                        act.copy(pT[s][:, :, :], two(bank[s][3])).then_inc(s_pT[s], 1)

            @block.vector
            def _(dve):
                arrived(dve, g, "L3_xattn")
                ln.vector_start(dve)
                with dve.Fori(1, TURNS + 1) as i:
                    for s in range(NS):
                        ln.vector_apply(dve, s, i)
                    dve.wait_ge(s_sq, NS * i)
                    r = rs.vector(dve, ss[:, :], 1.0 / D, 1e-6, i)
                    for s in range(NS):
                        dve.scalar_tensor_tensor(out=nm[s][:, :], in0=ln.xn[s][:, :], scalar=r[:, s:s + 1], in1=w["norm_w"],
                                                 op0=ALU.mult, op1=ALU.mult).then_inc(s_nm[s], 1)
                    for s in range(NS):
                        dve.wait_ge(s_z_ps[s], i)
                        dve.tensor_tensor(z[s][:, :], bank[s][2][:, 0:D], w["gate_b"], ALU.add).then_inc(s_z[s], 1)
                    for s in range(NS):
                        dve.wait_ge(s_l_ps[s], i)
                        dve.tensor_tensor(lgt[s][:, :, :], bank[s][1][:, 0:D].rearrange("p (k t) -> p k t", k=2),
                                          g.causal[:, :, :], ALU.add).then_inc(s_lg[s], 1)
                        dve.wait_ge(s_lg[s], i)
                        dve.tensor_reduce(mx[s][:, 0:1], lgt[s][:, :, :], AX.XY, ALU.max).then_inc(s_mx[s], 1)
                        dve.wait_ge(s_mx[s], i)
                        dve.tensor_scalar(mx[s][:, 1:2], mx[s][:, 0:1], -SCALE, None, ALU.mult).then_inc(s_nb[s], 1)
                    for s in range(NS):
                        dve.wait_ge(s_ez[s], i)
                        dve.tensor_scalar(z[s][:, :], z[s][:, :], 1.0, None, ALU.add).then_inc(s_ap1[s], 1)
                        dve.wait_ge(s_ap1[s], i)
                        dve.reciprocal(z[s][:, :], z[s][:, :]).then_inc(s_al[s], 1)
                    for s in range(NS):
                        dve.wait_ge(s_p[s], i)
                        dve.reciprocal(den[s][:, 1:2], den[s][:, 0:1]).then_inc(s_rd[s], 1)
                    for s in range(NS):
                        dve.wait_ge(s_rd[s], i)
                        dve.wait_ge(s_al[s], i)
                        dve.wait_ge(s_h[s], i)
                        dve.scalar_tensor_tensor(out=d[s][:, :], in0=bank[s][0][:, 0:D], scalar=den[s][:, 1:2],
                                                 in1=ln.xn[s][:, :], op0=ALU.mult, op1=ALU.subtract).then_inc(s_d1[s], 1)
                        dve.wait_ge(s_d1[s], i)
                        dve.tensor_tensor(d[s][:, :], d[s][:, :], z[s][:, :], ALU.mult).then_inc(s_d2[s], 1)
                        dve.wait_ge(s_d2[s], i)
                        dve.tensor_tensor(d[s][:, :], d[s][:, :], ln.xn[s][:, :], ALU.add).then_inc(s_d3[s], 1)
                        dve.wait_ge(s_d3[s], i)
                        dve.tensor_tensor(tile_of(g, i, s), d[s][:, :], tile_of(g, i, s), ALU.add).then_inc(s_x[s], 1)
                    for s in range(NS):
                        ln.vector_stats(dve, s, i, s_x)


def expert_gates(nc, g, w):
    sec = Section(nc, "L3g")
    E, HID = 4, 128
    with sec:
        ln = LayerNorm(sec, g)
        bank = banks_of(sec)
        mean = sec.sb("mean", [P, 1])
        pooled, hid = sec.sb("pooled", [P, DC, NB]), sec.sb("hid", [HID, NB])
        lg, dg = sec.sb("logits", [NB, E]), sec.sb("spread", [NB, NB, E])
        sw = sec.sb("shares", [NB, 4])
        wt = sec.sb("weights", [NB, 2, E])
        tk = TopTwo(sec, "top", NB, E)
        s_mean, s_ps, s_pool, s_hid_ps, s_hid, s_lg_ps, s_lg, s_e, s_st, s_g_ps = (sec.sem(n) for n in (
            "mean_column", "pooled_ps", "pooled", "hidden_ps", "hidden", "logits_ps", "logits", "exp", "steps",
            "gates_ps"))
        s_pp, s_pd = sec.per_stream("mean_ps"), sec.per_stream("mean_out")
        with sec.block() as block:
            @block.tensor
            def _(pe):
                arrived(pe, g, "L3_ffn")
                pe.wait_ge(s_mean, 1)
                with pe.Fori(1, TURNS + 1) as i:
                    for s in range(NS):
                        pe.wait_ge(ln.s_xn[s], i)
                        for c in range(DC):
                            mm = pe.matmul(bank[s][0][:, c:c + 1], ln.xn[s][:, c * P:c * P + P], mean[:, 0:1], start=True,
                                           stop=True)
                        mm.then_inc(s_pp[s], 1)
                for s in range(NS):
                    pe.wait_ge(s_pd[s], TURNS)
                for c in range(DC):
                    mm = pe.matmul(bank[0][1][0:HID, 0:NB], w["Wg1"][:, c, :], pooled[:, c, :], start=(c == 0),
                                   stop=(c == DC - 1))
                mm.then_inc(s_hid_ps, 1)
                pe.wait_ge(s_hid, 1)
                pe.matmul(bank[0][2][0:NB, 0:E], hid[:, :], w["Wg2"][:, 0, :], start=True, stop=True).then_inc(s_lg_ps, 1)
                pe.wait_ge(s_st, 6)
                pe.matmul(bank[0][3][:, 0:NB * E], g.onesP[0:NB, :], dg[:, :, :], start=True, stop=True).then_inc(s_g_ps, 1)

            @block.scalar
            def _(act):
                arrived(act, g, "L3_ffn")
                ln.scalar_start(act)
                act.wait_ge(s_hid_ps, 1)
                act.activation(hid[:, :], bank[0][1][0:HID, 0:NB], ACT.Relu, bias=w["bg1"][:, 0:1]).then_inc(s_hid, 1)
                act.wait_ge(s_st, 1)
                act.activation(sw[:, 1:2], sw[:, 0:1], ACT.Exp).then_inc(s_e, 1)

            @block.vector
            def _(dve):
                arrived(dve, g, "L3_ffn")
                dve.memset(mean[:, :], 1.0 / P).then_inc(s_mean, 1)
                ln.vector_start(dve)
                with dve.Fori(1, TURNS + 1) as i:
                    for s in range(NS):
                        ln.vector_apply(dve, s, i)
                    for s in range(NS):
                        dve.wait_ge(s_pp[s], i)
                        dve.tensor_copy(pooled[:, :, NS * (i - 1) + s], bank[s][0][:, 0:DC]).then_inc(s_pd[s], 1)
                dve.wait_ge(s_lg_ps, 1)
                dve.tensor_tensor(lg[:, :], bank[0][2][0:NB, 0:E], w["bg2"][0:NB, :], ALU.add).then_inc(s_lg, 1)
                dve.wait_ge(s_lg, 1)
                tk.vector(dve, g, lg[:, :], 1)
                dve.tensor_scalar(sw[:, 0:1], tk.m[:, 1:2], tk.m[:, 0:1], None, ALU.subtract).then_inc(s_st, 1)
                dve.wait_ge(s_e, 1)
                dve.tensor_scalar(sw[:, 2:3], sw[:, 1:2], 1.0, None, ALU.add).then_inc(s_st, 1)
                dve.wait_ge(s_st, 2)
                dve.reciprocal(sw[:, 2:3], sw[:, 2:3]).then_inc(s_st, 1)
                dve.wait_ge(s_st, 3)
                dve.tensor_tensor(sw[:, 3:4], sw[:, 2:3], sw[:, 1:2], ALU.mult)
                dve.tensor_scalar(wt[:, 0, :], tk.one[:, 0, :], sw[:, 2:3], None, ALU.mult).then_inc(s_st, 1)
                dve.wait_ge(s_st, 4)
                dve.scalar_tensor_tensor(out=wt[:, 1, :], in0=tk.one[:, 1, :], scalar=sw[:, 3:4], in1=wt[:, 0, :],
                                         op0=ALU.mult, op1=ALU.add).then_inc(s_st, 1)
                dve.wait_ge(s_st, 5)
                dve.tensor_tensor(dg[:, :, :], g.ident[0:NB, 0:NB].unsqueeze(2).to_broadcast([NB, NB, E]),
                                  wt[:, 1, :].unsqueeze(1).to_broadcast([NB, NB, E]), ALU.mult).then_inc(s_st, 1)
                dve.wait_ge(s_g_ps, 1)
                dve.tensor_copy(g.gates[:, :, :, 0], bank[0][3][:, 0:NB * E].rearrange("p (b e) -> p b e", e=E))


def start_loads(nc, g):
    sec = Section(nc, "loads")
    with sec, sec.block() as block:
        @block.sync
        def _(sp):
            for dst, src, what in g.loads:
                sp.dma_start(dst, src, allow_slow_non_contiguous=True).then_inc(g.loaded[what], 16)


def finish(nc, g, out):
    sec = Section(nc, "finish")
    with sec:
        s_out = sec.sem("out")
        with sec.block() as block:
            @block.sync
            def _(sp):
                sp.dma_start(out.rearrange("b p d -> p b d"), g.x[:, :, :]).then_inc(s_out, 16)
                sp.wait_ge(s_out, 16)


def program(nc, a, out):
    g = Globals()
    with ExitStack() as whole:
        scope = [whole]

        def sb(name, shape, dt=F32):
            return scope[-1].enter_context(nc.sbuf_tensor(name, shape, dt))

        g.loads, g.counts = [], {"x": 1}
        g.loaded = {"x": nc.alloc_semaphore("x_loaded")}

        def loading(what, dst, src):
            if what not in g.loaded:
                g.loaded[what] = nc.alloc_semaphore(f"{what}_loaded")
                g.counts[what] = 0
            g.counts[what] += 1
            g.loads.append((dst, src, what))

        def load(what, name, shape, src, dt=F32):
            t = sb(name, shape, dt)
            t = t[tuple(slice(None) for _ in shape)]
            loading(what, t, src)
            return t

        def matrix(what, name):
            r, n = a[name].shape
            return load(what, name, [P, r // P, n], a[name].rearrange("(c p) n -> p c n", p=P))

        def column(what, name):
            return load(what, name, [P, a[name].shape[0] // P], a[name].rearrange("(c p) -> p c", p=P))

        def row(what, name):
            return load(what, name, [P, a[name].shape[0]], a[name].partition_broadcast(P))

        g.x = sb("x_all", [P, NB, D])
        g.stats = sb("stats", [P, NB, 6])
        g.ctxT = sb("ctxT_all", [P, NB, DC, P])
        g.ident, g.hmask, g.causal = sb("ident", [P, P]), sb("hmask", [P, HC]), sb("causal", [P, 2, P])
        g.pad, g.pads = sb("pad", [1, PADS]), 0
        g.order, g.far, g.hidden = sb("order", [P, 8]), sb("far", [P, 1]), sb("hidden", [P, P], I32)
        g.gates = sb("gates", [P, NB, 4, 1])
        g.mask = load("mask", "mask", [P, P], a["mask_1x1xSxS2_bk0"].rearrange("a b q k -> (a b q) k"), U8)
        g.eps, g.magic, g.onesP = sb("eps", [P, 1]), sb("magic", [P, 1]), sb("onesP", [P, P])

        scope.append(whole.enter_context(ExitStack()))

        def xattn(n):
            what = f"L{n}_xattn"
            w = {k: matrix(what, f"{what}_{k}") for k in ("Wq", "Wk", "Wv", "Wo")}
            w.update({k: column(what, f"{what}_{k}") for k in ("bq", "bk")})
            w.update({k: row(what, f"{what}_{k}") for k in ("bv", "bo")})
            return w

        w0, f0 = xattn(0), {}
        for k in ("gate", "up"):
            f0[k] = sb(f"L0_ffn_{k}", [P, FC0, D])[:, :, :]
            src, full = a[f"L0_ffn_w_{k}"], F0 // P * P
            loading("L0_ffn", f0[k][:, 0:F0 // P, :], src[0:full, :].rearrange("(c p) n -> p c n", p=P))
            loading("L0_ffn", f0[k][0:F0 - full, F0 // P, :], src[full:F0, :])
        f0["down"] = sb("L0_ffn_down", [P, DC, FC0 * P])[:, :, :]
        loading("L0_ffn", f0["down"][:, :, 0:F0], a["L0_ffn_w_down"].rearrange("(c p) n -> p c n", p=P))
        f0.update({k: row("L0_ffn", f"L0_ffn_{k}") for k in ("clip_x", "clip_down")})
        w1 = xattn(1)
        f1 = {k: matrix("L1_ffn", f"L1_ffn_{k}") for k in ("w1", "w2")}
        f1.update({k: row("L1_ffn", f"L1_ffn_{k}") for k in ("b1", "b2")})
        setup(nc, g, a)
        attention(nc, g, "L0a", PLAIN, w0, None, ["L0_xattn"])
        fake_quant_ffn(nc, g, f0)
        turned_attention(nc, g, "L1a", PRUNED, w1, ["L1_xattn"])
        bitlinear_ffn(nc, g, f1)
        scope.pop().close()

        scope.append(whole.enter_context(ExitStack()))
        g.loads = []
        w2 = xattn(2)
        f2 = {k: matrix("L2_ffn", f"L2_ffn_{k}") for k in ("wi", "wo")}
        f2["lora_A"] = load("L2_ffn", "L2_ffn_lora_A", [P, D], a["L2_ffn_lora_A"].rearrange("e r d -> (e r) d"))
        f2["gate_w"] = load("L2_ffn", "L2_ffn_gate_w", [8, D], a["L2_ffn_gate_w"])
        f2["lora_B"] = sb("L2_ffn_lora_B", [P, 8, P])[:, :, :]
        for f in range(8):
            loading("L2_ffn", f2["lora_B"][:, f, :].rearrange("p (e r) -> p e r", e=8),
                    a["L2_ffn_lora_B"][:, f * P:f * P + P, :].rearrange("e p r -> p e r"))
        f2["bi"] = column("L2_ffn", "L2_ffn_bi")
        f2.update({k: row("L2_ffn", f"L2_ffn_{k}") for k in ("bo", "gate_b")})
        a3 = {k: matrix("L3_xattn", f"L3_xattn_{k}") for k in ("q_w", "k_w", "gate_w")}
        a3.update({k: row("L3_xattn", f"L3_xattn_{k}") for k in ("norm_w", "gate_b")})
        E3, bias = 4, 3 * DC * D
        g.mixw = bias + 2 * DC + D
        g.experts = sb("experts", [P, E3, g.mixw])
        for e in range(E3):
            for n, k in enumerate(("Wq", "Wk", "Wv")):
                loading("L3_ffn", g.experts[:, e, n * DC * D:(n + 1) * DC * D].rearrange("p (c n) -> p c n", c=DC),
                        a[f"L3_ffn_{k}"][e].rearrange("(c p) n -> p c n", p=P))
            for n, k in enumerate(("bq", "bk")):
                loading("L3_ffn", g.experts[:, e, bias + n * DC:bias + (n + 1) * DC],
                        a[f"L3_ffn_{k}"][e].rearrange("(c p) -> p c", p=P))
            loading("L3_ffn", g.experts[:, e, bias + 2 * DC:g.mixw], a["L3_ffn_bv"][e].partition_broadcast(P))
        f3 = {k: matrix("L3_ffn", f"L3_ffn_{k}") for k in ("Wo", "Wg1", "Wg2")}
        f3.update({k: row("L3_ffn", f"L3_ffn_{k}") for k in ("bo", "bg2")})
        f3["bg1"] = column("L3_ffn", "L3_ffn_bg1")
        start_loads(nc, g)
        turned_attention(nc, g, "L2a", MASKED, w2, ["L2_xattn"])
        lora_ffn(nc, g, f2)
        gated_attention(nc, g, a3, a["ctx_1024"])
        expert_gates(nc, g, f3)
        attention(nc, g, "L3f", MIXED, f3, None, ["L3_ffn"])
        finish(nc, g, out)


def turned_attention(nc, g, name, kind, w, needs):
    with ExitStack() as ctx:
        t, jobs = dict(w), []
        for k in ("Wq", "Wk", "Wv", "Wo"):
            t[k] = ctx.enter_context(nc.sbuf_tensor(f"{name}_{k}T", [P, DC, D], F32))[:, :, :]
            jobs += [(w[k][:, m, c * P:c * P + P], t[k][:, c, m * P:m * P + P]) for m in range(DC) for c in range(DC)]
        attention(nc, g, name, kind, t, jobs, needs)


_INS = ['x', 'ctx_1024', 'mask_1x1xSxS2_bk0'] + [f'L{n}_xattn_{k}' for n in range(3) for k in (
    'Wq', 'bq', 'Wk', 'bk', 'Wv', 'bv', 'Wo', 'bo')] + [f'L0_ffn_{k}' for k in (
        'clip_x', 'clip_down', 'w_gate', 'w_up', 'w_down')] + [f'L1_ffn_{k}' for k in ('w1', 'b1', 'w2', 'b2')] + [
    f'L2_ffn_{k}' for k in ('wi', 'bi', 'wo', 'bo', 'lora_A', 'lora_B', 'gate_w', 'gate_b')] + [
    f'L3_xattn_{k}' for k in ('q_w', 'k_w', 'norm_w', 'gate_w', 'gate_b')] + [f'L3_ffn_{k}' for k in (
        'Wq', 'bq', 'Wk', 'bk', 'Wv', 'bv', 'Wg1', 'bg1', 'Wg2', 'bg2', 'Wo', 'bo')]


def kernel(**inputs):
    import numpy as np
    import concourse.bacc as bacc
    from concourse.bass_utils import run_bass_kernel_spmd

    nc = bacc.Bacc("TRN2", target_bir_lowering=False, num_devices=1)
    arrays, aps = {}, {}
    for name in _INS:
        x = np.ascontiguousarray(inputs[name])
        arrays[f"in_{name}"] = x
        aps[name] = nc.dram_tensor(f"in_{name}", x.shape, mybir.dt.from_np(x.dtype), kind="ExternalInput").ap()
    out = nc.dram_tensor("out", (NB, P, D), F32, kind="ExternalOutput").ap()
    program(nc, aps, out)
    r = run_bass_kernel_spmd(nc, [arrays], core_ids=[0])
    return r.results[0]["out"]
```

```python
from contextlib import ExitStack

import concourse.bass as bass
from concourse import mybir

F32 = mybir.dt.float32
BF16 = mybir.dt.bfloat16
U8 = mybir.dt.uint8
I32 = mybir.dt.int32
ALU = mybir.AluOpType
ACT = mybir.ActivationFunctionType
AX = mybir.AxisListType

P = 128
NB = 16
D = 256
DC = D // P
NH = 16
DH = D // NH
HC = NH // DC
NQ = 4
HQ = NH // NQ
NS = 2
TURNS = NB // NS
BANK = 512
LN_EPS = 1e-5
BIG = 3.0e38
MAGIC = 1.5 * 2.0 ** 23
HIDDEN = -2.0 ** 100
KEEP = int(P * 0.9)
NDROP = P - KEEP
PADS = 64


class Section:

    def __init__(self, nc, name):
        self.nc, self.name, self.ctx, self.sems = nc, name, ExitStack(), []

    def __enter__(self):
        return self

    def sb(self, name, shape, dt=F32):
        return self.ctx.enter_context(self.nc.sbuf_tensor(f"{self.name}_{name}", shape, dt))

    def ps(self, name, shape, dt=F32):
        return self.ctx.enter_context(self.nc.psum_tensor(f"{self.name}_{name}", shape, dt))

    def sem(self, name):
        s = self.nc.alloc_semaphore(f"{self.name}_{name}")
        self.sems.append(s)
        return s

    def per_stream(self, name):
        return [self.sem(f"{name}{s}") for s in range(NS)]

    def block(self):
        return self.nc.Block()

    def __exit__(self, *exc):
        self.ctx.__exit__(*exc)
        if exc[0] is None and self.sems:
            self.nc.clear_and_free_semaphores(self.sems)
            self.nc.all_engine_barrier()
        return False


def arrived(eng, g, *groups):
    for what in groups:
        eng.wait_ge(g.loaded[what], 16 * g.counts[what])


def apart(dve, g):
    g.pads += 1
    n = g.pads % PADS
    dve.memset(g.pad[0:1, n:n + 1], 0.0)


class Turned:

    def __init__(self, sec, banks, jobs):
        self.banks, self.ps, self.sb = banks, sec.sem("turned_ps"), sec.sem("turned_sb")
        self.lots = [jobs[n:n + 4] for n in range(0, len(jobs), 4)]

    def tensor(self, pe, ident):
        for n, lot in enumerate(self.lots):
            if n >= 2:
                pe.wait_ge(self.sb, n - 1)
            for m, (src, _) in enumerate(lot):
                rows, cols = src.shape[0], src.shape[1]
                mm = pe.transpose(self.banks[n % 2][0:cols, m * P:m * P + rows], src, ident[0:rows, 0:rows])
            mm.then_inc(self.ps, 1)

    def scalar(self, act):
        for n, lot in enumerate(self.lots):
            act.wait_ge(self.ps, n + 1)
            for m, (src, dst) in enumerate(lot):
                rows, cols = src.shape[0], src.shape[1]
                cp = act.copy(dst, self.banks[n % 2][0:cols, m * P:m * P + rows])
            cp.then_inc(self.sb, 1)

    def wait(self, eng):
        eng.wait_ge(self.sb, len(self.lots))


class LayerNorm:

    def __init__(self, sec, g):
        self.g = g
        self.std, self.t1, self.t2 = sec.sb("ln_std", [P, NB]), sec.sb("ln_t1", [P, NB]), sec.sb("ln_t2", [P, NB])
        self.r0, self.rstd = sec.sb("ln_r0", [P, NB]), sec.sb("ln_rstd", [P, NB, 1])
        self.mv = sec.sb("ln_mv", [P, NB, 2])
        self.xn = [sec.sb(f"xn{s}", [P, D]) for s in range(NS)]
        self.s_aggr, self.s_std, self.s_step = sec.sem("ln_aggr"), sec.sem("ln_std"), sec.sem("ln_step")
        self.s_xn = sec.per_stream("xn")

    def vector_start(self, dve):
        for b in range(NB):
            ins = dve.bn_aggr(self.mv[:, b, :], self.g.stats[:, b, :])
        ins.then_inc(self.s_aggr, 1)
        var = self.mv[:, :, 1]
        dve.wait_ge(self.s_std, 1)
        dve.reciprocal(self.r0[:, :], self.std[:, :]).then_inc(self.s_step, 1)
        dve.wait_ge(self.s_step, 1)
        dve.scalar_tensor_tensor(out=self.t1[:, :], in0=var, scalar=LN_EPS, in1=self.r0[:, :], op0=ALU.add,
                                 op1=ALU.mult).then_inc(self.s_step, 1)
        dve.wait_ge(self.s_step, 2)
        dve.scalar_tensor_tensor(out=self.t2[:, :], in0=self.t1[:, :], scalar=-0.5, in1=self.r0[:, :],
                                 op0=ALU.mult, op1=ALU.mult).then_inc(self.s_step, 1)
        dve.wait_ge(self.s_step, 3)
        dve.scalar_tensor_tensor(out=self.rstd[:, :, 0], in0=self.t2[:, :], scalar=1.5, in1=self.r0[:, :],
                                 op0=ALU.add, op1=ALU.mult).then_inc(self.s_step, 1)
        dve.wait_ge(self.s_step, 4)

    def scalar_start(self, act):
        act.wait_ge(self.s_aggr, 1)
        act.activation(self.std[:, :], self.mv[:, :, 1], ACT.Sqrt, bias=self.g.eps[:, 0:1]).then_inc(self.s_std, 1)

    def vector_norm(self, dve, s, b):
        dve.tensor_scalar(self.xn[s][:, :], self.g.x[:, b, :], self.mv[:, b, 0:1], self.rstd[:, b, :],
                          ALU.subtract, ALU.mult).then_inc(self.s_xn[s], 1)

    def vector_apply(self, dve, s, i):
        self.vector_norm(dve, s, NS * (i - 1) + s)

    def vector_stats(self, dve, s, i, s_x):
        dve.wait_ge(s_x[s], i)
        apart(dve, self.g)
        dve.bn_stats(self.g.stats[:, NS * (i - 1) + s, :], tile_of(self.g, i, s))


class Rsqrt:
    STEPS = 12

    def __init__(self, sec, name, width):
        self.v, self.t, self.y = (sec.sb(f"{name}_{n}", [P, width]) for n in ("v", "t", "y"))
        self.u = sec.sb(f"{name}_u", [P, width])
        self.j = sec.sb(f"{name}_j", [P, width], I32)
        self.s = sec.sem(f"{name}_step")

    def vector(self, dve, src, scale, eps, i):
        n = Rsqrt.STEPS * (i - 1)

        def link(k, ins):
            ins.then_inc(self.s, 1)
            dve.wait_ge(self.s, n + k)
        v, t, u, y, j = self.v[:, :], self.t[:, :], self.u[:, :], self.y[:, :], self.j[:, :]
        link(1, dve.tensor_scalar(v, src, scale, eps, ALU.mult, ALU.add))
        link(2, dve.tensor_scalar(j, v.bitcast(I32), 1, None, ALU.arith_shift_right))
        link(3, dve.tensor_scalar(y.bitcast(I32), j, -1.0, float(0x5F3759DF), ALU.mult, ALU.add))
        for k in (4, 7, 10):
            link(k, dve.tensor_tensor(t, v, y, ALU.mult))
            link(k + 1, dve.scalar_tensor_tensor(out=u, in0=t, scalar=-0.5, in1=y, op0=ALU.mult, op1=ALU.mult))
            link(k + 2, dve.scalar_tensor_tensor(out=y, in0=u, scalar=1.5, in1=y, op0=ALU.add, op1=ALU.mult))
        return y


def tile_of(g, i, s):
    return g.x[:, NS * (i - 1) + s, :]


class Pair:

    def __init__(self, first, v):
        self.first, self.v = first, v
        self.pair = bass.ds(first, NS)

    def b(self, s):
        return self.first + s


def sweep_pairs(eng, step):
    pairs = [Pair(NS * n, n + 1) for n in range(TURNS)]
    step(None, None, pairs[0])
    step(None, pairs[0], pairs[1])
    with eng.Fori(1, TURNS - 1) as i:
        step(*(Pair(NS * (i + n), eng.snap(i + n + 1) if n >= 0 else i) for n in (-1, 0, 1)))
    step(pairs[-2], pairs[-1], None)
    step(pairs[-1], None, None)


def banks_of(sec):
    return [[sec.ps(f"bank{s}_{n}", [P, BANK]) for n in range(4)] for s in range(NS)]


class Globals:
    pass


def setup(nc, g, a):
    sec = Section(nc, "setup")
    with sec:
        ctx_nat = sec.sb("ctx_nat", [P, NB, D])
        banks = banks_of(sec)
        s_const, s_zero = sec.sem("const"), sec.sem("zero")
        s_ps, s_sb = sec.sem("ctx_ps"), sec.sem("ctx_sb")
        s_ctx = sec.sem("ctx_in")
        flat = [banks[s][n] for n in range(4) for s in range(NS)]
        with sec.block() as block:
            @block.sync
            def _(sp):
                for q in range(4):
                    sp.dma_start(ctx_nat[:, 4 * q:4 * q + 4, :],
                                 a["ctx_1024"][4 * q:4 * q + 4].rearrange("b p d -> p b d")).then_inc(s_ctx, 16)
                sp.dma_start(g.x[:, :, :], a["x"].rearrange("b p d -> p b d")).then_inc(g.loaded["x"], 16)
                for dst, src, what in g.loads:
                    sp.dma_start(dst, src, allow_slow_non_contiguous=True).then_inc(g.loaded[what], 16)
                sp.wait_ge(g.loaded["x"], 16)

            @block.gpsimd
            def _(pool):
                pool.memset(g.ident[:, :], 0.0).then_inc(s_zero, 1)
                pool.memset(g.hmask[:, :], 1.0).then_inc(s_zero, 1)
                pool.memset(g.causal[:, :, :], 0.0).then_inc(s_zero, 1)
                pool.wait_ge(s_zero, 3)
                pool.affine_select(out=g.ident[:, :], in_=g.ident[:, :], compare_op=ALU.not_equal, fill=1.0,
                                   base=0, pattern=[[-1, P]], channel_multiplier=1).then_inc(s_const, 1)
                pool.affine_select(out=g.hmask[:, :], in_=g.hmask[:, :], compare_op=ALU.is_ge, fill=0.0,
                                   base=0, pattern=[[-DH, HC]], channel_multiplier=1).then_inc(s_zero, 1)
                pool.wait_ge(s_zero, 4)
                pool.affine_select(out=g.hmask[:, :], in_=g.hmask[:, :], compare_op=ALU.is_ge, fill=0.0,
                                   base=DH - 1, pattern=[[DH, HC]], channel_multiplier=-1).then_inc(s_const, 1)
                pool.affine_select(out=g.causal[:, 0, :], in_=g.causal[:, 0, :], compare_op=ALU.is_ge, fill=-BIG,
                                   base=0, pattern=[[-1, P]], channel_multiplier=1).then_inc(s_const, 1)

            @block.vector
            def _(dve):
                dve.memset(g.eps[:, :], LN_EPS).then_inc(s_const, 1)
                dve.memset(g.onesP[:, :], 1.0).then_inc(s_const, 1)
                dve.memset(g.magic[:, :], MAGIC).then_inc(s_const, 1)
                dve.wait_ge(g.loaded["x"], 16)
                for b in range(NB):
                    dve.bn_stats(g.stats[:, b, :], g.x[:, b, :])
                for e in range(8):
                    dve.memset(g.order[:, e:e + 1], 8.0 - e)
                dve.wait_ge(s_const, 6)
                dve.tensor_copy(g.identb[:, :], g.ident[:, :])
                arrived(dve, g, "mask")
                dve.tensor_scalar(g.hidden[:, :], g.mask, 0.0, HIDDEN, ALU.is_equal, ALU.mult)
                for n in range(1, NB, 2):
                    dve.wait_ge(s_ps, n + 1)
                    dve.tensor_copy(g.ctxT[:, n, :, :], flat[n % 8][:, 0:D]
                                    .rearrange("p (c t) -> p c t", c=DC)).then_inc(s_sb, 1)

            @block.scalar
            def _(act):
                for n in range(0, NB, 2):
                    act.wait_ge(s_ps, n + 1)
                    act.copy(g.ctxT[:, n, :, :], flat[n % 8][:, 0:D]
                             .rearrange("p (c t) -> p c t", c=DC)).then_inc(s_sb, 1)

            @block.tensor
            def _(pe):
                pe.wait_ge(s_const, 6)
                for n in range(NB):
                    if n % 4 == 0:
                        pe.wait_ge(s_ctx, 16 * NB // 4)
                    if n == 8:
                        pe.wait_ge(s_sb, 8)
                    for c in range(DC):
                        mm = pe.transpose(flat[n % 8][:, c * P:c * P + P], ctx_nat[:, n, c * P:c * P + P],
                                          g.ident[:, :])
                    mm.then_inc(s_ps, 1)


class Seq:

    def __init__(self, b, s, v, nth, earlier):
        self.b, self.s, self.v, self.nth, self.earlier = b, s, v, nth, earlier


class FixedStep:

    def __init__(self, b):
        self.b = b

    def at(self, k):
        b = self.b + k
        if not 0 <= b < NB:
            return None
        return Seq(b, b % 2, b // 2 + 1, lambda t: NQ * (b // 2) + 1 + t, lambda n: self.at(k - n))


class LoopStep:

    def __init__(self, eng, i, odd, known):
        self.eng, self.i, self.odd, self.known = eng, i, odd, known

    def snap(self, factor, plus):
        if (factor, plus) == (1, 0):
            return self.i
        if (factor, plus) not in self.known:
            self.known[factor, plus] = self.eng.snap(factor * self.i + plus)
        return self.known[factor, plus]

    def at(self, k):
        n = self.odd + k
        half = n // 2
        return Seq(2 * self.i + n, n % 2, self.snap(1, half + 1), lambda t: self.snap(NQ, NQ * half + 1 + t),
                   lambda m: self.at(k - m))


def sweep(eng, step, ahead=2, behind=2):
    for b in range(-ahead, 2):
        step(FixedStep(b))
    with eng.Fori(1, NB // 2 - 1) as i:
        known = {}
        for odd in range(2):
            step(LoopStep(eng, i, odd, known))
    for b in range(NB - 2, NB + behind):
        step(FixedStep(b))


PLAIN, PRUNED, MASKED, MIXED = range(4)


def attention(nc, g, name, kind, w, turned, needs):
    sec = Section(nc, name)
    LAG = 2 if kind == PRUNED else 1
    with sec:
        ln = LayerNorm(sec, g)
        S = [sec.ps(f"scores{n}", [P, BANK]) for n in range(2)]
        T = [sec.ps(f"probsT{n}", [P, BANK]) for n in range(2)]
        F = [sec.ps(f"projected{n}", [P, BANK]) for n in range(2)]
        OB, C = sec.ps("values", [P, BANK]), sec.ps("other", [P, BANK])
        Y = OB if kind == PRUNED else C
        O = OB[:, 0:NH * (DH + 1)].rearrange("p (h e) -> p h e", h=NH)
        two = lambda ps: ps[:, 0:D].rearrange("p (c t) -> p c t", c=DC)
        heads = lambda ap: ap.rearrange("p (h e) -> p h e", h=NH)
        sbs = lambda nm, shape, dt=F32: [sec.sb(f"{nm}{s}", shape, dt) for s in range(2)]
        xT, ctxT, qT, kT = (sbs(n, [P, DC, P]) for n in ("xT", "ctxT", "qT", "kT"))
        v = sbs("v", [P, NH, DH + 1])
        kbd = sbs("kbd", [P, DC, HC, P])
        pr = sec.sb("pr", [P, NQ, HQ, P])
        prT = sbs("prT", [P, NQ, HQ, P])
        mx, rl = sbs("mx", [P, NH]), sbs("rl", [P, NH])
        on, oT = sbs("on", [P, NH, DH]), sbs("oT", [P, DC, P])
        (s_ctx, s_xT_ps, s_xT, s_q_ps, s_k_ps, s_v_ps, s_q, s_k, s_v, s_kbd, s_sc, s_mx, s_sh, s_ex, s_tp,
         s_pt, s_av, s_rl, s_on, s_oT_ps, s_oT, s_y, s_bo, s_x) = (sec.per_stream(n) for n in (
             "ctx_loaded", "xT_ps", "xT", "q_ps", "k_ps", "v_ps", "q", "k", "v", "kbd", "scores", "max",
             "shifted", "exp", "probsT_ps", "probsT", "av", "recip", "out", "outT_ps", "outT", "y",
             "bo_added", "x_done"))
        s_one = sec.sem("ones_set")
        turn_w = Turned(sec, S, turned) if turned else None
        if kind == PRUNED:
            vp = sbs("vp", [P, NH, DH + 1])
            ls, rls = sbs("ls", [P, NH]), sbs("rls", [P, NH])
            cs, keepT = sbs("cs", [P, NH]), sbs("keepT", [P, NH])
            cst, cst2 = sbs("cst", [NH, P]), sbs("cst2", [NH, P])
            m8 = sbs("m8", [NH, 2, 8])
            s_rls, s_cs, s_csT, s_ct, s_m1, s_r1, s_m2, s_fill, s_r2, s_keep, s_kT, s_kTs, s_vp = (
                sec.per_stream(n) for n in ("rowrecip", "colsum", "colsumT_ps", "colsumT",
                                            "least8", "drop8", "least16", "fill", "drop13", "keep", "keepT_ps",
                                            "keepT", "v_pruned"))
            colsum, CT, KT = C[:, 0:NH], F[0][0:NH, D:D + P], OB[:, 0:NH]
            val = vp
        else:
            val = v
        if kind == MIXED:
            mix, mix1 = sbs("mix", [P, g.mixw]), sec.sb("mixed_more", [P, g.mixw])
            s_share, s_more, s_mixed = ([sec.per_stream(f"{nm}{n}_") for n in range(2)] for nm in (
                "share", "share_more", "mixed"))
            lots = (slice(0, g.mixk), slice(g.mixk, g.mixw))

        def weights(s):
            if kind != MIXED:
                return w
            m = mix[s]
            q = {n: m[:, at:at + DC * D].rearrange("p (c n) -> p c n", c=DC) for n, at in g.mixed_at.items()
                 if n[0] == "W"}
            at = g.mixed_at
            q.update(bq=m[:, at["bq"]:at["bq"] + DC], bk=m[:, at["bk"]:at["bk"] + DC], bv=m[:, at["bv"]:at["bv"] + D])
            return q

        kv = xT if kind == MIXED else ctxT
        with sec.block() as block:
            @block.sync
            def _(sp):
                def step(st):
                    new, cur = st.at(2), st.at(0)
                    if new:
                        if cur:
                            sp.wait_ge(s_v_ps[cur.s], cur.v)
                        sp.dma_start(ctxT[new.s][:, :, :], g.ctxT[:, new.b, :, :]).then_inc(s_ctx[new.s], 16)
                if kind != MIXED:
                    sweep(sp, step)

            @block.gpsimd
            def _(pool):
                arrived(pool, g, *needs)
                for s in range(2):
                    pool.memset(v[s][:, :, :], 1.0).then_inc(s_one, 1)
                    if kind == PRUNED:
                        pool.memset(vp[s][:, :, :], 1.0).then_inc(s_one, 1)

                def step(st):
                    nxt, new = st.at(1), st.at(2)
                    if nxt:
                        s = nxt.s
                        pool.wait_ge(s_k[s], nxt.v)
                        for c in range(DC):
                            pool.tensor_tensor(
                                kbd[s][:, c, :, :], kT[s][:, c, :].unsqueeze(1).to_broadcast([P, HC, P]),
                                g.hmask[:, :].unsqueeze(2).to_broadcast([P, HC, P]), ALU.mult).then_inc(s_kbd[s], 1)
                    if new and kind == MIXED:
                        for n in range(2):
                            pool.wait_ge(s_more[n][new.s], new.v)
                        for n, lot in enumerate(lots):
                            pool.tensor_tensor(mix[new.s][:, lot], mix[new.s][:, lot], mix1[:, lot], ALU.add
                                               ).then_inc(s_mixed[n][new.s], 1)
                    if nxt:
                        pool.wait_ge(ln.s_xn[s], nxt.v)
                        pool.tensor_tensor(g.x[:, nxt.b, :], g.x[:, nxt.b, :], w["bo"], ALU.add
                                           ).then_inc(s_bo[s], 1)
                sweep(pool, step)

            @block.tensor
            def _(pe):
                arrived(pe, g, *needs)
                if turn_w:
                    turn_w.tensor(pe, g.ident)
                    turn_w.wait(pe)
                pe.wait_ge(s_one, 4 if kind == PRUNED else 2)

                def turn_x(q):
                    pe.wait_ge(ln.s_xn[q.s], q.v)
                    before = q.earlier(1)
                    if before:
                        pe.wait_ge(s_q[before.s], before.v)
                    for c in range(DC):
                        mm = pe.transpose(F[0][:, c * P:c * P + P], ln.xn[q.s][:, c * P:c * P + P], g.ident[:, :])
                    mm.then_inc(s_xT_ps[q.s], 1)

                def project(out, W, inp):
                    for m in range(DC):
                        for c in range(DC):
                            mm = pe.matmul(out[:, m * P:m * P + P], W[:, c, m * P:m * P + P], inp[:, c, :],
                                           start=(c == 0), stop=(c == DC - 1))
                    return mm

                def project_k(q):
                    before = q.earlier(1)
                    if before:
                        pe.wait_ge(s_v[before.s], before.v)
                    if kind == MIXED:
                        pe.wait_ge(s_mixed[0][q.s], q.v)
                        pe.wait_ge(s_xT[q.s], q.v)
                    else:
                        pe.wait_ge(s_ctx[q.s], 16 * q.v)
                    project(F[1], weights(q.s)["Wk"], kv[q.s]).then_inc(s_k_ps[q.s], 1)

                def project_q(q):
                    pe.wait_ge(s_xT[q.s], q.v)
                    if kind == MIXED:
                        pe.wait_ge(s_mixed[1][q.s], q.v)
                    project(F[0], weights(q.s)["Wq"], xT[q.s]).then_inc(s_q_ps[q.s], 1)

                def project_v(q):
                    pe.wait_ge(s_k[q.s], q.v)
                    for c in range(DC):
                        mm = pe.matmul(F[1][:, 0:D], kv[q.s][:, c, :], weights(q.s)["Wv"][:, c, :],
                                       start=(c == 0), stop=(c == DC - 1))
                    mm.then_inc(s_v_ps[q.s], 1)

                def scores(q, t):
                    c, h = t * HQ // HC, t * HQ % HC
                    if t == 0:
                        pe.wait_ge(s_q[q.s], q.v)
                    if h == 0:
                        pe.wait_ge(s_kbd[q.s], DC * q.v - DC + 1 + c)
                    last = q if t >= 2 else q.earlier(1)
                    if last:
                        pe.wait_ge(s_sh[last.s], last.nth((t - 2) % NQ))
                    mm = pe.matmul(S[t % 2][:, :], qT[q.s][:, c, :], kbd[q.s][:, c, h:h + HQ, :], start=True,
                                   stop=(kind != MASKED))
                    if kind == MASKED:
                        mm = pe.matmul(S[t % 2][:, :], g.identb[:, :],
                                       g.hidden[:, :].unsqueeze(1).to_broadcast([P, HQ, P]), start=False, stop=True)
                    mm.then_inc(s_sc[q.s], 1)

                def turn_probs(q, t):
                    before = q.earlier(1)
                    pe.wait_ge(s_ex[q.s], q.nth(t))
                    if kind == PRUNED:
                        pe.wait_ge(s_rls[q.s], q.nth(t))
                        if t == 0 and before:
                            pe.wait_ge(s_cs[before.s], before.v)
                        for h in range(HQ):
                            n = t * HQ + h
                            pe.matmul(colsum[:, n:n + 1], pr[:, t, h, :], rls[q.s][:, n:n + 1], start=True, stop=True)
                    last = q if t >= 2 else before
                    if last:
                        pe.wait_ge(s_pt[last.s], last.nth((t - 2) % NQ))
                    for h in range(HQ):
                        mm = pe.transpose(T[t % 2][:, h * P:h * P + P], pr[:, t, h, :], g.ident[:, :])
                    mm.then_inc(s_tp[q.s], 1)

                def values(q, t):
                    before = q.earlier(1)
                    pe.wait_ge(s_pt[q.s], q.nth(t))
                    if t == 0:
                        if kind == PRUNED:
                            pe.wait_ge(s_vp[q.s], q.v)
                        else:
                            pe.wait_ge(s_v[q.s], q.v)
                        if before:
                            done = s_x if kind == PRUNED else s_on
                            pe.wait_ge(done[before.s], before.v)
                    for h in range(t * HQ, t * HQ + HQ):
                        mm = pe.matmul(O[:, h, :], prT[q.s][:, t, h % HQ, :], val[q.s][:, h, :], start=True,
                                       stop=True)
                    if t == NQ - 1:
                        mm.then_inc(s_av[q.s], 1)

                def turn_out(q):
                    pe.wait_ge(s_on[q.s], q.v)
                    before = q.earlier(1)
                    if before:
                        pe.wait_ge(s_x[before.s], before.v)
                    for c in range(DC):
                        mm = pe.transpose(Y[:, c * P:c * P + P],
                                          on[q.s][:, c * HC:(c + 1) * HC, :].rearrange("p h e -> p (h e)"),
                                          g.ident[:, :])
                    mm.then_inc(s_oT_ps[q.s], 1)

                def project_out(q):
                    pe.wait_ge(s_oT[q.s], q.v)
                    for c in range(DC):
                        mm = pe.matmul(Y[:, D:2 * D], oT[q.s][:, c, :], w["Wo"][:, c, :], start=(c == 0),
                                       stop=(c == DC - 1))
                    mm.then_inc(s_y[q.s], 1)

                def step(st):
                    cur, prev, nxt, new, last = st.at(0), st.at(-1), st.at(1), st.at(2), st.at(-LAG)
                    for t in range(NQ):
                        if cur:
                            scores(cur, t)
                        if kind == PRUNED:
                            if last and t < 2:
                                values(last, 2 * t)
                                values(last, 2 * t + 1)
                        elif t < 2:
                            if prev:
                                values(prev, t + 2)
                        elif cur:
                            values(cur, t - 2)
                        if t == 0 and nxt:
                            project_k(nxt)
                        if t == 1:
                            if nxt:
                                project_q(nxt)
                            if kind == PRUNED and prev:
                                pe.wait_ge(s_cs[prev.s], prev.v)
                                pe.transpose(CT, cs[prev.s][:, :], g.ident[:, :]).then_inc(s_csT[prev.s], 1)
                        if t == 2:
                            if last:
                                turn_out(last)
                            if nxt:
                                project_v(nxt)
                        if t == 3:
                            if new:
                                turn_x(new)
                            if last:
                                project_out(last)
                            if kind == PRUNED and prev:
                                pe.wait_ge(s_keep[prev.s], prev.v)
                                pe.matmul(KT, cst2[prev.s][:, :], g.ident[0:NH, 0:NH], start=True,
                                          stop=True).then_inc(s_kT[prev.s], 1)
                        if t == 0 and prev:
                            turn_probs(prev, NQ - 1)
                        if t > 0 and cur:
                            turn_probs(cur, t - 1)
                sweep(pe, step)

            @block.scalar
            def _(act):
                if turn_w:
                    turn_w.scalar(act)
                ln.scalar_start(act)

                def copy_probs(q, t):
                    act.wait_ge(s_tp[q.s], q.nth(t))
                    act.copy(prT[q.s][:, t, :, :], T[t % 2][:, :].rearrange("p (h k) -> p h k", h=HQ)
                             ).then_inc(s_pt[q.s], 1)

                def step(st):
                    cur, prev, nxt, new, last = st.at(0), st.at(-1), st.at(1), st.at(2), st.at(-LAG)
                    for t in range(NQ):
                        if t == 2 and last:
                            act.wait_ge(s_oT_ps[last.s], last.v)
                            act.copy(oT[last.s][:, :, :], two(Y)).then_inc(s_oT[last.s], 1)
                        if t == 3 and new:
                            act.wait_ge(s_xT_ps[new.s], new.v)
                            act.copy(xT[new.s][:, :, :], two(F[0])).then_inc(s_xT[new.s], 1)
                        if cur:
                            act.wait_ge(s_sh[cur.s], cur.nth(t))
                            if kind == PRUNED:
                                for h in range(HQ):
                                    n = t * HQ + h
                                    ex = act.activation(pr[:, t, h, :], pr[:, t, h, :], ACT.Exp, scale=DH ** -0.5,
                                                        accum_out=ls[cur.s][:, n:n + 1])
                            else:
                                ex = act.activation(pr[:, t, :, :], pr[:, t, :, :], ACT.Exp, scale=DH ** -0.5)
                            ex.then_inc(s_ex[cur.s], 1)
                        if t == 0 and prev:
                            copy_probs(prev, NQ - 1)
                        if t > 0 and cur:
                            copy_probs(cur, t - 1)
                        if kind == MIXED and new and t < 2:
                            if t == 0 and cur:
                                act.wait_ge(s_v[cur.s], cur.v)
                            if t == 1 and nxt:
                                act.wait_ge(s_mixed[1][nxt.s], nxt.v)
                            act.activation((mix[new.s], mix1)[t][:, :], g.experts[:, t, :], ACT.Copy,
                                           scale=g.gates[:, new.b, t, :]).then_inc(s_share[t][new.s], 1)
                sweep(act, step)

            @block.vector
            def _(dve):
                arrived(dve, g, *needs)
                dve.wait_ge(s_one, 4 if kind == PRUNED else 2)
                ln.vector_start(dve)

                def soft(q, t, last_group):
                    s, before = q.s, q.earlier(1)
                    sc = S[t % 2][:, :].rearrange("p (h k) -> p h k", h=HQ)
                    m4 = mx[s][:, t * HQ:t * HQ + HQ]
                    dve.wait_ge(s_sc[s], q.nth(t))
                    dve.tensor_reduce(m4, sc, AX.X, ALU.max).then_inc(s_mx[s], 1)
                    if kind == PRUNED and last_group[0]:
                        row_factors(*last_group)
                    if before:
                        dve.wait_ge(s_tp[before.s], before.nth(t))
                    dve.wait_ge(s_mx[s], q.nth(t))
                    dve.tensor_tensor(pr[:, t, :, :], sc, m4.unsqueeze(2).to_broadcast([P, HQ, P]),
                                      ALU.subtract).then_inc(s_sh[s], 1)

                def row_factors(q, t):
                    s, l4 = q.s, slice(t * HQ, t * HQ + HQ)
                    dve.wait_ge(s_ex[s], q.nth(t))
                    dve.reciprocal(rls[s][:, l4], ls[s][:, l4]).then_inc(s_rls[s], 1)

                def add_k(q):
                    dve.wait_ge(s_k_ps[q.s], q.v)
                    dve.tensor_tensor(kT[q.s][:, :, :], two(F[1]),
                                      weights(q.s)["bk"].unsqueeze(2).to_broadcast([P, DC, P]), ALU.add
                                      ).then_inc(s_k[q.s], 1)

                def add_q(q):
                    dve.wait_ge(s_q_ps[q.s], q.v)
                    dve.tensor_tensor(qT[q.s][:, :, :], two(F[0]),
                                      weights(q.s)["bq"].unsqueeze(2).to_broadcast([P, DC, P]), ALU.add
                                      ).then_inc(s_q[q.s], 1)

                def add_v(q):
                    dve.wait_ge(s_v_ps[q.s], q.v)
                    dve.tensor_tensor(v[q.s][:, :, 0:DH], heads(F[1][:, 0:D]), heads(weights(q.s)["bv"]), ALU.add
                                      ).then_inc(s_v[q.s], 1)

                def drop_keys(q):
                    s = q.s
                    apart(dve, g)
                    dve.max(m8[s][:, 0, :], cst[s][:, :]).then_inc(s_m1[s], 1)
                    dve.wait_ge(s_m1[s], q.v)
                    apart(dve, g)
                    dve.match_replace(cst2[s][:, :], m8[s][:, 0, :], cst[s][:, :], -BIG).then_inc(s_r1[s], 1)
                    dve.wait_ge(s_r1[s], q.v)
                    apart(dve, g)
                    dve.max(m8[s][:, 1, :], cst2[s][:, :]).then_inc(s_m2[s], 1)
                    dve.wait_ge(s_m2[s], q.v)
                    apart(dve, g)
                    dve.tensor_scalar(m8[s][:, 1, NDROP - 8:8], m8[s][:, 1, NDROP - 8:8], 0.0, -BIG,
                                      ALU.mult, ALU.add).then_inc(s_fill[s], 1)
                    dve.wait_ge(s_fill[s], q.v)
                    apart(dve, g)
                    dve.match_replace(cst[s][:, :], m8[s][:, 1, :], cst2[s][:, :], -BIG).then_inc(s_r2[s], 1)
                    dve.wait_ge(s_r2[s], q.v)
                    dve.tensor_scalar(cst2[s][:, ::-1], cst[s][:, :], -0.5 * BIG, None, ALU.is_gt
                                      ).then_inc(s_keep[s], 1)

                def norm_out(q):
                    s = q.s
                    dve.wait_ge(s_av[s], q.v)
                    dve.reciprocal(rl[s][:, :], O[:, :, DH]).then_inc(s_rl[s], 1)
                    dve.wait_ge(s_rl[s], q.v)
                    dve.tensor_tensor(on[s][:, :, :], O[:, :, 0:DH], rl[s][:, :].unsqueeze(2).to_broadcast([P, NH, DH]),
                                      ALU.mult).then_inc(s_on[s], 1)

                def step(st):
                    cur, prev, nxt, new, last = st.at(0), st.at(-1), st.at(1), st.at(2), st.at(-LAG)
                    for t in range(NQ):
                        if t == 1:
                            if kind == PRUNED and prev:
                                dve.wait_ge(s_tp[prev.s], prev.nth(NQ - 1))
                                dve.tensor_copy(cs[prev.s][:, :], colsum).then_inc(s_cs[prev.s], 1)
                            if nxt:
                                add_k(nxt)
                        if t == 2:
                            if kind == PRUNED and prev:
                                dve.wait_ge(s_csT[prev.s], prev.v)
                                dve.tensor_scalar(cst[prev.s][:, ::-1], CT, -1.0, None, ALU.mult
                                                  ).then_inc(s_ct[prev.s], 1)
                            if nxt:
                                add_q(nxt)
                        before = (cur, t - 1) if t > 0 else (prev, NQ - 1)
                        if cur:
                            soft(cur, t, before)
                        elif kind == PRUNED and before[0]:
                            row_factors(*before)
                        if t == 1 and last:
                            norm_out(last)
                        if kind == MIXED and new and 1 <= t <= 2:
                            to = (mix[new.s], mix1)[t - 1][:, :]
                            dve.wait_ge(s_share[t - 1][new.s], new.v)
                            dve.scalar_tensor_tensor(
                                out=to, in0=g.experts[:, t + 1, :], scalar=g.gates[:, new.b, t + 1, :], in1=to,
                                op0=ALU.mult, op1=ALU.add).then_inc(s_more[t - 1][new.s], 1)
                        if t == 2:
                            if kind == PRUNED and prev:
                                dve.wait_ge(s_ct[prev.s], prev.v)
                                drop_keys(prev)
                            if new:
                                ln.vector_norm(dve, new.s, new.b)
                    if kind == PRUNED and prev:
                        s = prev.s
                        dve.wait_ge(s_kT[s], prev.v)
                        dve.tensor_copy(keepT[s][:, :], KT).then_inc(s_kTs[s], 1)
                        dve.wait_ge(s_kTs[s], prev.v)
                        dve.tensor_tensor(vp[s][:, :, 0:DH], v[s][:, :, 0:DH],
                                          keepT[s][:, :].unsqueeze(2).to_broadcast([P, NH, DH]), ALU.mult
                                          ).then_inc(s_vp[s], 1)
                        dve.wait_ge(s_vp[s], prev.v)
                    if nxt:
                        add_v(nxt)
                    if last:
                        s = last.s
                        dve.wait_ge(s_y[s], last.v)
                        dve.wait_ge(s_bo[s], last.v)
                        dve.tensor_tensor(g.x[:, last.b, :], Y[:, D:2 * D], g.x[:, last.b, :], ALU.add
                                          ).then_inc(s_x[s], 1)
                        dve.wait_ge(s_x[s], last.v)
                        apart(dve, g)
                        dve.bn_stats(g.stats[:, last.b, :], g.x[:, last.b, :])
                sweep(dve, step)


QMAX = 127.0
F0 = 704
FC0 = -(-F0 // P)
TG = 4
NG = NB // TG


def rounded(eng, out, tmp, src, scalar, sem, n, clip=None):
    lo, hi = clip or (-128.0, 127.0)
    eng.tensor_scalar(tmp, src, scalar, MAGIC, ALU.mult, ALU.add).then_inc(sem, 1)
    eng.wait_ge(sem, n + 1)
    eng.tensor_scalar(tmp, tmp, MAGIC + hi, MAGIC + lo, ALU.min, ALU.max).then_inc(sem, 1)
    eng.wait_ge(sem, n + 2)
    eng.tensor_scalar(out, tmp, MAGIC, None, ALU.subtract).then_inc(sem, 1)
    eng.wait_ge(sem, n + 3)


class GlobalMax:

    def __init__(self, sec, name, bank):
        self.ps, self.one = bank, sec.sb(f"{name}_one", [1, 1])
        self.s_row, self.s_one, self.s_all = sec.sem(f"{name}_row"), sec.sem(f"{name}_one"), sec.sem(f"{name}_all")

    def tensor(self, pe, g, col, s_col, n):
        pe.wait_ge(s_col, n)
        pe.transpose(self.ps[0:1, 0:P], col, g.ident[:, :]).then_inc(self.s_row, 1)
        pe.wait_ge(self.s_one, 1)
        pe.matmul(self.ps[:, P:P + 1], g.onesP[0:1, :], self.one[:, :], start=True, stop=True
                  ).then_inc(self.s_all, 1)

    def vector(self, dve):
        dve.wait_ge(self.s_row, 1)
        dve.tensor_reduce(self.one[:, :], self.ps[0:1, 0:P], AX.X, ALU.max).then_inc(self.s_one, 1)
        dve.wait_ge(self.s_all, 1)
        return self.ps[:, P:P + 1]


def fake_quant_ffn(nc, g, w):
    sec = Section(nc, "L0f")
    with sec:
        ln = LayerNorm(sec, g)
        banks = [sec.ps(f"bank{n}", [P, BANK]) for n in range(8)]
        act_scale = sec.sb("act_scale", [P, 8])
        sg, su, iw = (sec.sb(n, [P, FC0]) for n in ("gate_scale", "up_scale", "inv_w"))
        sd, sd_row = sec.sb("down_scale", [P, DC]), sec.sb("down_row", [P, D])
        xqT = sec.sb("xqT", [P, DC, NB * P], BF16)
        wT = {n: sec.sb(f"{n}T", [P, DC, FC0 * P], BF16) for n in ("gate", "up")}
        wdT = sec.sb("downT", [P, FC0, D], BF16)
        amax, hmax = sec.sb("amax", [P, NB, 1]), sec.sb("hmax", [P, NG * FC0])
        gm1, gm2 = GlobalMax(sec, "xmax", banks[7]), GlobalMax(sec, "hmax", banks[7])
        s_sc, s_w, s_w2, s_amax, s_col, s_q, s_xq = (sec.sem(n) for n in (
            "scales", "w_steps", "w_rounded", "tile_amax", "amax_col", "q_steps", "xq_ready"))
        s_dr, s_t_ps, s_t_sb, s_row_ps = sec.sem("x_steps"), sec.sem("turned_ps"), sec.sem("turned_sb"), sec.sem("row_ps")
        half_col = sec.sb("amax_cols", [P, 2])
        s_idb = sec.sem("identb")
        with ExitStack() as early:
            xn_all = early.enter_context(nc.sbuf_tensor("L0f_xn_all", [P, NB, D], F32))
            xq = early.enter_context(nc.sbuf_tensor("L0f_xq", [P, NB, D], BF16))
            wq = {n: early.enter_context(nc.sbuf_tensor(f"L0f_{n}q", [P, FC0, D], BF16)) for n in ("gate", "up")}
            wdq = early.enter_context(nc.sbuf_tensor("L0f_downq", [P, DC, FC0 * P], BF16))
            wtmp = early.enter_context(nc.sbuf_tensor("L0f_wtmp", [P, FC0, D], F32))
            identb = early.enter_context(nc.sbuf_tensor("L0f_identb", [P, P], BF16))
            blocks = [(wq[n][:, f, c * P:c * P + P], wT[n][:, c, f * P:f * P + P])
                      for n in ("gate", "up") for f in range(FC0) for c in range(DC)]
            blocks += [(wdq[:, c, f * P:f * P + P], wdT[:, f, c * P:c * P + P]) for f in range(FC0) for c in range(DC)]
            with sec.block() as block:
                @block.tensor
                def _(pe):
                    pe.wait_ge(s_idb, 1)
                    pe.wait_ge(s_w2, 3)
                    for n in range(0, len(blocks), 4):
                        k = n // 4
                        if k >= 6:
                            pe.wait_ge(s_t_sb, k - 5)
                        for m, (src, _) in enumerate(blocks[n:n + 4]):
                            mm = pe.transpose(banks[k % 6][:, :].bitcast(BF16)[:, m * P:m * P + P], src, identb[:, :])
                        mm.then_inc(s_t_ps, 1)
                    for c in range(DC):
                        mm = pe.matmul(banks[6][:, c * P:c * P + P], sd[:, c:c + 1].to_broadcast([P, P]),
                                       g.ident[:, :], start=True, stop=True)
                    mm.then_inc(s_row_ps, 1)
                    gm1.tensor(pe, g, half_col[:, 0:1], s_col, 1)
                    nw = len(blocks) // 4
                    for t in range(NB // 2):
                        k = nw + t
                        pe.wait_ge(s_xq, t // 2 + 1)
                        pe.wait_ge(s_t_sb, k - 5)
                        for m in range(4):
                            b, c = 2 * t + m // 2, m % 2
                            mm = pe.transpose(banks[k % 6][:, :].bitcast(BF16)[:, m * P:m * P + P],
                                              xq[:, b, c * P:c * P + P], identb[:, :])
                        mm.then_inc(s_t_ps, 1)

                @block.scalar
                def _(act):
                    arrived(act, g, "L0_ffn")
                    act.copy(identb[:, :], g.ident[:, :]).then_inc(s_idb, 1)
                    ln.scalar_start(act)
                    act.activation(act_scale[:, 0:1], w["clip_x"], ACT.Exp, scale=-1.0).then_inc(s_sc, 1)
                    act.activation(act_scale[:, 1:2], w["clip_down"], ACT.Exp, scale=-1.0).then_inc(s_sc, 1)
                    for k in range(len(blocks) // 4):
                        act.wait_ge(s_t_ps, k + 1)
                        for m in range(4):
                            dst = blocks[4 * k + m][1]
                            cp = act.copy(dst, banks[k % 6][:, :].bitcast(BF16)[:, m * P:m * P + P])
                        cp.then_inc(s_t_sb, 1)
                    for t in range(NB // 2):
                        k = len(blocks) // 4 + t
                        act.wait_ge(s_t_ps, k + 1)
                        act.copy(xqT[:, :, 2 * t * P:(2 * t + 2) * P].rearrange("p c (b n) -> p b c n", b=2),
                                 banks[k % 6][:, :].bitcast(BF16)[:, 0:4 * P].rearrange("p (b c n) -> p b c n", b=2, c=2)
                                 ).then_inc(s_t_sb, 1)

                @block.vector
                def _(dve):
                    arrived(dve, g, "L0_ffn")
                    n = 0
                    dve.memset(w["gate"][F0 % P:P, FC0 - 1, :], 0.0)
                    dve.memset(w["up"][F0 % P:P, FC0 - 1, :], 0.0)
                    dve.memset(w["down"][:, :, F0:FC0 * P], 0.0).then_inc(s_w, 1)
                    n += 1
                    dve.wait_ge(s_w, n)

                    def scales(src, out):
                        k = src.shape[1]
                        dve.tensor_reduce(iw[:, 0:k], src, AX.X, ALU.max, apply_absolute_value=True).then_inc(s_w, 1)
                        dve.wait_ge(s_w, n + 1)
                        dve.tensor_scalar(out, iw[:, 0:k], 1.0 / QMAX, 1e-37, ALU.mult, ALU.max).then_inc(s_w, 1)
                        dve.wait_ge(s_w, n + 2)
                        dve.reciprocal(iw[:, 0:k], out).then_inc(s_w, 1)
                        dve.wait_ge(s_w, n + 3)

                    for src, out, q in (("gate", sg, wq["gate"]), ("up", su, wq["up"]), ("down", sd, wdq)):
                        k = w[src].shape[1]
                        tmp = wtmp[:, :, :] if src != "down" else wtmp[:, :, :].rearrange("p f n -> p (f n)")[
                            :, 0:DC * FC0 * P].rearrange("p (c n) -> p c n", c=DC)
                        scales(w[src], out[:, :])
                        n += 3
                        dve.tensor_tensor(tmp, w[src], iw[:, 0:k].unsqueeze(2).to_broadcast(list(w[src].shape)),
                                          ALU.mult).then_inc(s_w, 1)
                        dve.wait_ge(s_w, n + 1)
                        dve.tensor_scalar(tmp, tmp, MAGIC, None, ALU.add).then_inc(s_w, 1)
                        dve.wait_ge(s_w, n + 2)
                        dve.tensor_scalar(q[:, :, :], tmp, MAGIC, None, ALU.subtract).then_inc(s_w2, 1)
                        n += 2
                        dve.wait_ge(s_w2, {"gate": 1, "up": 2, "down": 3}[src])
                    ln.vector_start(dve)
                    with dve.Fori(1, NB + 1) as i:
                        dve.tensor_scalar(xn_all[:, i - 1, :], g.x[:, i - 1, :], ln.mv[:, i - 1, 0:1],
                                          ln.rstd[:, i - 1, :], ALU.subtract, ALU.mult).then_inc(ln.s_xn[0], 1)
                        dve.wait_ge(ln.s_xn[0], i)
                        dve.tensor_reduce(amax[:, i - 1, :], xn_all[:, i - 1, :], AX.X, ALU.max, apply_absolute_value=True).then_inc(s_amax, 1)
                    dve.wait_ge(s_amax, NB)
                    dve.tensor_reduce(half_col[:, 0:1], amax[:, :, 0], AX.X, ALU.max).then_inc(s_col, 1)
                    dve.wait_ge(s_sc, 2)
                    dve.tensor_scalar(act_scale[:, 2:4], act_scale[:, 0:2], 1.0, QMAX, ALU.add, ALU.mult).then_inc(s_sc, 1)
                    dve.wait_ge(s_sc, 3)
                    dve.reciprocal(act_scale[:, 2:4], act_scale[:, 2:4]).then_inc(s_sc, 1)
                    dve.wait_ge(s_row_ps, 1)
                    dve.tensor_copy(sd_row[:, :], banks[6][:, 0:D]).then_inc(s_sc, 1)
                    top = gm1.vector(dve)
                    dve.wait_ge(s_sc, 5)
                    dve.tensor_tensor(act_scale[:, 4:5], top, act_scale[:, 2:3], ALU.mult).then_inc(s_sc, 1)
                    dve.wait_ge(s_sc, 6)
                    dve.reciprocal(act_scale[:, 5:6], act_scale[:, 4:5]).then_inc(s_sc, 1)
                    dve.tensor_scalar(sg[:, :], sg[:, :], act_scale[:, 4:5], None, ALU.mult)
                    dve.tensor_scalar(su[:, :], su[:, :], act_scale[:, 4:5], None, ALU.mult)
                    dve.wait_ge(s_sc, 7)
                    for q in range(4):
                        part = xn_all[:, 4 * q:4 * q + 4, :]
                        rounded(dve, xq[:, 4 * q:4 * q + 4, :], part, part, act_scale[:, 5:6], s_dr, 3 * q)
                        dve.memset(g.pad[0:1, q:q + 1], 0.0).then_inc(s_xq, 1)

        h = sec.sb("h", [P, FC0, NB * P])
        ga = sec.sb("silu_gate", [P, 3, BANK])
        s_gu_ps, s_silu, s_h, s_free, s_mx = (sec.sem(n) for n in ("gate_up_ps", "silu", "h", "banks_free", "h_amax"))
        with sec.block() as block:
            @block.tensor
            def _(pe):
                with pe.Fori(1, NG + 1) as i:
                    for f in range(FC0):
                        k = f % 3
                        pe.wait_ge(s_free, FC0 * i - FC0 + f + 1)
                        for m, n in enumerate(("gate", "up")):
                            for c in range(DC):
                                mm = pe.matmul(banks[2 * k + m][:, :], wT[n][:, c, f * P:f * P + P],
                                               xqT[:, c, bass.ts(i - 1, BANK)], start=(c == 0), stop=(c == DC - 1))
                        mm.then_inc(s_gu_ps, 1)
                gm2.tensor(pe, g, half_col[:, 1:2], s_col, 2)

            @block.scalar
            def _(act):
                with act.Fori(1, NG + 1) as i:
                    for f in range(FC0):
                        act.wait_ge(s_free, FC0 * i - FC0 + f + 1)
                        act.wait_ge(s_gu_ps, FC0 * i - FC0 + f + 1)
                        act.activation(ga[:, f % 3, :], banks[2 * (f % 3)][:, :], ACT.Silu,
                                       scale=sg[:, f:f + 1]).then_inc(s_silu, 1)

            @block.vector
            def _(dve):
                dve.memset(g.pad[0:1, 0:1], 0.0).then_inc(s_free, 3)
                with dve.Fori(1, NG + 1) as i:
                    for f in range(FC0):
                        dve.wait_ge(s_silu, FC0 * i - FC0 + f + 1)
                        dve.scalar_tensor_tensor(out=h[:, f, bass.ts(i - 1, BANK)], in0=banks[2 * (f % 3) + 1][:, :],
                                                 scalar=su[:, f:f + 1], in1=ga[:, f % 3, :], op0=ALU.mult,
                                                 op1=ALU.mult).then_inc(s_free, 1)
                dve.wait_ge(s_free, NG * FC0 + 3)
                for f in range(FC0):
                    dve.tensor_reduce(hmax[:, f:f + 1], h[:, f, :], AX.X, ALU.max, apply_absolute_value=True).then_inc(s_mx, 1)
                dve.wait_ge(s_mx, FC0)
                dve.tensor_reduce(half_col[:, 1:2], hmax[:, 0:FC0], AX.X, ALU.max).then_inc(s_col, 1)
                top = gm2.vector(dve)
                dve.tensor_tensor(act_scale[:, 6:7], top, act_scale[:, 3:4], ALU.mult).then_inc(s_sc, 1)
                dve.wait_ge(s_sc, 8)
                dve.reciprocal(act_scale[:, 7:8], act_scale[:, 6:7])
                dve.tensor_scalar(sd_row[:, :], sd_row[:, :], act_scale[:, 6:7], None, ALU.mult)

        hq = sec.sb("hq", [P, 2, FC0, P], BF16)
        yt = sec.sb("yt", [P, 2, D])
        s_hr, s_hc, s_hq, s_y, s_yt, s_x = (sec.sem(n) for n in ("h_scaled", "h_clipped", "hq", "y", "y_scaled", "x_done"))
        with sec.block() as block:
            @block.scalar
            def _(act):
                with act.Fori(1, NB + 1) as i:
                    hb = h[:, :, bass.ts(i - 1, P)]
                    act.activation(hb, hb, ACT.Identity, bias=g.magic[:, 0:1], scale=act_scale[:, 7:8]).then_inc(s_hr, 1)

            @block.vector
            def _(dve):
                with dve.Fori(1, NB // 2 + 1) as i:
                    for s in range(2):
                        b = 2 * i - 2 + s
                        hb = h[:, :, bass.ts(b, P)]
                        dve.wait_ge(s_hr, 2 * i - 1 + s)
                        dve.tensor_scalar(hb, hb, MAGIC + QMAX, MAGIC - QMAX - 1.0, ALU.min, ALU.max).then_inc(s_hc, 1)
                        dve.wait_ge(s_hc, 2 * i - 1 + s)
                        dve.tensor_scalar(hq[:, s, :, :], hb, MAGIC, None, ALU.subtract).then_inc(s_hq, 1)
                    for s in range(2):
                        b = 2 * i - 2 + s
                        dve.wait_ge(s_y, 2 * i - 1 + s)
                        dve.tensor_tensor(yt[:, s, :], banks[s][:, 0:D], sd_row[:, :], ALU.mult).then_inc(s_yt, 1)
                        dve.wait_ge(s_yt, 2 * i - 1 + s)
                        dve.tensor_tensor(g.x[:, b, :], yt[:, s, :], g.x[:, b, :], ALU.add).then_inc(s_x, 1)
                    dve.wait_ge(s_x, 2 * i)
                    apart(dve, g)
                    for s in range(2):
                        dve.bn_stats(g.stats[:, 2 * i - 2 + s, :], g.x[:, 2 * i - 2 + s, :])

            @block.tensor
            def _(pe):
                with pe.Fori(1, NB // 2 + 1) as i:
                    for s in range(2):
                        pe.wait_ge(s_hq, 2 * i - 1 + s)
                        for f in range(FC0):
                            mm = pe.matmul(banks[s][:, 0:D], hq[:, s, f, :], wdT[:, f, :], start=(f == 0),
                                           stop=(f == FC0 - 1))
                        mm.then_inc(s_y, 1)


def bitlinear_ffn(nc, g, w):
    sec = Section(nc, "L1f")
    F = 1024
    FC = F // P
    with sec:
        ln = LayerNorm(sec, g)
        H, T2 = ([[sec.ps(f"{n}{s}_{m}", [P, BANK]) for m in range(2)] for s in range(NS)] for n in (
            "hidden", "h_turned"))
        XT = [H[s][0][:, 0:D] for s in range(NS)]
        sbs = lambda nm, shape, dt=F32: [sec.sb(f"{nm}{s}", shape, dt) for s in range(NS)]
        w1T, w2T = sec.sb("w1T", [P, DC, F], BF16), sec.sb("w2T", [P, FC, D], BF16)
        xs, xqT = sbs("xs", [P, D]), sbs("xqT", [P, DC, P], BF16)
        hh, hs = sbs("h", [P, F]), sbs("hs", [P, F])
        hqT = sbs("hqT", [P, FC, P], BF16)
        hp, junk, deq_old = sbs("hp", [P, F]), sbs("junk", [P, F]), sec.sb("dequant_old", [P, NS])
        s_dq = sec.sem("dequant_old")
        am, fac, deq, tmp = (sec.sb(n, [P, 2, NS]) for n in ("am", "factor", "dequant", "tmp"))
        ss, ms, nmagic, warm = sec.sb("ss", [P, NS]), sec.sb("ms", [P, NB]), sec.sb("nmagic", [P, 1]), sec.sb("warm", [P, 1])
        rs0, rs1 = Rsqrt(sec, "rs0", NB), Rsqrt(sec, "rs1", NS)
        wsum, wmean, winv = sec.sb("wsum", [P, 2]), sec.sb("wmean", [P, 2]), sec.sb("winv", [P, 2])
        s_f1, s_f2, s_f3, s_fac, s_deq = ([sec.sem(f"{n}{k}") for k in range(2)] for n in (
            "amax_normed", "scale", "inverse", "factor", "dequant"))
        s_am, s_scaled, s_qT_ps, s_qT = ([sec.per_stream(f"{n}{k}_") for k in range(2)] for n in (
            "amax", "scaled", "qT_ps", "qT"))
        s_h_ps, s_h = ([[sec.sem(f"{n}{s}_{m}") for m in range(2)] for s in range(NS)] for n in ("h_ps", "h_pre"))
        s_sq, s_gelu, s_y, s_bo, s_x = (sec.per_stream(n) for n in ("squares", "gelu", "y", "b2_added", "x_done"))
        s_ms, s_nm = sec.sem("mean_square"), sec.sem("minus_magic")
        s_ws, s_wps, s_wst, s_wq = sec.sem("w_sums"), sec.sem("w_mean_ps"), sec.sem("w_steps"), sec.sem("w_rounded")
        with ExitStack() as early:
            wq = [early.enter_context(nc.sbuf_tensor(f"L1f_w{n}q", [P, 8, D] if n == 0 else [P, DC, F], BF16))
                  for n in range(2)]
            flat = T2[0] + T2[1] + H[0]
            lots = [([wq[0][:, f + m, c * P:c * P + P] for m in range(4)],
                     w1T[:, c, f * P:(f + 4) * P].rearrange("p (m n) -> p m n", m=4))
                    for c in range(DC) for f in range(0, FC, 4)]
            lots += [([wq[1][:, c, (f + m) * P:(f + m + 1) * P] for m in range(4)], w2T[:, f:f + 4, c * P:c * P + P])
                     for c in range(DC) for f in range(0, FC, 4)]
            s_t_ps, s_t_sb = sec.sem("turned_ps"), sec.sem("turned_sb")
            with sec.block() as block:
                @block.tensor
                def _(pe):
                    pe.wait_ge(s_ws, 2)
                    pe.matmul(H[1][0][:, 0:2], g.onesP[:, :], wsum[:, :], start=True, stop=True).then_inc(s_wps, 1)
                    pe.wait_ge(s_wq, 2)
                    for k in range(len(lots)):
                        if k >= 6:
                            pe.wait_ge(s_t_sb, k - 5)
                        for m in range(4):
                            mm = pe.transpose(flat[k % 6][:, :].bitcast(BF16)[:, m * P:m * P + P],
                                              lots[k][0][m], g.identb[:, :])
                        mm.then_inc(s_t_ps, 1)

                @block.scalar
                def _(act):
                    for k in range(len(lots)):
                        act.wait_ge(s_t_ps, k + 1)
                        act.copy(lots[k][1], flat[k % 6][:, :].bitcast(BF16)[:, 0:4 * P]
                                 .rearrange("p (m n) -> p m n", m=4)).then_inc(s_t_sb, 1)

                @block.vector
                def _(dve):
                    arrived(dve, g, "L1_ffn")
                    for n in range(2):
                        dve.tensor_reduce(wsum[:, n:n + 1], w[f"w{n + 1}"], AX.XY, ALU.add,
                                          apply_absolute_value=True).then_inc(s_ws, 1)
                    dve.wait_ge(s_wps, 1)
                    dve.tensor_scalar(wmean[:, :], H[1][0][:, 0:2], 1.0 / (F * D), 1e-5, ALU.mult,
                                      ALU.max).then_inc(s_wst, 1)
                    dve.wait_ge(s_wst, 1)
                    dve.reciprocal(winv[:, :], wmean[:, :]).then_inc(s_wst, 1)
                    dve.wait_ge(s_wst, 2)
                    for n in range(2):
                        src = w[f"w{n + 1}"]
                        rounded(dve, wq[n][:, :, :], src, src, winv[:, n:n + 1], s_wst, 2 + 3 * n, (-1.0, 1.0))
                        dve.memset(g.pad[0:1, n:n + 1], 0.0).then_inc(s_wq, 1)

        with sec.block() as block:
            @block.gpsimd
            def _(pool):
                arrived(pool, g, "L1_ffn")

                def step(old, cur, nxt):
                    if nxt:
                        for s in range(NS):
                            b = nxt.b(s)
                            pool.wait_ge(ln.s_xn[s], nxt.v)
                            pool.tensor_tensor(g.x[:, b, :], g.x[:, b, :], w["b2"], ALU.add).then_inc(s_bo[s], 1)
                sweep_pairs(pool, step)

            @block.scalar
            def _(act):
                ln.scalar_start(act)
                act.wait_ge(s_nm, 1)
                act.activation(warm[:, :], nmagic[:, :], ACT.Gelu)

                def step(old, cur, nxt):
                    if old:
                        for s in range(NS):
                            act.wait_ge(s_fac[1], old.v)
                            act.activation(hs[s][:, :], hh[s][:, :], ACT.Identity, bias=g.magic[:, 0:1],
                                           scale=fac[:, 1, s:s + 1]).then_inc(s_scaled[1][s], 1)
                    if cur:
                        for s in range(NS):
                            act.wait_ge(s_h[s][1], cur.v)
                            if old:
                                act.wait_ge(s_scaled[1][s], old.v)
                            act.activation(hh[s][:, :], hp[s][:, :], ACT.Gelu).then_inc(s_gelu[s], 1)
                    if nxt:
                        for s in range(NS):
                            act.wait_ge(s_fac[0], nxt.v)
                            act.activation(xs[s][:, :], ln.xn[s][:, :], ACT.Identity, bias=g.magic[:, 0:1],
                                           scale=fac[:, 0, s:s + 1]).then_inc(s_scaled[0][s], 1)
                    if nxt:
                        for s in range(NS):
                            act.wait_ge(s_qT_ps[0][s], nxt.v)
                            act.activation(xqT[s][:, :, :], XT[s].rearrange("p (c t) -> p c t", c=DC),
                                           ACT.Identity, bias=nmagic[:, 0:1]).then_inc(s_qT[0][s], 1)
                    if cur:
                        for s in range(NS):
                            act.wait_ge(s_gelu[s], cur.v)
                            act.activation(junk[s][:, :], hh[s][:, :], ACT.Square, accum_out=ss[:, s:s + 1]
                                           ).then_inc(s_sq[s], 1)
                    if old:
                        for s in range(NS):
                            act.wait_ge(s_qT_ps[1][s], old.v)
                            for m in range(2):
                                cp = act.activation(hqT[s][:, 4 * m:4 * m + 4, :],
                                                    T2[s][m][:, :].rearrange("p (c t) -> p c t", c=4),
                                                    ACT.Identity, bias=nmagic[:, 0:1])
                            cp.then_inc(s_qT[1][s], 1)
                sweep_pairs(act, step)

            @block.vector
            def _(dve):
                arrived(dve, g, "L1_ffn")
                dve.memset(nmagic[:, :], -MAGIC).then_inc(s_nm, 1)
                ln.vector_start(dve)
                dve.tensor_tensor(ms[:, :], ln.mv[:, :, 1], ln.rstd[:, :, 0], ALU.mult).then_inc(s_ms, 1)
                dve.wait_ge(s_ms, 1)
                dve.tensor_tensor(ms[:, :], ms[:, :], ln.rstd[:, :, 0], ALU.mult).then_inc(s_ms, 1)
                dve.wait_ge(s_ms, 2)
                r0 = rs0.vector(dve, ms[:, :], 1.0, 1e-5, 1)

                def factors(k, r, v):
                    t = tmp[:, k, :]
                    dve.tensor_tensor(t, r, am[:, k, :], ALU.mult).then_inc(s_f1[k], 1)
                    dve.wait_ge(s_f1[k], v)
                    dve.tensor_scalar(t, t, 1e-5, 1.0 / QMAX, ALU.max, ALU.mult).then_inc(s_f2[k], 1)
                    dve.wait_ge(s_f2[k], v)
                    dve.tensor_scalar(deq[:, k, :], t, wmean[:, k:k + 1], None, ALU.mult).then_inc(s_deq[k], 1)
                    dve.reciprocal(fac[:, k, :], t).then_inc(s_f3[k], 1)
                    dve.wait_ge(s_f3[k], v)
                    dve.tensor_tensor(fac[:, k, :], fac[:, k, :], r, ALU.mult).then_inc(s_fac[k], 1)
                    dve.wait_ge(s_deq[k], v)

                def take_h(q, s):
                    for m in range(2):
                        dve.wait_ge(s_h_ps[s][m], q.v)
                        dve.scalar_tensor_tensor(out=hp[s][:, m * BANK:(m + 1) * BANK], in0=H[s][m][:, :],
                                                 scalar=deq[:, 0, s:s + 1], in1=w["b1"][:, m * BANK:(m + 1) * BANK],
                                                 op0=ALU.mult, op1=ALU.add).then_inc(s_h[s][m], 1)

                def step(old, cur, nxt):
                    if nxt:
                        for s in range(NS):
                            ln.vector_norm(dve, s, nxt.b(s))
                        for s in range(NS):
                            dve.wait_ge(ln.s_xn[s], nxt.v)
                            dve.tensor_reduce(am[:, 0, s:s + 1], ln.xn[s][:, :], AX.X, ALU.max,
                                              apply_absolute_value=True).then_inc(s_am[0][s], 1)
                        for s in range(NS):
                            dve.wait_ge(s_am[0][s], nxt.v)
                        if cur:
                            dve.wait_ge(s_h[1][1], cur.v)
                        factors(0, r0[:, nxt.pair], nxt.v)
                    if cur:
                        for s in range(NS):
                            dve.wait_ge(s_gelu[s], cur.v)
                            dve.tensor_reduce(am[:, 1, s:s + 1], hh[s][:, :], AX.X, ALU.max,
                                              apply_absolute_value=True).then_inc(s_am[1][s], 1)
                    if old:
                        dve.tensor_copy(deq_old[:, :], deq[:, 1, :]).then_inc(s_dq, 1)
                        dve.wait_ge(s_dq, old.v)
                    if cur:
                        for s in range(NS):
                            dve.wait_ge(s_am[1][s], cur.v)
                            dve.wait_ge(s_sq[s], cur.v)
                        factors(1, rs1.vector(dve, ss[:, :], 1.0 / F, 1e-5, cur.v), cur.v)
                    if nxt:
                        take_h(nxt, 0)
                        take_h(nxt, 1)
                    if old:
                        for s in range(NS):
                            b = old.b(s)
                            dve.wait_ge(s_y[s], old.v)
                            dve.wait_ge(s_bo[s], old.v)
                            dve.scalar_tensor_tensor(out=g.x[:, b, :], in0=T2[s][0][:, 0:D],
                                                     scalar=deq_old[:, s:s + 1], in1=g.x[:, b, :], op0=ALU.mult,
                                                     op1=ALU.add).then_inc(s_x[s], 1)
                        for s in range(NS):
                            dve.wait_ge(s_x[s], old.v)
                            apart(dve, g)
                            dve.bn_stats(g.stats[:, old.b(s), :], g.x[:, old.b(s), :])
                sweep_pairs(dve, step)

            @block.tensor
            def _(pe):
                def step(old, cur, nxt):
                    if nxt:
                        for s in range(NS):
                            pe.wait_ge(s_scaled[0][s], nxt.v)
                            if cur:
                                pe.wait_ge(s_h[s][0], cur.v)
                            for c in range(DC):
                                mm = pe.transpose(XT[s][:, c * P:c * P + P], xs[s][:, c * P:c * P + P], g.ident[:, :])
                            mm.then_inc(s_qT_ps[0][s], 1)
                    if old:
                        for s in range(NS):
                            pe.wait_ge(s_scaled[1][s], old.v)
                            if not nxt:
                                pe.wait_ge(s_x[s], old.v - 1)
                            for f in range(FC):
                                mm = pe.transpose(T2[s][f // 4][:, f % 4 * P:f % 4 * P + P],
                                                  hs[s][:, f * P:f * P + P], g.ident[:, :])
                            mm.then_inc(s_qT_ps[1][s], 1)
                    if nxt:
                        for s in range(NS):
                            pe.wait_ge(s_qT[0][s], nxt.v)
                            for m in range(2):
                                if cur and m == 1:
                                    pe.wait_ge(s_h[s][m], cur.v)
                                for c in range(DC):
                                    mm = pe.matmul(H[s][m][:, :], xqT[s][:, c, :], w1T[:, c, m * BANK:(m + 1) * BANK],
                                                   start=(c == 0), stop=(c == DC - 1))
                                mm.then_inc(s_h_ps[s][m], 1)
                    if old:
                        for s in range(NS):
                            pe.wait_ge(s_qT[1][s], old.v)
                            for f in range(FC):
                                mm = pe.matmul(T2[s][0][:, 0:D], hqT[s][:, f, :], w2T[:, f, :], start=(f == 0),
                                               stop=(f == FC - 1))
                            mm.then_inc(s_y[s], 1)
                sweep_pairs(pe, step)


class TopTwo:
    STEPS = 11

    def __init__(self, sec, name, rows, groups, n):
        self.shape = [rows, groups, n]
        self.m, self.f = (sec.sb(f"{name}_{k}", [rows, 2, groups]) for k in ("m", "f"))
        self.c, self.d, self.one = (sec.sb(f"{name}_{k}", [rows, 2, groups, n]) for k in ("c", "d", "one"))
        self.rest = sec.sb(f"{name}_rest", self.shape)
        self.s = sec.sem(f"{name}_step")

    def vector(self, dve, g, lg, v):
        n, shape = TopTwo.STEPS * (v - 1), self.shape

        def link(k, ins):
            ins.then_inc(self.s, 1)
            dve.wait_ge(self.s, n + k)
        order = g.order[0:shape[0], 0:shape[2]].unsqueeze(1).to_broadcast(shape)
        src = lg
        for k in range(2):
            m, f, c, d, one = self.m[:, k, :], self.f[:, k, :], self.c[:, k], self.d[:, k], self.one[:, k]
            link(6 * k + 1, dve.tensor_reduce(m, src, AX.X, ALU.max))
            link(6 * k + 2, dve.tensor_tensor(c, src, m.unsqueeze(2).to_broadcast(shape), ALU.is_equal))
            link(6 * k + 3, dve.tensor_tensor(d, c, order, ALU.mult))
            link(6 * k + 4, dve.tensor_reduce(f, d, AX.X, ALU.max))
            link(6 * k + 5, dve.tensor_tensor(one, d, f.unsqueeze(2).to_broadcast(shape), ALU.is_equal))
            if k == 0:
                link(6, dve.scalar_tensor_tensor(out=self.rest[:, :, :], in0=one, scalar=-BIG, in1=lg, op0=ALU.mult,
                                                 op1=ALU.add))
                src = self.rest[:, :, :]


def lora_ffn(nc, g, w):
    sec = Section(nc, "L2f")
    E, R, F = 8, 16, 1024
    FC = F // P
    with sec:
        ln = LayerNorm(sec, g)
        U = [[sec.ps(f"inner{s}_{t}", [P, BANK]) for t in range(2)] for s in range(NS)]
        X, Y = ([sec.ps(f"{n}{s}", [P, BANK]) for s in range(NS)] for n in ("x_turned", "y_ps"))
        sbs = lambda nm, shape, dt=F32: [sec.sb(f"{nm}{s}", shape, dt) for s in range(NS)]
        wiT, woT, bT = sec.sb("wiT", [P, DC, F]), sec.sb("woT", [P, FC, D]), sec.sb("loraBT", [P, F])
        agT = sec.sb("loraA_gateT", [P, DC, P + E])
        bo2 = sec.sb("bo2", [P, D])
        xT, xTb, y = sbs("xT", [P, DC, P]), sbs("xTb", [P, DC, P]), sbs("y", [P, D])
        lg, dl, diff = sec.sb("logits", [P, NS, E]), sec.sb("dl", [P, NS, E + 1]), sec.sb("diff", [P, NS, E])
        den, rden, vs, warm = (sec.sb(n, [P, k]) for n, k in (("den", NS), ("rden", NS), ("vs", NS), ("warm", 1)))
        tk = TopTwo(sec, "top", P, NS, E)
        ta, tb = sbs("ta", [P, 2, P]), sbs("taT", [P, 2, P])
        hs, u = sbs("hs", [P, FC, P]), [sbs(f"u{s}_", [P, 4, P]) for s in range(NS)]
        jobs = [(w["wi"][:, f, c * P:c * P + P], wiT[:, c, f * P:f * P + P]) for c in range(DC) for f in range(FC)]
        jobs += [(w["wo"][:, c, f * P:f * P + P], woT[:, f, c * P:c * P + P]) for f in range(FC) for c in range(DC)]
        jobs += [(w["lora_B"][:, f, :], bT[:, f * P:f * P + P]) for f in range(FC)]
        jobs += [(w["lora_A"][:, c * P:c * P + P], agT[:, c, 0:P]) for c in range(DC)]
        jobs += [(w["gate_w"][:, c * P:c * P + P], agT[:, c, P:P + E]) for c in range(DC)]
        turn_w = Turned(sec, [U[0][0], U[1][0]], jobs)
        (s_xT_ps, s_xT, s_xTb, s_t_ps, s_lg, s_ta, s_taT_ps, s_taT, s_first, s_y_ps, s_y, s_x) = (
            sec.per_stream(n) for n in ("xT_ps", "xT", "xTb", "lora_ps", "logits", "masked", "maskedT_ps",
                                        "maskedT", "first_made", "y_ps", "y", "x_done"))
        s_u1, s_r1, s_u2, s_hs = ([[sec.sem(f"{n}{s}_{t}") for t in range(2)] for s in range(NS)] for n in (
            "first", "first_relu", "second", "hidden"))
        s_u_ps = [[[sec.sem(f"{n}{s}_{t}") for t in range(2)] for s in range(NS)] for n in ("first_ps", "second_ps")]
        s_dl, s_e, s_vs, s_diff, s_den, s_rden = (sec.sem(n) for n in (
            "shifted", "exp", "val_sum", "mask_diff", "den", "inverse_den"))
        s_bo2 = sec.sem("bo2")
        with sec.block() as block:
            @block.tensor
            def _(pe):
                arrived(pe, g, "L2_ffn")
                turn_w.tensor(pe, g.ident)
                turn_w.wait(pe)

                def first(q, s):
                    pe.wait_ge(s_xTb[s], q.v)
                    for f in range(FC):
                        for c in range(DC):
                            mm = pe.matmul(U[s][f // 4][:, f % 4 * P:f % 4 * P + P], wiT[:, c, f * P:f * P + P],
                                           xTb[s][:, c, :], start=(f % 4 == 0 and c == 0), stop=False,
                                           skip_group_check=True)
                    mm.then_inc(s_first[s], 1)

                def expert(q, s, k):
                    pe.wait_ge(s_taT[s], q.v)
                    for f in range(FC):
                        if k == 1 and f % 4 == 0:
                            pe.wait_ge(s_u1[s][f // 4], q.v)
                        mm = pe.matmul(U[s][f // 4][:, f % 4 * P:f % 4 * P + P], bT[:, f * P:f * P + P],
                                       tb[s][:, k, :], start=False, stop=(k == 1), skip_group_check=True)
                        if f % 4 == 3:
                            mm.then_inc(s_u_ps[k][s][f // 4], 1)

                def down(q, s, cur):
                    if cur:
                        pe.wait_ge(s_taT[s], cur.v)
                    elif q.v > 1:
                        pe.wait_ge(s_y[s], q.v - 1)
                    for f in range(FC):
                        if f % 4 == 0:
                            pe.wait_ge(s_hs[s][f // 4], q.v)
                        mm = pe.matmul(Y[s][:, 0:D], hs[s][:, f, :], woT[:, f, :], start=(f == 0), stop=(f == FC - 1))
                    mm.then_inc(s_y_ps[s], 1)

                def step(old, cur, nxt):
                    if old:
                        for s in range(NS):
                            first(old, s)
                        for s in range(NS):
                            expert(old, s, 0)
                    if cur:
                        for s in range(NS):
                            pe.wait_ge(s_ta[s], cur.v)
                            for k in range(2):
                                mm = pe.transpose(Y[s][:, k * P:(k + 1) * P], ta[s][:, k, :], g.ident[:, :])
                            mm.then_inc(s_taT_ps[s], 1)
                    if old:
                        for s in range(NS):
                            expert(old, s, 1)
                    if nxt:
                        for s in range(NS):
                            pe.wait_ge(ln.s_xn[s], nxt.v)
                            for c in range(DC):
                                mm = pe.transpose(X[s][:, c * P:c * P + P], ln.xn[s][:, c * P:c * P + P], g.ident[:, :])
                            mm.then_inc(s_xT_ps[s], 1)
                    if old:
                        down(old, 0, cur)
                    if nxt:
                        for s in range(NS):
                            pe.wait_ge(s_xT[s], nxt.v)
                            for c in range(DC):
                                mm = pe.matmul(X[s][:, D:D + P + E], xT[s][:, c, :], agT[:, c, :], start=(c == 0),
                                               stop=(c == DC - 1))
                            mm.then_inc(s_t_ps[s], 1)
                    if old:
                        down(old, 1, cur)
                sweep_pairs(pe, step)

            @block.scalar
            def _(act):
                turn_w.scalar(act)
                ln.scalar_start(act)
                act.activation(warm[:, :], g.eps[:, :], ACT.Exp)

                def step(old, cur, nxt):
                    if cur:
                        for s in range(NS):
                            act.wait_ge(s_xT[s], cur.v)
                            if old:
                                act.wait_ge(s_first[s], old.v)
                            act.copy(xTb[s][:, :, :], xT[s][:, :, :]).then_inc(s_xTb[s], 1)
                        act.wait_ge(s_dl, cur.v)
                        act.activation(dl[:, :, :], dl[:, :, :], ACT.Exp).then_inc(s_e, 1)
                    if old:
                        for s in range(NS):
                            for t in range(2):
                                act.wait_ge(s_u1[s][t], old.v)
                                act.activation(hs[s][:, 4 * t:4 * t + 4, :], hs[s][:, 4 * t:4 * t + 4, :], ACT.Relu
                                               ).then_inc(s_r1[s][t], 1)
                    if cur:
                        for s in range(NS):
                            act.wait_ge(s_taT_ps[s], cur.v)
                            if old:
                                act.wait_ge(s_u_ps[1][s][1], old.v)
                            act.copy(tb[s][:, :, :], Y[s][:, 0:2 * P].rearrange("p (k t) -> p k t", k=2)
                                     ).then_inc(s_taT[s], 1)
                    if nxt:
                        for s in range(NS):
                            act.wait_ge(s_xT_ps[s], nxt.v)
                            if cur:
                                act.wait_ge(s_xTb[s], cur.v)
                            act.copy(xT[s][:, :, :], X[s][:, 0:D].rearrange("p (c t) -> p c t", c=DC)
                                     ).then_inc(s_xT[s], 1)
                sweep_pairs(act, step)

            @block.gpsimd
            def _(pool):
                arrived(pool, g, "L2_ffn")
                pool.tensor_tensor(bo2[:, :], w["bo"], w["bo"], ALU.add).then_inc(s_bo2, 1)

            @block.vector
            def _(dve):
                arrived(dve, g, "L2_ffn")
                dve.wait_ge(s_bo2, 1)
                ln.vector_start(dve)
                one = tk.one
                bi = lambda t: w["bi"][:, 4 * t:4 * t + 4].unsqueeze(2).to_broadcast([P, 4, P])
                ps = lambda s, t: U[s][t][:, :].rearrange("p (m t) -> p m t", m=4)
                er = lambda ap: ap.rearrange("p (e r) -> p e r", e=E)

                def gate(q):
                    for s in range(NS):
                        dve.wait_ge(s_t_ps[s], q.v)
                        dve.tensor_tensor(lg[:, s, :], X[s][:, D + P:D + P + E], w["gate_b"], ALU.add
                                          ).then_inc(s_lg[s], 1)
                    for s in range(NS):
                        dve.wait_ge(s_lg[s], q.v)
                    tk.vector(dve, g, lg[:, :, :], q.v)
                    top = tk.m[:, 0, :]
                    dve.tensor_tensor(dl[:, :, 0:E], lg[:, :, :], top.unsqueeze(2).to_broadcast([P, NS, E]),
                                      ALU.subtract)
                    dve.tensor_tensor(dl[:, :, E], tk.m[:, 1, :], top, ALU.subtract).then_inc(s_dl, 1)
                    dve.tensor_tensor(diff[:, :, :], one[:, 1, :, :], one[:, 0, :, :], ALU.subtract
                                      ).then_inc(s_diff, 1)
                    dve.wait_ge(s_diff, q.v)
                    for s in range(NS):
                        t_ps = er(X[s][:, D:D + P])
                        dve.tensor_tensor(er(ta[s][:, 0, :]), t_ps, one[:, 0, s, :].unsqueeze(2).to_broadcast([P, E, R]),
                                          ALU.mult)
                        dve.tensor_tensor(er(ta[s][:, 1, :]), t_ps, diff[:, s, :].unsqueeze(2).to_broadcast([P, E, R]),
                                          ALU.mult).then_inc(s_ta[s], 1)

                def step(old, cur, nxt):
                    if cur:
                        gate(cur)
                    if nxt:
                        for s in range(NS):
                            ln.vector_norm(dve, s, nxt.b(s))
                    if old:
                        for s in range(NS):
                            for t in range(2):
                                dve.wait_ge(s_u_ps[0][s][t], old.v)
                                dve.tensor_tensor(hs[s][:, 4 * t:4 * t + 4, :], ps(s, t), bi(t), ALU.add
                                                  ).then_inc(s_u1[s][t], 1)
                        for s in range(NS):
                            for t in range(2):
                                dve.wait_ge(s_u_ps[1][s][t], old.v)
                                dve.tensor_tensor(u[s][t][:, :, :], ps(s, t), bi(t), ALU.add).then_inc(s_u2[s][t], 1)
                            for t in range(2):
                                dve.wait_ge(s_u2[s][t], old.v)
                                dve.wait_ge(s_r1[s][t], old.v)
                                dve.scalar_tensor_tensor(out=hs[s][:, 4 * t:4 * t + 4, :], in0=u[s][t][:, :, :],
                                                         scalar=0.0, in1=hs[s][:, 4 * t:4 * t + 4, :], op0=ALU.max,
                                                         op1=ALU.add).then_inc(s_hs[s][t], 1)
                        for s in range(NS):
                            b = old.b(s)
                            dve.wait_ge(s_y_ps[s], old.v)
                            dve.tensor_tensor(y[s][:, :], Y[s][:, 0:D], bo2[:, :], ALU.add).then_inc(s_y[s], 1)
                            dve.wait_ge(s_y[s], old.v)
                            dve.scalar_tensor_tensor(out=g.x[:, b, :], in0=y[s][:, :], scalar=vs[:, s:s + 1],
                                                     in1=g.x[:, b, :], op0=ALU.mult, op1=ALU.add).then_inc(s_x[s], 1)
                        for s in range(NS):
                            dve.wait_ge(s_x[s], old.v)
                            apart(dve, g)
                            dve.bn_stats(g.stats[:, old.b(s), :], g.x[:, old.b(s), :])
                    if cur:
                        dve.wait_ge(s_e, cur.v)
                        dve.tensor_reduce(den[:, :], dl[:, :, 0:E], AX.X, ALU.add).then_inc(s_den, 1)
                        dve.wait_ge(s_den, cur.v)
                        dve.reciprocal(rden[:, :], den[:, :]).then_inc(s_rden, 1)
                        dve.wait_ge(s_rden, cur.v)
                        dve.scalar_tensor_tensor(out=vs[:, :], in0=dl[:, :, E], scalar=1.0, in1=rden[:, :],
                                                 op0=ALU.add, op1=ALU.mult).then_inc(s_vs, 1)
                        dve.wait_ge(s_vs, cur.v)
                sweep_pairs(dve, step)


def gated_attention(nc, g, w, ctx_dram):
    sec = Section(nc, "L3a")
    SCALE = D ** -0.5
    with sec:
        ln = LayerNorm(sec, g)
        bank = banks_of(sec)
        sbs = lambda nm, shape, dt=F32: [sec.sb(f"{nm}{s}", shape, dt) for s in range(NS)]
        qk, gwT = sec.sb("qk", [P, DC, D]), sec.sb("gate_wT", [P, DC, D])
        mem, memT = sbs("mem", [P, D]), sbs("memT", [P, DC, P])
        ss, rs = sec.sb("ss", [P, NS]), Rsqrt(sec, "rs", NS)
        sq, nm = sbs("squares", [P, D]), sbs("nm", [P, D])
        xT, nmT, qT = sbs("xT", [P, DC, P]), sbs("nmT", [P, DC, P]), sbs("qT", [P, DC, P])
        lgt, pT = sbs("logits", [P, 2, P]), sbs("probsT", [P, 2, P])
        mx, den = sbs("mx", [P, 2]), sbs("den", [P, 2])
        z, d = sbs("z", [P, D]), sbs("d", [P, D])
        jobs = [(w["gate_w"][:, m, c * P:c * P + P], gwT[:, c, m * P:m * P + P]) for m in range(DC) for c in range(DC)]
        turn_w = Turned(sec, [bank[0][0], bank[1][0]], jobs)
        s_qk_ps, s_qk, s_sq = sec.sem("qk_ps"), sec.sem("qk"), sec.sem("sumsq")
        (s_mem, s_memT, s_nm, s_xT_ps, s_xT, s_q_ps, s_q, s_z_ps, s_z, s_ez, s_ap1, s_al, s_l_ps, s_lg, s_mx, s_nb,
         s_p, s_pT_ps, s_pT, s_h, s_rd, s_d1, s_d2, s_d3, s_x, s_nmT_ps, s_nmT) = (sec.per_stream(n) for n in (
             "mem", "memT", "normed", "xT_ps", "xT", "q_ps", "q", "z_ps", "z", "exp_z", "alpha1", "alpha", "logits_ps",
             "logits", "max", "neg_max", "probs", "probsT_ps", "probsT", "h_tilde", "recip", "d1", "d2", "d3",
             "x_done", "nmT_ps", "nmT"))
        with sec.block() as block:
            @block.sync
            def _(sp):
                for s in range(NS):
                    sp.dma_start(mem[s][:, :], ctx_dram[s, :, :]).then_inc(s_mem[s], 16)
                    sp.dma_start(memT[s][:, :, :], g.ctxT[:, s, :, :]).then_inc(s_memT[s], 16)
                with sp.Fori(1, TURNS) as i:
                    for s in range(NS):
                        sp.wait_ge(s_h[s], i)
                        sp.dma_start(mem[s][:, :], ctx_dram[NS * i + s, :, :]).then_inc(s_mem[s], 16)
                        sp.dma_start(memT[s][:, :, :], g.ctxT[:, NS * i + s, :, :]).then_inc(s_memT[s], 16)

            @block.tensor
            def _(pe):
                arrived(pe, g, "L3_xattn")
                turn_w.tensor(pe, g.ident)
                for m in range(DC):
                    for c in range(DC):
                        mm = pe.matmul(bank[0][2][:, m * D:m * D + D], w["q_w"][:, c, m * P:m * P + P], w["k_w"][:, c, :],
                                       start=(c == 0), stop=(c == DC - 1))
                mm.then_inc(s_qk_ps, 1)
                turn_w.wait(pe)
                pe.wait_ge(s_qk, 1)
                with pe.Fori(1, TURNS + 1) as i:
                    def turn(s, src, out, s_done):
                        for c in range(DC):
                            mm = pe.transpose(out[:, c * P:c * P + P], src[s][:, c * P:c * P + P], g.ident[:, :])
                        mm.then_inc(s_done[s], 1)
                    for s in range(NS):
                        pe.wait_ge(ln.s_xn[s], i)
                        turn(s, ln.xn, bank[s][3], s_xT_ps)
                    for s in range(NS):
                        pe.wait_ge(s_xT[s], i)
                        for c in range(DC):
                            mm = pe.matmul(bank[s][2][:, 0:D], xT[s][:, c, :], gwT[:, c, :], start=(c == 0),
                                           stop=(c == DC - 1))
                        mm.then_inc(s_z_ps[s], 1)
                    for s in range(NS):
                        pe.wait_ge(s_nm[s], i)
                        turn(s, nm, bank[s][3], s_nmT_ps)
                    for s in range(NS):
                        pe.wait_ge(s_nmT[s], i)
                        for m in range(DC):
                            for c in range(DC):
                                mm = pe.matmul(bank[s][0][:, m * P:m * P + P], qk[:, c, m * P:m * P + P], nmT[s][:, c, :],
                                               start=(c == 0), stop=(c == DC - 1))
                        mm.then_inc(s_q_ps[s], 1)
                    for s in range(NS):
                        pe.wait_ge(s_q[s], i)
                        pe.wait_ge(s_memT[s], 16 * i)
                        for k, keys in enumerate((nmT, memT)):
                            for c in range(DC):
                                mm = pe.matmul(bank[s][1][:, k * P:k * P + P], qT[s][:, c, :], keys[s][:, c, :],
                                               start=(c == 0), stop=(c == DC - 1))
                        mm.then_inc(s_l_ps[s], 1)
                    for s in range(NS):
                        pe.wait_ge(s_p[s], i)
                        for k in range(2):
                            mm = pe.transpose(bank[s][3][:, k * P:k * P + P], lgt[s][:, k, :], g.ident[:, :])
                        mm.then_inc(s_pT_ps[s], 1)
                    for s in range(NS):
                        pe.wait_ge(s_pT[s], i)
                        pe.wait_ge(s_mem[s], 16 * i)
                        pe.matmul(bank[s][0][:, 0:D], pT[s][:, 0, :], nm[s][:, :], start=True, stop=False)
                        pe.matmul(bank[s][0][:, 0:D], pT[s][:, 1, :], mem[s][:, :], start=False, stop=True
                                  ).then_inc(s_h[s], 1)

            @block.scalar
            def _(act):
                turn_w.scalar(act)
                act.wait_ge(s_qk_ps, 1)
                act.copy(qk[:, :, :], bank[0][2][:, :].rearrange("p (c n) -> p c n", c=DC)).then_inc(s_qk, 1)
                ln.scalar_start(act)
                two = lambda ap: ap[:, 0:D].rearrange("p (c t) -> p c t", c=DC)
                with act.Fori(1, TURNS + 1) as i:
                    for s in range(NS):
                        act.wait_ge(ln.s_xn[s], i)
                        act.activation(sq[s][:, :], ln.xn[s][:, :], ACT.Square, accum_out=ss[:, s:s + 1]).then_inc(s_sq, 1)
                    for s in range(NS):
                        act.wait_ge(s_xT_ps[s], i)
                        act.copy(xT[s][:, :, :], two(bank[s][3])).then_inc(s_xT[s], 1)
                    for s in range(NS):
                        act.wait_ge(s_nmT_ps[s], i)
                        act.copy(nmT[s][:, :, :], two(bank[s][3])).then_inc(s_nmT[s], 1)
                    for s in range(NS):
                        act.wait_ge(s_q_ps[s], i)
                        act.copy(qT[s][:, :, :], two(bank[s][0])).then_inc(s_q[s], 1)
                    for s in range(NS):
                        act.wait_ge(s_z[s], i)
                        act.activation(z[s][:, :], z[s][:, :], ACT.Exp, scale=-1.0).then_inc(s_ez[s], 1)
                    for s in range(NS):
                        act.wait_ge(s_nb[s], i)
                        act.activation(lgt[s][:, :, :], lgt[s][:, :, :], ACT.Exp, bias=mx[s][:, 1:2], scale=SCALE,
                                       accum_out=den[s][:, 0:1]).then_inc(s_p[s], 1)
                    for s in range(NS):
                        act.wait_ge(s_pT_ps[s], i)
                        act.copy(pT[s][:, :, :], two(bank[s][3])).then_inc(s_pT[s], 1)

            @block.vector
            def _(dve):
                arrived(dve, g, "L3_xattn")
                ln.vector_start(dve)
                with dve.Fori(1, TURNS + 1) as i:
                    for s in range(NS):
                        ln.vector_apply(dve, s, i)
                    dve.wait_ge(s_sq, NS * i)
                    r = rs.vector(dve, ss[:, :], 1.0 / D, 1e-6, i)
                    for s in range(NS):
                        dve.scalar_tensor_tensor(out=nm[s][:, :], in0=ln.xn[s][:, :], scalar=r[:, s:s + 1], in1=w["norm_w"],
                                                 op0=ALU.mult, op1=ALU.mult).then_inc(s_nm[s], 1)
                    for s in range(NS):
                        dve.wait_ge(s_z_ps[s], i)
                        dve.tensor_tensor(z[s][:, :], bank[s][2][:, 0:D], w["gate_b"], ALU.add).then_inc(s_z[s], 1)
                    for s in range(NS):
                        dve.wait_ge(s_l_ps[s], i)
                        dve.tensor_tensor(lgt[s][:, :, :], bank[s][1][:, 0:D].rearrange("p (k t) -> p k t", k=2),
                                          g.causal[:, :, :], ALU.add).then_inc(s_lg[s], 1)
                        dve.wait_ge(s_lg[s], i)
                        dve.tensor_reduce(mx[s][:, 0:1], lgt[s][:, :, :], AX.XY, ALU.max).then_inc(s_mx[s], 1)
                        dve.wait_ge(s_mx[s], i)
                        dve.tensor_scalar(mx[s][:, 1:2], mx[s][:, 0:1], -SCALE, None, ALU.mult).then_inc(s_nb[s], 1)
                    for s in range(NS):
                        dve.wait_ge(s_ez[s], i)
                        dve.tensor_scalar(z[s][:, :], z[s][:, :], 1.0, None, ALU.add).then_inc(s_ap1[s], 1)
                        dve.wait_ge(s_ap1[s], i)
                        dve.reciprocal(z[s][:, :], z[s][:, :]).then_inc(s_al[s], 1)
                    for s in range(NS):
                        dve.wait_ge(s_p[s], i)
                        dve.reciprocal(den[s][:, 1:2], den[s][:, 0:1]).then_inc(s_rd[s], 1)
                    for s in range(NS):
                        dve.wait_ge(s_rd[s], i)
                        dve.wait_ge(s_al[s], i)
                        dve.wait_ge(s_h[s], i)
                        dve.scalar_tensor_tensor(out=d[s][:, :], in0=bank[s][0][:, 0:D], scalar=den[s][:, 1:2],
                                                 in1=ln.xn[s][:, :], op0=ALU.mult, op1=ALU.subtract).then_inc(s_d1[s], 1)
                        dve.wait_ge(s_d1[s], i)
                        dve.tensor_tensor(d[s][:, :], d[s][:, :], z[s][:, :], ALU.mult).then_inc(s_d2[s], 1)
                        dve.wait_ge(s_d2[s], i)
                        dve.tensor_tensor(d[s][:, :], d[s][:, :], ln.xn[s][:, :], ALU.add).then_inc(s_d3[s], 1)
                        dve.wait_ge(s_d3[s], i)
                        dve.tensor_tensor(tile_of(g, i, s), d[s][:, :], tile_of(g, i, s), ALU.add).then_inc(s_x[s], 1)
                    for s in range(NS):
                        ln.vector_stats(dve, s, i, s_x)


def expert_gates(nc, g, w):
    sec = Section(nc, "L3g")
    E, HID = 4, 128
    with sec:
        ln = LayerNorm(sec, g)
        bank = banks_of(sec)
        r, mr = sec.sb("r", [P, NB, 1]), sec.sb("mr", [P, NB])
        pooled, hid = sec.sb("pooled", [P, DC, NB]), sec.sb("hid", [HID, NB])
        lg, dg = sec.sb("logits", [NB, E]), sec.sb("spread", [NB, NB, E])
        sw = sec.sb("shares", [NB, 4])
        wt = sec.sb("weights", [NB, 2, E])
        tk = TopTwo(sec, "top", NB, 1, E)
        s_mr, s_ps, s_pool, s_hid_ps, s_hid, s_lg_ps, s_lg, s_e, s_st, s_g_ps = (sec.sem(n) for n in (
            "mean_factors", "pooled_ps", "pooled", "hidden_ps", "hidden", "logits_ps", "logits", "exp", "steps",
            "gates_ps"))
        corr = sec.sb("correction", [P, NB])
        s_corr = sec.sem("correction")
        with sec.block() as block:
            @block.tensor
            def _(pe):
                arrived(pe, g, "L3_ffn")
                pe.wait_ge(s_mr, 2)
                pe.matmul(bank[0][0][:, 0:NB], g.onesP[:, :], mr[:, :], start=True, stop=True)
                for b in range(NB):
                    for c in range(DC):
                        n = NB * (c + 1) + b
                        mm = pe.matmul(bank[0][0][:, n:n + 1], g.x[:, b, c * P:c * P + P], r[:, b, :], start=True,
                                       stop=True)
                mm.then_inc(s_ps, 1)
                pe.wait_ge(s_pool, 1)
                for c in range(DC):
                    mm = pe.matmul(bank[0][1][0:HID, 0:NB], w["Wg1"][:, c, :], pooled[:, c, :], start=(c == 0),
                                   stop=(c == DC - 1))
                mm.then_inc(s_hid_ps, 1)
                pe.wait_ge(s_hid, 1)
                pe.matmul(bank[0][2][0:NB, 0:E], hid[:, :], w["Wg2"][:, 0, :], start=True, stop=True).then_inc(s_lg_ps, 1)
                pe.wait_ge(s_st, 6)
                pe.matmul(bank[0][3][:, 0:NB * E], g.onesP[0:NB, :], dg[:, :, :], start=True, stop=True).then_inc(s_g_ps, 1)

            @block.scalar
            def _(act):
                arrived(act, g, "L3_ffn")
                ln.scalar_start(act)
                act.wait_ge(s_hid_ps, 1)
                act.activation(hid[:, :], bank[0][1][0:HID, 0:NB], ACT.Relu, bias=w["bg1"][:, 0:1]).then_inc(s_hid, 1)
                act.wait_ge(s_st, 1)
                act.activation(sw[:, 1:2], sw[:, 0:1], ACT.Exp).then_inc(s_e, 1)

            @block.vector
            def _(dve):
                arrived(dve, g, "L3_ffn")
                ln.vector_start(dve)
                dve.tensor_scalar(r[:, :, 0], ln.rstd[:, :, 0], 1.0 / P, None, ALU.mult).then_inc(s_mr, 1)
                dve.wait_ge(s_mr, 1)
                dve.tensor_tensor(mr[:, :], r[:, :, 0], ln.mv[:, :, 0], ALU.mult).then_inc(s_mr, 1)
                dve.wait_ge(s_ps, 1)
                dve.tensor_copy(corr[:, :], bank[0][0][:, 0:NB]).then_inc(s_corr, 1)
                dve.wait_ge(s_corr, 1)
                dve.tensor_tensor(pooled[:, :, :],
                                  bank[0][0][:, NB:3 * NB].rearrange("p (c b) -> p c b", c=DC),
                                  corr[:, :].unsqueeze(1).to_broadcast([P, DC, NB]), ALU.subtract).then_inc(s_pool, 1)
                dve.wait_ge(s_lg_ps, 1)
                dve.tensor_tensor(lg[:, :], bank[0][2][0:NB, 0:E], w["bg2"][0:NB, :], ALU.add).then_inc(s_lg, 1)
                dve.wait_ge(s_lg, 1)
                tk.vector(dve, g, lg[:, :].unsqueeze(1), 1)
                dve.tensor_scalar(sw[:, 0:1], tk.m[:, 1:2], tk.m[:, 0:1], None, ALU.subtract).then_inc(s_st, 1)
                dve.wait_ge(s_e, 1)
                dve.tensor_scalar(sw[:, 2:3], sw[:, 1:2], 1.0, None, ALU.add).then_inc(s_st, 1)
                dve.wait_ge(s_st, 2)
                dve.reciprocal(sw[:, 2:3], sw[:, 2:3]).then_inc(s_st, 1)
                dve.wait_ge(s_st, 3)
                dve.tensor_tensor(sw[:, 3:4], sw[:, 2:3], sw[:, 1:2], ALU.mult)
                dve.tensor_scalar(wt[:, 0, :], tk.one[:, 0, 0, :], sw[:, 2:3], None, ALU.mult).then_inc(s_st, 1)
                dve.wait_ge(s_st, 4)
                dve.scalar_tensor_tensor(out=wt[:, 1, :], in0=tk.one[:, 1, 0, :], scalar=sw[:, 3:4], in1=wt[:, 0, :],
                                         op0=ALU.mult, op1=ALU.add).then_inc(s_st, 1)
                dve.wait_ge(s_st, 5)
                dve.tensor_tensor(dg[:, :, :], g.ident[0:NB, 0:NB].unsqueeze(2).to_broadcast([NB, NB, E]),
                                  wt[:, 1, :].unsqueeze(1).to_broadcast([NB, NB, E]), ALU.mult).then_inc(s_st, 1)
                dve.wait_ge(s_g_ps, 1)
                dve.tensor_copy(g.gates[:, :, :, 0], bank[0][3][:, 0:NB * E].rearrange("p (b e) -> p b e", e=E))


def start_loads(nc, g):
    sec = Section(nc, "loads")
    with sec, sec.block() as block:
        @block.sync
        def _(sp):
            for dst, src, what in g.loads:
                sp.dma_start(dst, src, allow_slow_non_contiguous=True).then_inc(g.loaded[what], 16)


def finish(nc, g, out):
    sec = Section(nc, "finish")
    with sec:
        s_out = sec.sem("out")
        with sec.block() as block:
            @block.sync
            def _(sp):
                sp.dma_start(out.rearrange("b p d -> p b d"), g.x[:, :, :]).then_inc(s_out, 16)
                sp.wait_ge(s_out, 16)


def program(nc, a, out):
    g = Globals()
    with ExitStack() as whole:
        scope = [whole]

        def sb(name, shape, dt=F32):
            return scope[-1].enter_context(nc.sbuf_tensor(name, shape, dt))

        g.loads, g.counts = [], {"x": 1}
        g.loaded = {"x": nc.alloc_semaphore("x_loaded")}

        def loading(what, dst, src):
            if what not in g.loaded:
                g.loaded[what] = nc.alloc_semaphore(f"{what}_loaded")
                g.counts[what] = 0
            g.counts[what] += 1
            g.loads.append((dst, src, what))

        def load(what, name, shape, src, dt=F32):
            t = sb(name, shape, dt)
            t = t[tuple(slice(None) for _ in shape)]
            loading(what, t, src)
            return t

        def matrix(what, name):
            r, n = a[name].shape
            return load(what, name, [P, r // P, n], a[name].rearrange("(c p) n -> p c n", p=P))

        def column(what, name):
            return load(what, name, [P, a[name].shape[0] // P], a[name].rearrange("(c p) -> p c", p=P))

        def row(what, name):
            return load(what, name, [P, a[name].shape[0]], a[name].partition_broadcast(P))

        g.x = sb("x_all", [P, NB, D])
        g.stats = sb("stats", [P, NB, 6])
        g.ctxT = sb("ctxT_all", [P, NB, DC, P])
        g.ident, g.hmask, g.causal = sb("ident", [P, P]), sb("hmask", [P, HC]), sb("causal", [P, 2, P])
        g.pad, g.pads = sb("pad", [1, PADS]), 0
        g.order, g.hidden, g.identb = sb("order", [P, 8]), sb("hidden", [P, P], BF16), sb("identb", [P, P], BF16)
        g.gates = sb("gates", [P, NB, 4, 1])
        g.mask = load("mask", "mask", [P, P], a["mask_1x1xSxS2_bk0"].rearrange("a b q k -> (a b q) k"), U8)
        g.eps, g.magic, g.onesP = sb("eps", [P, 1]), sb("magic", [P, 1]), sb("onesP", [P, P])

        scope.append(whole.enter_context(ExitStack()))

        def xattn(n):
            what = f"L{n}_xattn"
            w = {k: matrix(what, f"{what}_{k}") for k in ("Wq", "Wk", "Wv", "Wo")}
            w.update({k: column(what, f"{what}_{k}") for k in ("bq", "bk")})
            w.update({k: row(what, f"{what}_{k}") for k in ("bv", "bo")})
            return w

        w0, f0 = xattn(0), {}
        for k in ("gate", "up"):
            f0[k] = sb(f"L0_ffn_{k}", [P, FC0, D])[:, :, :]
            src, full = a[f"L0_ffn_w_{k}"], F0 // P * P
            loading("L0_ffn", f0[k][:, 0:F0 // P, :], src[0:full, :].rearrange("(c p) n -> p c n", p=P))
            loading("L0_ffn", f0[k][0:F0 - full, F0 // P, :], src[full:F0, :])
        f0["down"] = sb("L0_ffn_down", [P, DC, FC0 * P])[:, :, :]
        loading("L0_ffn", f0["down"][:, :, 0:F0], a["L0_ffn_w_down"].rearrange("(c p) n -> p c n", p=P))
        f0.update({k: row("L0_ffn", f"L0_ffn_{k}") for k in ("clip_x", "clip_down")})
        w1 = xattn(1)
        f1 = {k: matrix("L1_ffn", f"L1_ffn_{k}") for k in ("w1", "w2")}
        f1.update({k: row("L1_ffn", f"L1_ffn_{k}") for k in ("b1", "b2")})
        setup(nc, g, a)
        attention(nc, g, "L0a", PLAIN, w0, None, ["L0_xattn"])
        fake_quant_ffn(nc, g, f0)
        turned_attention(nc, g, "L1a", PRUNED, w1, ["L1_xattn"])
        bitlinear_ffn(nc, g, f1)
        scope.pop().close()

        scope.append(whole.enter_context(ExitStack()))
        g.loads = []
        w2 = xattn(2)
        f2 = {k: matrix("L2_ffn", f"L2_ffn_{k}") for k in ("wi", "wo")}
        f2["lora_A"] = load("L2_ffn", "L2_ffn_lora_A", [P, D], a["L2_ffn_lora_A"].rearrange("e r d -> (e r) d"))
        f2["gate_w"] = load("L2_ffn", "L2_ffn_gate_w", [8, D], a["L2_ffn_gate_w"])
        f2["lora_B"] = sb("L2_ffn_lora_B", [P, 8, P])[:, :, :]
        for f in range(8):
            loading("L2_ffn", f2["lora_B"][:, f, :].rearrange("p (e r) -> p e r", e=8),
                    a["L2_ffn_lora_B"][:, f * P:f * P + P, :].rearrange("e p r -> p e r"))
        f2["bi"] = column("L2_ffn", "L2_ffn_bi")
        f2.update({k: row("L2_ffn", f"L2_ffn_{k}") for k in ("bo", "gate_b")})
        a3 = {k: matrix("L3_xattn", f"L3_xattn_{k}") for k in ("q_w", "k_w", "gate_w")}
        a3.update({k: row("L3_xattn", f"L3_xattn_{k}") for k in ("norm_w", "gate_b")})
        E3, g.mixed_at, g.mixw = 4, {}, 0
        for k in ("Wk", "bk", "bq", "Wq", "Wv", "bv"):
            g.mixed_at[k] = g.mixw
            g.mixw += DC * D if k[0] == "W" else D if k == "bv" else DC
        g.mixk = g.mixed_at["Wq"]
        g.experts = sb("experts", [P, E3, g.mixw])
        for e in range(E3):
            for k, at in g.mixed_at.items():
                src = a[f"L3_ffn_{k}"][e]
                if k[0] == "W":
                    loading("L3_ffn", g.experts[:, e, at:at + DC * D].rearrange("p (c n) -> p c n", c=DC),
                            src.rearrange("(c p) n -> p c n", p=P))
                elif k == "bv":
                    loading("L3_ffn", g.experts[:, e, at:at + D], src.partition_broadcast(P))
                else:
                    loading("L3_ffn", g.experts[:, e, at:at + DC], src.rearrange("(c p) -> p c", p=P))
        f3 = {k: matrix("L3_ffn", f"L3_ffn_{k}") for k in ("Wo", "Wg1", "Wg2")}
        f3.update({k: row("L3_ffn", f"L3_ffn_{k}") for k in ("bo", "bg2")})
        f3["bg1"] = column("L3_ffn", "L3_ffn_bg1")
        start_loads(nc, g)
        turned_attention(nc, g, "L2a", MASKED, w2, ["L2_xattn"])
        lora_ffn(nc, g, f2)
        gated_attention(nc, g, a3, a["ctx_1024"])
        expert_gates(nc, g, f3)
        attention(nc, g, "L3f", MIXED, f3, None, ["L3_ffn"])
        finish(nc, g, out)


def turned_attention(nc, g, name, kind, w, needs):
    with ExitStack() as ctx:
        t, jobs = dict(w), []
        for k in ("Wq", "Wk", "Wv", "Wo"):
            t[k] = ctx.enter_context(nc.sbuf_tensor(f"{name}_{k}T", [P, DC, D], F32))[:, :, :]
            jobs += [(w[k][:, m, c * P:c * P + P], t[k][:, c, m * P:m * P + P]) for m in range(DC) for c in range(DC)]
        attention(nc, g, name, kind, t, jobs, needs)


_INS = ['x', 'ctx_1024', 'mask_1x1xSxS2_bk0'] + [f'L{n}_xattn_{k}' for n in range(3) for k in (
    'Wq', 'bq', 'Wk', 'bk', 'Wv', 'bv', 'Wo', 'bo')] + [f'L0_ffn_{k}' for k in (
        'clip_x', 'clip_down', 'w_gate', 'w_up', 'w_down')] + [f'L1_ffn_{k}' for k in ('w1', 'b1', 'w2', 'b2')] + [
    f'L2_ffn_{k}' for k in ('wi', 'bi', 'wo', 'bo', 'lora_A', 'lora_B', 'gate_w', 'gate_b')] + [
    f'L3_xattn_{k}' for k in ('q_w', 'k_w', 'norm_w', 'gate_w', 'gate_b')] + [f'L3_ffn_{k}' for k in (
        'Wq', 'bq', 'Wk', 'bk', 'Wv', 'bv', 'Wg1', 'bg1', 'Wg2', 'bg2', 'Wo', 'bo')]


def kernel(**inputs):
    import numpy as np
    import concourse.bacc as bacc
    from concourse.bass_utils import run_bass_kernel_spmd

    nc = bacc.Bacc("TRN2", target_bir_lowering=False, num_devices=1)
    arrays, aps = {}, {}
    for name in _INS:
        x = np.ascontiguousarray(inputs[name])
        arrays[f"in_{name}"] = x
        aps[name] = nc.dram_tensor(f"in_{name}", x.shape, mybir.dt.from_np(x.dtype), kind="ExternalInput").ap()
    out = nc.dram_tensor("out", (NB, P, D), F32, kind="ExternalOutput").ap()
    program(nc, aps, out)
    r = run_bass_kernel_spmd(nc, [arrays], core_ids=[0])
    return r.results[0]["out"]
```

```python
from contextlib import ExitStack

import concourse.bass as bass
from concourse import mybir

F32 = mybir.dt.float32
BF16 = mybir.dt.bfloat16
U8 = mybir.dt.uint8
I32 = mybir.dt.int32
ALU = mybir.AluOpType
ACT = mybir.ActivationFunctionType
AX = mybir.AxisListType

P = 128
NB = 16
D = 256
DC = D // P
NH = 16
DH = D // NH
HC = NH // DC
NQ = 4
HQ = NH // NQ
NS = 2
TURNS = NB // NS
BANK = 512
LN_EPS = 1e-5
BIG = 3.0e38
MAGIC = 1.5 * 2.0 ** 23
HIDDEN = -2.0 ** 100
KEEP = int(P * 0.9)
NDROP = P - KEEP
PADS = 64


class Section:

    def __init__(self, nc, name):
        self.nc, self.name, self.ctx, self.sems = nc, name, ExitStack(), []

    def __enter__(self):
        return self

    def sb(self, name, shape, dt=F32):
        return self.ctx.enter_context(self.nc.sbuf_tensor(f"{self.name}_{name}", shape, dt))

    def ps(self, name, shape, dt=F32):
        return self.ctx.enter_context(self.nc.psum_tensor(f"{self.name}_{name}", shape, dt))

    def sem(self, name):
        s = self.nc.alloc_semaphore(f"{self.name}_{name}")
        self.sems.append(s)
        return s

    def per_stream(self, name):
        return [self.sem(f"{name}{s}") for s in range(NS)]

    def block(self):
        return self.nc.Block()

    def __exit__(self, *exc):
        self.ctx.__exit__(*exc)
        if exc[0] is None and self.sems:
            self.nc.clear_and_free_semaphores(self.sems)
            self.nc.all_engine_barrier()
        return False


def arrived(eng, g, *groups):
    for what in groups:
        eng.wait_ge(g.loaded[what], 16 * g.counts[what])


def apart(dve, g):
    g.pads += 1
    n = g.pads % PADS
    dve.memset(g.pad[0:1, n:n + 1], 0.0)


class Turned:

    def __init__(self, sec, banks, lots):
        self.banks, self.lots = banks, lots
        self.ps, self.sb = sec.sem("turned_ps"), sec.sem("turned_sb")

    def tensor(self, pe, ident):
        for n, (sources, _) in enumerate(self.lots):
            if n >= 2:
                pe.wait_ge(self.sb, n - 1)
            for m, src in enumerate(sources):
                rows, cols = src.shape[0], src.shape[1]
                mm = pe.transpose(self.banks[n % 2][0:cols, m * P:m * P + rows], src, ident[0:rows, 0:rows])
            mm.then_inc(self.ps, 1)

    def scalar(self, act):
        for n, (sources, dst) in enumerate(self.lots):
            act.wait_ge(self.ps, n + 1)
            rows = sources[0].shape[0]
            ps = self.banks[n % 2][:, :].rearrange("p (m r) -> p m r", r=P)
            act.copy(dst, ps[:, 0:len(sources), 0:rows]).then_inc(self.sb, 1)

    def wait(self, eng):
        eng.wait_ge(self.sb, len(self.lots))


def square_lot(src, dst):
    return ([src[:, m, c * P:c * P + P] for c in range(DC) for m in range(DC)],
            dst[:, :, :].rearrange("p c (m n) -> p (c m) n", n=P))


class LayerNorm:

    def __init__(self, sec, g):
        self.g = g
        self.std, self.t1, self.t2 = sec.sb("ln_std", [P, NB]), sec.sb("ln_t1", [P, NB]), sec.sb("ln_t2", [P, NB])
        self.r0, self.rstd = sec.sb("ln_r0", [P, NB]), sec.sb("ln_rstd", [P, NB, 1])
        self.mv = sec.sb("ln_mv", [P, NB, 2])
        self.xn = [sec.sb(f"xn{s}", [P, D]) for s in range(NS)]
        self.s_aggr, self.s_std, self.s_step = sec.sem("ln_aggr"), sec.sem("ln_std"), sec.sem("ln_step")
        self.s_xn = sec.per_stream("xn")

    def vector_start(self, dve):
        for b in range(NB):
            ins = dve.bn_aggr(self.mv[:, b, :], self.g.stats[:, b, :])
        ins.then_inc(self.s_aggr, 1)
        var = self.mv[:, :, 1]
        dve.wait_ge(self.s_std, 1)
        dve.reciprocal(self.r0[:, :], self.std[:, :]).then_inc(self.s_step, 1)
        dve.wait_ge(self.s_step, 1)
        dve.scalar_tensor_tensor(out=self.t1[:, :], in0=var, scalar=LN_EPS, in1=self.r0[:, :], op0=ALU.add,
                                 op1=ALU.mult).then_inc(self.s_step, 1)
        dve.wait_ge(self.s_step, 2)
        dve.scalar_tensor_tensor(out=self.t2[:, :], in0=self.t1[:, :], scalar=-0.5, in1=self.r0[:, :],
                                 op0=ALU.mult, op1=ALU.mult).then_inc(self.s_step, 1)
        dve.wait_ge(self.s_step, 3)
        dve.scalar_tensor_tensor(out=self.rstd[:, :, 0], in0=self.t2[:, :], scalar=1.5, in1=self.r0[:, :],
                                 op0=ALU.add, op1=ALU.mult).then_inc(self.s_step, 1)
        dve.wait_ge(self.s_step, 4)

    def scalar_start(self, act):
        act.wait_ge(self.s_aggr, 1)
        act.activation(self.std[:, :], self.mv[:, :, 1], ACT.Sqrt, bias=self.g.eps[:, 0:1]).then_inc(self.s_std, 1)

    def vector_norm(self, dve, s, b):
        dve.tensor_scalar(self.xn[s][:, :], self.g.x[:, b, :], self.mv[:, b, 0:1], self.rstd[:, b, :],
                          ALU.subtract, ALU.mult).then_inc(self.s_xn[s], 1)


class Rsqrt:
    STEPS = 12

    def __init__(self, sec, name, width):
        self.v, self.t, self.y = (sec.sb(f"{name}_{n}", [P, width]) for n in ("v", "t", "y"))
        self.u = sec.sb(f"{name}_u", [P, width])
        self.j = sec.sb(f"{name}_j", [P, width], I32)
        self.s = sec.sem(f"{name}_step")

    def vector(self, dve, src, scale, eps, i):
        n = Rsqrt.STEPS * (i - 1)

        def link(k, ins):
            ins.then_inc(self.s, 1)
            dve.wait_ge(self.s, n + k)
        v, t, u, y, j = self.v[:, :], self.t[:, :], self.u[:, :], self.y[:, :], self.j[:, :]
        link(1, dve.tensor_scalar(v, src, scale, eps, ALU.mult, ALU.add))
        link(2, dve.tensor_scalar(j, v.bitcast(I32), 1, None, ALU.arith_shift_right))
        link(3, dve.tensor_scalar(y.bitcast(I32), j, -1.0, float(0x5F3759DF), ALU.mult, ALU.add))
        for k in (4, 7, 10):
            link(k, dve.tensor_tensor(t, v, y, ALU.mult))
            link(k + 1, dve.scalar_tensor_tensor(out=u, in0=t, scalar=-0.5, in1=y, op0=ALU.mult, op1=ALU.mult))
            link(k + 2, dve.scalar_tensor_tensor(out=y, in0=u, scalar=1.5, in1=y, op0=ALU.add, op1=ALU.mult))
        return y


class Pair:

    def __init__(self, first, v):
        self.first, self.v = first, v
        self.pair = bass.ds(first, NS)

    def b(self, s):
        return self.first + s


def sweep_pairs(eng, step):
    pairs = [Pair(NS * n, n + 1) for n in range(TURNS)]
    step(None, None, pairs[0])
    step(None, pairs[0], pairs[1])
    with eng.Fori(1, TURNS - 1) as i:
        step(*(Pair(NS * (i + n), eng.snap(i + n + 1) if n >= 0 else i) for n in (-1, 0, 1)))
    step(pairs[-2], pairs[-1], None)
    step(pairs[-1], None, None)


def banks_of(sec):
    return [[sec.ps(f"bank{s}_{n}", [P, BANK]) for n in range(4)] for s in range(NS)]


class Globals:
    pass


def setup(nc, g, a, loads):
    sec = Section(nc, "setup")
    with sec:
        ctx_nat = sec.sb("ctx_nat", [P, NB, D])
        banks = banks_of(sec)
        s_const, s_zero = sec.sem("const"), sec.sem("zero")
        s_ps, s_sb = sec.sem("ctx_ps"), sec.sem("ctx_sb")
        s_ctx = sec.sem("ctx_in")
        flat = [banks[s][n] for n in range(4) for s in range(NS)]
        with sec.block() as block:
            @block.sync
            def _(sp):
                for q in range(4):
                    sp.dma_start(ctx_nat[:, 4 * q:4 * q + 4, :],
                                 a["ctx_1024"][4 * q:4 * q + 4].rearrange("b p d -> p b d")).then_inc(s_ctx, 16)
                sp.dma_start(g.x[:, :, :], a["x"].rearrange("b p d -> p b d")).then_inc(g.loaded["x"], 16)
                for dst, src, what in loads:
                    sp.dma_start(dst, src, allow_slow_non_contiguous=True).then_inc(g.loaded[what], 16)
                sp.wait_ge(g.loaded["x"], 16)

            @block.gpsimd
            def _(pool):
                pool.memset(g.ident[:, :], 0.0).then_inc(s_zero, 1)
                pool.memset(g.hmask[:, :], 1.0).then_inc(s_zero, 1)
                pool.memset(g.causal[:, :, :], 0.0).then_inc(s_zero, 1)
                pool.wait_ge(s_zero, 3)
                pool.affine_select(out=g.ident[:, :], in_=g.ident[:, :], compare_op=ALU.not_equal, fill=1.0,
                                   base=0, pattern=[[-1, P]], channel_multiplier=1).then_inc(s_const, 1)
                pool.affine_select(out=g.hmask[:, :], in_=g.hmask[:, :], compare_op=ALU.is_ge, fill=0.0,
                                   base=0, pattern=[[-DH, HC]], channel_multiplier=1).then_inc(s_zero, 1)
                pool.wait_ge(s_zero, 4)
                pool.affine_select(out=g.hmask[:, :], in_=g.hmask[:, :], compare_op=ALU.is_ge, fill=0.0,
                                   base=DH - 1, pattern=[[DH, HC]], channel_multiplier=-1).then_inc(s_const, 1)
                pool.affine_select(out=g.causal[:, 0, :], in_=g.causal[:, 0, :], compare_op=ALU.is_ge, fill=-BIG,
                                   base=0, pattern=[[-1, P]], channel_multiplier=1).then_inc(s_const, 1)

            @block.vector
            def _(dve):
                dve.memset(g.eps[:, :], LN_EPS).then_inc(s_const, 1)
                dve.memset(g.onesP[:, :], 1.0).then_inc(s_const, 1)
                dve.memset(g.magic[:, :], MAGIC).then_inc(s_const, 1)
                for e in range(8):
                    dve.memset(g.order[:, e:e + 1], 8.0 - e)
                dve.memset(g.nmagic[:, :], -MAGIC)
                dve.wait_ge(s_const, 6)
                dve.tensor_copy(g.identb[:, :], g.ident[:, :])
                for n in range(1, NB, 2):
                    if n == 9:
                        dve.wait_ge(g.loaded["x"], 16)
                        for b in range(NB):
                            dve.bn_stats(g.stats[:, b, :], g.x[:, b, :])
                    dve.wait_ge(s_ps, n + 1)
                    dve.tensor_copy(g.ctxT[:, n, :, :], flat[n % 8][:, 0:D]
                                    .rearrange("p (c t) -> p c t", c=DC)).then_inc(s_sb, 1)
                arrived(dve, g, "mask")
                dve.tensor_scalar(g.hidden[:, :], g.mask, 0.0, HIDDEN, ALU.is_equal, ALU.mult)

            @block.scalar
            def _(act):
                for n in range(0, NB, 2):
                    act.wait_ge(s_ps, n + 1)
                    act.copy(g.ctxT[:, n, :, :], flat[n % 8][:, 0:D]
                             .rearrange("p (c t) -> p c t", c=DC)).then_inc(s_sb, 1)

            @block.tensor
            def _(pe):
                pe.wait_ge(s_const, 6)
                for n in range(NB):
                    if n % 4 == 0:
                        pe.wait_ge(s_ctx, 16 * NB // 4)
                    if n == 8:
                        pe.wait_ge(s_sb, 8)
                    for c in range(DC):
                        mm = pe.transpose(flat[n % 8][:, c * P:c * P + P], ctx_nat[:, n, c * P:c * P + P],
                                          g.ident[:, :])
                    mm.then_inc(s_ps, 1)


class Seq:

    def __init__(self, b, s, v, nth, earlier):
        self.b, self.s, self.v, self.nth, self.earlier = b, s, v, nth, earlier


class FixedStep:

    def __init__(self, b, count):
        self.b, self.count = b, count

    def at(self, k):
        b = self.b + k
        if not 0 <= b < self.count:
            return None
        return Seq(b, b % 2, b // 2 + 1, lambda t: NQ * (b // 2) + 1 + t, lambda n: self.at(k - n))


class LoopStep:

    def __init__(self, eng, i, odd, known):
        self.eng, self.i, self.odd, self.known = eng, i, odd, known

    def snap(self, factor, plus):
        if (factor, plus) == (1, 0):
            return self.i
        if (factor, plus) not in self.known:
            self.known[factor, plus] = self.eng.snap(factor * self.i + plus)
        return self.known[factor, plus]

    def at(self, k):
        n = self.odd + k
        half = n // 2
        return Seq(2 * self.i + n, n % 2, self.snap(1, half + 1), lambda t: self.snap(NQ, NQ * half + 1 + t),
                   lambda m: self.at(k - m))


def sweep(eng, step, ahead=2, behind=2, count=NB):
    first = max(ahead, behind + 1)
    last = count - first
    for b in range(-ahead, first):
        step(FixedStep(b, count))
    with eng.Fori(1, (last - first) // 2 + 1) as i:
        known = {}
        for odd in range(first - 2, first):
            step(LoopStep(eng, i, odd, known))
    for b in range(last, count + behind):
        step(FixedStep(b, count))


PLAIN, PRUNED, MASKED, MIXED = range(4)


def attention(nc, g, name, kind, w, turned, needs, later=()):
    sec = Section(nc, name)
    LAG = 2 if kind == PRUNED else 1
    with sec:
        ln = LayerNorm(sec, g)
        S = [sec.ps(f"scores{n}", [P, BANK]) for n in range(2)]
        T = [sec.ps(f"probsT{n}", [P, BANK]) for n in range(2)]
        F = [sec.ps(f"projected{n}", [P, BANK]) for n in range(2)]
        OB, C = sec.ps("values", [P, BANK]), sec.ps("other", [P, BANK])
        Y = OB if kind == PRUNED else C
        O = OB[:, 0:NH * (DH + 1)].rearrange("p (h e) -> p h e", h=NH)
        two = lambda ps: ps[:, 0:D].rearrange("p (c t) -> p c t", c=DC)
        heads = lambda ap: ap.rearrange("p (h e) -> p h e", h=NH)
        sbs = lambda nm, shape, dt=F32: [sec.sb(f"{nm}{s}", shape, dt) for s in range(2)]
        xT, ctxT, qT, kT = (sbs(n, [P, DC, P]) for n in ("xT", "ctxT", "qT", "kT"))
        v = sbs("v", [P, NH, DH + 1])
        kbd = sbs("kbd", [P, DC, HC, P])
        pr = sec.sb("pr", [P, NQ, HQ, P])
        prT = sbs("prT", [P, NQ, HQ, P])
        mx, rl = sbs("mx", [P, NH]), sbs("rl", [P, NH])
        on, oT = sbs("on", [P, NH, DH]), sbs("oT", [P, DC, P])
        (s_ctx, s_xT_ps, s_xT, s_q_ps, s_k_ps, s_v_ps, s_q, s_k, s_v, s_kbd, s_sc, s_mx, s_sh, s_ex, s_tp,
         s_pt, s_av, s_rl, s_on, s_oT_ps, s_oT, s_y, s_bo, s_x) = (sec.per_stream(n) for n in (
             "ctx_loaded", "xT_ps", "xT", "q_ps", "k_ps", "v_ps", "q", "k", "v", "kbd", "scores", "max",
             "shifted", "exp", "probsT_ps", "probsT", "av", "recip", "out", "outT_ps", "outT", "y",
             "bo_added", "x_done"))
        s_one = sec.sem("ones_set")
        turn_w = Turned(sec, S, turned) if turned else None
        if kind == PRUNED:
            vp = sbs("vp", [P, NH, DH + 1])
            ls, rls = sbs("ls", [P, NH]), sbs("rls", [P, NH])
            cs, keepT = sbs("cs", [P, NH]), sbs("keepT", [P, NH])
            cst, cst2 = sbs("cst", [NH, P]), sbs("cst2", [NH, P])
            m8 = sbs("m8", [NH, 2, 8])
            s_rls, s_cs, s_csT, s_ct, s_m1, s_r1, s_m2, s_fill, s_r2, s_keep, s_kT, s_kTs, s_vp = (
                sec.per_stream(n) for n in ("rowrecip", "colsum", "colsumT_ps", "colsumT",
                                            "least8", "drop8", "least16", "fill", "drop13", "keep", "keepT_ps",
                                            "keepT", "v_pruned"))
            colsum, CT, KT = C[:, 0:NH], F[0][0:NH, D:D + P], OB[:, 0:NH]
            val = vp
        else:
            val = v
        if kind == MIXED:
            mix, mix1 = sbs("mix", [P, g.mixw]), sec.sb("mixed_more", [P, g.mixw])
            s_share, s_more, s_mixed = ([sec.per_stream(f"{nm}{n}_") for n in range(2)] for nm in (
                "share", "share_more", "mixed"))
            lots = (slice(0, g.mixk), slice(g.mixk, g.mixw))

        def weights(s):
            if kind != MIXED:
                return w
            m = mix[s]
            q = {n: m[:, at:at + DC * D].rearrange("p (c n) -> p c n", c=DC) for n, at in g.mixed_at.items()
                 if n[0] == "W"}
            at = g.mixed_at
            q.update(bq=m[:, at["bq"]:at["bq"] + DC], bk=m[:, at["bk"]:at["bk"] + DC], bv=m[:, at["bv"]:at["bv"] + D])
            return q

        kv = xT if kind == MIXED else ctxT
        with sec.block() as block:
            @block.sync
            def _(sp):
                def step(st):
                    new, cur = st.at(2), st.at(0)
                    if new:
                        if cur:
                            sp.wait_ge(s_v_ps[cur.s], cur.v)
                        sp.dma_start(ctxT[new.s][:, :, :], g.ctxT[:, new.b, :, :]).then_inc(s_ctx[new.s], 16)
                if kind != MIXED and not later:
                    sweep(sp, step)
                elif later:
                    share = -(-len(later) // NB)
                    for b in range(-2, NB - 2):
                        step(FixedStep(b, NB))
                        for dst, src, what in later[(b + 2) * share:(b + 3) * share]:
                            sp.dma_start(dst, src, allow_slow_non_contiguous=True).then_inc(g.loaded[what], 16)

            @block.gpsimd
            def _(pool):
                arrived(pool, g, *needs)
                for s in range(2):
                    pool.memset(v[s][:, :, :], 1.0).then_inc(s_one, 1)
                    if kind == PRUNED:
                        pool.memset(vp[s][:, :, :], 1.0).then_inc(s_one, 1)

                def step(st):
                    nxt, new = st.at(1), st.at(2)
                    if nxt:
                        s = nxt.s
                        pool.wait_ge(s_k[s], nxt.v)
                        for c in range(DC):
                            pool.tensor_tensor(
                                kbd[s][:, c, :, :], kT[s][:, c, :].unsqueeze(1).to_broadcast([P, HC, P]),
                                g.hmask[:, :].unsqueeze(2).to_broadcast([P, HC, P]), ALU.mult).then_inc(s_kbd[s], 1)
                    if new and kind == MIXED:
                        for n in range(2):
                            pool.wait_ge(s_more[n][new.s], new.v)
                        for n, lot in enumerate(lots):
                            pool.tensor_tensor(mix[new.s][:, lot], mix[new.s][:, lot], mix1[:, lot], ALU.add
                                               ).then_inc(s_mixed[n][new.s], 1)
                    if nxt:
                        pool.wait_ge(ln.s_xn[s], nxt.v)
                        pool.tensor_tensor(g.x[:, nxt.b, :], g.x[:, nxt.b, :], w["bo"], ALU.add
                                           ).then_inc(s_bo[s], 1)
                sweep(pool, step)

            @block.tensor
            def _(pe):
                arrived(pe, g, *needs)
                if turn_w:
                    turn_w.tensor(pe, g.ident)
                    turn_w.wait(pe)
                pe.wait_ge(s_one, 4 if kind == PRUNED else 2)

                def turn_x(q):
                    pe.wait_ge(ln.s_xn[q.s], q.v)
                    before = q.earlier(1)
                    if before:
                        pe.wait_ge(s_q[before.s], before.v)
                    for c in range(DC):
                        mm = pe.transpose(F[0][:, c * P:c * P + P], ln.xn[q.s][:, c * P:c * P + P], g.ident[:, :])
                    mm.then_inc(s_xT_ps[q.s], 1)

                def project(out, W, inp):
                    for m in range(DC):
                        for c in range(DC):
                            mm = pe.matmul(out[:, m * P:m * P + P], W[:, c, m * P:m * P + P], inp[:, c, :],
                                           start=(c == 0), stop=(c == DC - 1))
                    return mm

                def project_k(q):
                    before = q.earlier(1)
                    if before:
                        pe.wait_ge(s_v[before.s], before.v)
                    if kind == MIXED:
                        pe.wait_ge(s_mixed[0][q.s], q.v)
                        pe.wait_ge(s_xT[q.s], q.v)
                    else:
                        pe.wait_ge(s_ctx[q.s], 16 * q.v)
                    project(F[1], weights(q.s)["Wk"], kv[q.s]).then_inc(s_k_ps[q.s], 1)

                def project_q(q):
                    pe.wait_ge(s_xT[q.s], q.v)
                    if kind == MIXED:
                        pe.wait_ge(s_mixed[1][q.s], q.v)
                    project(F[0], weights(q.s)["Wq"], xT[q.s]).then_inc(s_q_ps[q.s], 1)

                def project_v(q):
                    pe.wait_ge(s_k[q.s], q.v)
                    for c in range(DC):
                        mm = pe.matmul(F[1][:, 0:D], kv[q.s][:, c, :], weights(q.s)["Wv"][:, c, :],
                                       start=(c == 0), stop=(c == DC - 1))
                    mm.then_inc(s_v_ps[q.s], 1)

                def scores(q, t):
                    c, h = t * HQ // HC, t * HQ % HC
                    if t == 0:
                        pe.wait_ge(s_q[q.s], q.v)
                    if h == 0:
                        pe.wait_ge(s_kbd[q.s], DC * q.v - DC + 1 + c)
                    last = q if t >= 2 else q.earlier(1)
                    if last:
                        pe.wait_ge(s_sh[last.s], last.nth((t - 2) % NQ))
                    mm = pe.matmul(S[t % 2][:, :], qT[q.s][:, c, :], kbd[q.s][:, c, h:h + HQ, :], start=True,
                                   stop=(kind != MASKED))
                    if kind == MASKED:
                        mm = pe.matmul(S[t % 2][:, :], g.identb[:, :],
                                       g.hidden[:, :].unsqueeze(1).to_broadcast([P, HQ, P]), start=False, stop=True)
                    mm.then_inc(s_sc[q.s], 1)

                def turn_probs(q, t):
                    before = q.earlier(1)
                    pe.wait_ge(s_ex[q.s], q.nth(t))
                    if kind == PRUNED:
                        pe.wait_ge(s_rls[q.s], q.nth(t))
                        if t == 0 and before:
                            pe.wait_ge(s_cs[before.s], before.v)
                        for h in range(HQ):
                            n = t * HQ + h
                            pe.matmul(colsum[:, n:n + 1], pr[:, t, h, :], rls[q.s][:, n:n + 1], start=True, stop=True)
                    last = q if t >= 2 else before
                    if last:
                        pe.wait_ge(s_pt[last.s], last.nth((t - 2) % NQ))
                    for h in range(HQ):
                        mm = pe.transpose(T[t % 2][:, h * P:h * P + P], pr[:, t, h, :], g.ident[:, :])
                    mm.then_inc(s_tp[q.s], 1)

                def values(q, t):
                    before = q.earlier(1)
                    pe.wait_ge(s_pt[q.s], q.nth(t))
                    if t == 0:
                        if kind == PRUNED:
                            pe.wait_ge(s_vp[q.s], q.v)
                        else:
                            pe.wait_ge(s_v[q.s], q.v)
                        if before:
                            done = s_x if kind == PRUNED else s_on
                            pe.wait_ge(done[before.s], before.v)
                    for h in range(t * HQ, t * HQ + HQ):
                        mm = pe.matmul(O[:, h, :], prT[q.s][:, t, h % HQ, :], val[q.s][:, h, :], start=True,
                                       stop=True)
                    if t == NQ - 1:
                        mm.then_inc(s_av[q.s], 1)

                def turn_out(q):
                    pe.wait_ge(s_on[q.s], q.v)
                    before = q.earlier(1)
                    if before:
                        pe.wait_ge(s_x[before.s], before.v)
                    for c in range(DC):
                        mm = pe.transpose(Y[:, c * P:c * P + P],
                                          on[q.s][:, c * HC:(c + 1) * HC, :].rearrange("p h e -> p (h e)"),
                                          g.ident[:, :])
                    mm.then_inc(s_oT_ps[q.s], 1)

                def project_out(q):
                    pe.wait_ge(s_oT[q.s], q.v)
                    for c in range(DC):
                        mm = pe.matmul(Y[:, D:2 * D], oT[q.s][:, c, :], w["Wo"][:, c, :], start=(c == 0),
                                       stop=(c == DC - 1))
                    mm.then_inc(s_y[q.s], 1)

                def turn_sums(q):
                    pe.wait_ge(s_cs[q.s], q.v)
                    pe.transpose(CT, cs[q.s][:, :], g.ident[:, :]).then_inc(s_csT[q.s], 1)

                def turn_kept(q):
                    pe.wait_ge(s_keep[q.s], q.v)
                    pe.matmul(KT, cst2[q.s][:, :], g.ident[0:NH, 0:NH], start=True, stop=True).then_inc(s_kT[q.s], 1)

                def step(st):
                    cur, prev, nxt, new, last = st.at(0), st.at(-1), st.at(1), st.at(2), st.at(-LAG)

                    def piece(q, work, *args):
                        if q:
                            work(q, *args)

                    if kind == PRUNED:
                        piece(cur, scores, 0)
                        piece(last, values, 0)
                        piece(last, values, 1)
                        piece(nxt, project_k)
                        piece(prev, turn_probs, 3)
                        piece(cur, scores, 1)
                        piece(last, values, 2)
                        piece(last, values, 3)
                        piece(nxt, project_q)
                        piece(prev, turn_sums)
                        piece(cur, turn_probs, 0)
                        piece(cur, scores, 2)
                        piece(last, turn_out)
                        piece(nxt, project_v)
                        piece(cur, turn_probs, 1)
                        piece(cur, scores, 3)
                        piece(new, turn_x)
                        piece(last, project_out)
                        piece(prev, turn_kept)
                        piece(cur, turn_probs, 2)
                    else:
                        piece(cur, scores, 0)
                        piece(cur, scores, 1)
                        piece(prev, values, 2)
                        piece(nxt, project_k)
                        piece(prev, values, 3)
                        piece(cur, turn_probs, 0)
                        piece(cur, scores, 2)
                        piece(cur, scores, 3)
                        piece(nxt, project_q)
                        piece(cur, turn_probs, 1)
                        piece(cur, values, 0)
                        piece(last, turn_out)
                        piece(nxt, project_v)
                        piece(cur, turn_probs, 2)
                        piece(new, turn_x)
                        piece(last, project_out)
                        piece(cur, values, 1)
                        piece(cur, turn_probs, 3)
                sweep(pe, step)

            @block.scalar
            def _(act):
                ln.scalar_start(act)
                if turn_w:
                    turn_w.scalar(act)

                def copy_probs(q, t):
                    act.wait_ge(s_tp[q.s], q.nth(t))
                    act.copy(prT[q.s][:, t, :, :], T[t % 2][:, :].rearrange("p (h k) -> p h k", h=HQ)
                             ).then_inc(s_pt[q.s], 1)

                def exp(q, t):
                    act.wait_ge(s_sh[q.s], q.nth(t))
                    if kind == PRUNED:
                        for h in range(HQ):
                            n = t * HQ + h
                            ex = act.activation(pr[:, t, h, :], pr[:, t, h, :], ACT.Exp, scale=DH ** -0.5,
                                                accum_out=ls[q.s][:, n:n + 1])
                    else:
                        ex = act.activation(pr[:, t, :, :], pr[:, t, :, :], ACT.Exp, scale=DH ** -0.5)
                    ex.then_inc(s_ex[q.s], 1)

                def copy_out(q):
                    act.wait_ge(s_oT_ps[q.s], q.v)
                    act.copy(oT[q.s][:, :, :], two(Y)).then_inc(s_oT[q.s], 1)

                def copy_x(q):
                    act.wait_ge(s_xT_ps[q.s], q.v)
                    act.copy(xT[q.s][:, :, :], two(F[0])).then_inc(s_xT[q.s], 1)

                def share(q, e):
                    act.activation((mix[q.s], mix1)[e][:, :], g.experts[:, e, :], ACT.Copy,
                                   scale=g.gates[:, q.b, e, :]).then_inc(s_share[e][q.s], 1)

                def step(st):
                    cur, prev, nxt, new, last = st.at(0), st.at(-1), st.at(1), st.at(2), st.at(-LAG)
                    if kind == PRUNED:
                        for t in range(NQ):
                            if t == 2 and last:
                                copy_out(last)
                            if t == 3 and new:
                                copy_x(new)
                            if cur:
                                exp(cur, t)
                            before = cur if t else prev
                            if before:
                                copy_probs(before, (t - 1) % NQ)
                    else:
                        if prev:
                            copy_probs(prev, NQ - 1)
                        if kind == MIXED and new:
                            if cur:
                                act.wait_ge(s_v[cur.s], cur.v)
                            share(new, 0)
                        if cur:
                            exp(cur, 0)
                            exp(cur, 1)
                            copy_probs(cur, 0)
                        if kind == MIXED and new:
                            if nxt:
                                act.wait_ge(s_mixed[1][nxt.s], nxt.v)
                            share(new, 1)
                        if cur:
                            copy_probs(cur, 1)
                        if last:
                            copy_out(last)
                        if cur:
                            exp(cur, 2)
                            exp(cur, 3)
                            copy_probs(cur, 2)
                        if new:
                            copy_x(new)
                sweep(act, step)

            @block.vector
            def _(dve):
                arrived(dve, g, *needs)
                dve.wait_ge(s_one, 4 if kind == PRUNED else 2)
                ln.vector_start(dve)

                def soft(q, t, last_group=(None, 0)):
                    s, before = q.s, q.earlier(1)
                    sc = S[t % 2][:, :].rearrange("p (h k) -> p h k", h=HQ)
                    m4 = mx[s][:, t * HQ:t * HQ + HQ]
                    dve.wait_ge(s_sc[s], q.nth(t))
                    dve.tensor_reduce(m4, sc, AX.X, ALU.max).then_inc(s_mx[s], 1)
                    if last_group[0]:
                        row_factors(*last_group)
                    if before:
                        dve.wait_ge(s_tp[before.s], before.nth(t))
                    dve.wait_ge(s_mx[s], q.nth(t))
                    dve.tensor_tensor(pr[:, t, :, :], sc, m4.unsqueeze(2).to_broadcast([P, HQ, P]),
                                      ALU.subtract).then_inc(s_sh[s], 1)

                def row_factors(q, t):
                    s, l4 = q.s, slice(t * HQ, t * HQ + HQ)
                    dve.wait_ge(s_ex[s], q.nth(t))
                    dve.reciprocal(rls[s][:, l4], ls[s][:, l4]).then_inc(s_rls[s], 1)

                def add_k(q):
                    dve.wait_ge(s_k_ps[q.s], q.v)
                    dve.tensor_tensor(kT[q.s][:, :, :], two(F[1]),
                                      weights(q.s)["bk"].unsqueeze(2).to_broadcast([P, DC, P]), ALU.add
                                      ).then_inc(s_k[q.s], 1)

                def add_q(q):
                    dve.wait_ge(s_q_ps[q.s], q.v)
                    dve.tensor_tensor(qT[q.s][:, :, :], two(F[0]),
                                      weights(q.s)["bq"].unsqueeze(2).to_broadcast([P, DC, P]), ALU.add
                                      ).then_inc(s_q[q.s], 1)

                def add_v(q):
                    dve.wait_ge(s_v_ps[q.s], q.v)
                    dve.tensor_tensor(v[q.s][:, :, 0:DH], heads(F[1][:, 0:D]), heads(weights(q.s)["bv"]), ALU.add
                                      ).then_inc(s_v[q.s], 1)

                def drop_keys(q):
                    s = q.s
                    apart(dve, g)
                    dve.max(m8[s][:, 0, :], cst[s][:, :]).then_inc(s_m1[s], 1)
                    dve.wait_ge(s_m1[s], q.v)
                    apart(dve, g)
                    dve.match_replace(cst2[s][:, :], m8[s][:, 0, :], cst[s][:, :], -BIG).then_inc(s_r1[s], 1)
                    dve.wait_ge(s_r1[s], q.v)
                    apart(dve, g)
                    dve.max(m8[s][:, 1, :], cst2[s][:, :]).then_inc(s_m2[s], 1)
                    dve.wait_ge(s_m2[s], q.v)
                    apart(dve, g)
                    dve.tensor_scalar(m8[s][:, 1, NDROP - 8:8], m8[s][:, 1, NDROP - 8:8], 0.0, -BIG,
                                      ALU.mult, ALU.add).then_inc(s_fill[s], 1)
                    dve.wait_ge(s_fill[s], q.v)
                    apart(dve, g)
                    dve.match_replace(cst[s][:, :], m8[s][:, 1, :], cst2[s][:, :], -BIG).then_inc(s_r2[s], 1)
                    dve.wait_ge(s_r2[s], q.v)
                    dve.tensor_scalar(cst2[s][:, ::-1], cst[s][:, :], -0.5 * BIG, None, ALU.is_gt
                                      ).then_inc(s_keep[s], 1)

                def keep_values(q):
                    s = q.s
                    dve.wait_ge(s_kT[s], q.v)
                    dve.tensor_copy(keepT[s][:, :], KT).then_inc(s_kTs[s], 1)
                    dve.wait_ge(s_kTs[s], q.v)
                    dve.tensor_tensor(vp[s][:, :, 0:DH], v[s][:, :, 0:DH],
                                      keepT[s][:, :].unsqueeze(2).to_broadcast([P, NH, DH]), ALU.mult
                                      ).then_inc(s_vp[s], 1)
                    dve.wait_ge(s_vp[s], q.v)

                def more(q, e):
                    to = (mix[q.s], mix1)[e][:, :]
                    dve.wait_ge(s_share[e][q.s], q.v)
                    dve.scalar_tensor_tensor(
                        out=to, in0=g.experts[:, e + 2, :], scalar=g.gates[:, q.b, e + 2, :], in1=to,
                        op0=ALU.mult, op1=ALU.add).then_inc(s_more[e][q.s], 1)

                def add_out(q):
                    s = q.s
                    dve.wait_ge(s_y[s], q.v)
                    dve.wait_ge(s_bo[s], q.v)
                    dve.tensor_tensor(g.x[:, q.b, :], Y[:, D:2 * D], g.x[:, q.b, :], ALU.add).then_inc(s_x[s], 1)
                    dve.wait_ge(s_x[s], q.v)
                    apart(dve, g)
                    dve.bn_stats(g.stats[:, q.b, :], g.x[:, q.b, :])

                def norm_out(q):
                    s = q.s
                    dve.wait_ge(s_av[s], q.v)
                    dve.reciprocal(rl[s][:, :], O[:, :, DH]).then_inc(s_rl[s], 1)
                    dve.wait_ge(s_rl[s], q.v)
                    dve.tensor_tensor(on[s][:, :, :], O[:, :, 0:DH], rl[s][:, :].unsqueeze(2).to_broadcast([P, NH, DH]),
                                      ALU.mult).then_inc(s_on[s], 1)

                def step(st):
                    cur, prev, nxt, new, last = st.at(0), st.at(-1), st.at(1), st.at(2), st.at(-LAG)
                    if kind == PRUNED:
                        for t in range(NQ):
                            if t == 1 and prev:
                                dve.wait_ge(s_tp[prev.s], prev.nth(NQ - 1))
                                dve.tensor_copy(cs[prev.s][:, :], colsum).then_inc(s_cs[prev.s], 1)
                            if t == 1 and nxt:
                                add_k(nxt)
                            if t == 2 and prev:
                                dve.wait_ge(s_csT[prev.s], prev.v)
                                dve.tensor_scalar(cst[prev.s][:, ::-1], CT, -1.0, None, ALU.mult
                                                  ).then_inc(s_ct[prev.s], 1)
                            if t == 2 and nxt:
                                add_q(nxt)
                            before = (cur, t - 1) if t else (prev, NQ - 1)
                            if cur:
                                soft(cur, t, before)
                            elif before[0]:
                                row_factors(*before)
                            if t == 1 and last:
                                norm_out(last)
                            if t == 2 and prev:
                                dve.wait_ge(s_ct[prev.s], prev.v)
                                drop_keys(prev)
                            if t == 2 and new:
                                ln.vector_norm(dve, new.s, new.b)
                        if prev:
                            keep_values(prev)
                    else:
                        if cur:
                            soft(cur, 0)
                            soft(cur, 1)
                        if nxt:
                            add_k(nxt)
                        if new:
                            ln.vector_norm(dve, new.s, new.b)
                        if last:
                            norm_out(last)
                        if kind == MIXED and new:
                            more(new, 0)
                        if cur:
                            soft(cur, 2)
                            soft(cur, 3)
                        if nxt:
                            add_q(nxt)
                        if kind == MIXED and new:
                            more(new, 1)
                    if nxt:
                        add_v(nxt)
                    if last:
                        add_out(last)
                sweep(dve, step)


QMAX = 127.0
F0 = 704
FC0 = -(-F0 // P)
TG = 4
NG = NB // TG


def rounded(eng, out, tmp, src, scalar, sem, n, clip=None):
    lo, hi = clip or (-128.0, 127.0)
    eng.tensor_scalar(tmp, src, scalar, MAGIC, ALU.mult, ALU.add).then_inc(sem, 1)
    eng.wait_ge(sem, n + 1)
    eng.tensor_scalar(tmp, tmp, MAGIC + hi, MAGIC + lo, ALU.min, ALU.max).then_inc(sem, 1)
    eng.wait_ge(sem, n + 2)
    eng.tensor_scalar(out, tmp, MAGIC, None, ALU.subtract).then_inc(sem, 1)
    eng.wait_ge(sem, n + 3)


class GlobalMax:

    def __init__(self, sec, name, bank):
        self.ps, self.one = bank, sec.sb(f"{name}_one", [1, 1])
        self.s_row, self.s_one, self.s_all = sec.sem(f"{name}_row"), sec.sem(f"{name}_one"), sec.sem(f"{name}_all")

    def tensor(self, pe, g, col, s_col, n):
        pe.wait_ge(s_col, n)
        pe.transpose(self.ps[0:1, 0:P], col, g.ident[:, :]).then_inc(self.s_row, 1)
        pe.wait_ge(self.s_one, 1)
        pe.matmul(self.ps[:, P:P + 1], g.onesP[0:1, :], self.one[:, :], start=True, stop=True
                  ).then_inc(self.s_all, 1)

    def vector(self, dve):
        dve.wait_ge(self.s_row, 1)
        dve.tensor_reduce(self.one[:, :], self.ps[0:1, 0:P], AX.X, ALU.max).then_inc(self.s_one, 1)
        dve.wait_ge(self.s_all, 1)
        return self.ps[:, P:P + 1]


def fake_quant_ffn(nc, g, w):
    sec = Section(nc, "L0f")
    with sec:
        ln = LayerNorm(sec, g)
        banks = [sec.ps(f"bank{n}", [P, BANK]) for n in range(8)]
        act_scale = sec.sb("act_scale", [P, 8])
        sg, su = (sec.sb(n, [P, FC0]) for n in ("gate_scale", "up_scale"))
        iw = [sec.sb(f"inv_{n}", [P, k]) for n, k in (("gate", FC0), ("up", FC0), ("down", DC))]
        sd, sd_row = sec.sb("down_scale", [P, DC]), sec.sb("down_row", [P, D])
        xqT = sec.sb("xqT", [P, DC, NB * P], BF16)
        wT = {n: sec.sb(f"{n}T", [P, DC, FC0 * P], BF16) for n in ("gate", "up")}
        wdT = sec.sb("downT", [P, FC0, D], BF16)
        amax, hmax = sec.sb("amax", [P, NG, 1]), sec.sb("hmax", [P, NG, FC0 // 3])
        gm1, gm2 = GlobalMax(sec, "xmax", banks[7]), GlobalMax(sec, "hmax", banks[7])
        s_sc, s_w, s_iw, s_w2, s_amax, s_col, s_xq = (sec.sem(n) for n in (
            "scales", "w_steps", "w_inverse", "w_scaled", "tile_amax", "amax_col", "xq_ready"))
        s_dr, s_t_ps, s_t_sb, s_row_ps = sec.sem("x_steps"), sec.sem("turned_ps"), sec.sem("turned_sb"), sec.sem("row_ps")
        half_col = sec.sb("amax_cols", [P, 2])
        with ExitStack() as early:
            xn_all = early.enter_context(nc.sbuf_tensor("L0f_xn_all", [P, NB, D], F32))
            lots = [([w[n][:, f + m, c * P:c * P + P] for m in range(3)], wT[n][:, c, f * P:(f + 3) * P])
                    for n in ("gate", "up") for f in range(0, FC0, 3) for c in range(DC)]
            lots += [([w["down"][:, c, (f + m) * P:(f + m + 1) * P] for m in range(3)],
                      wdT[:, f:f + 3, c * P:c * P + P]) for c in range(DC) for f in range(0, FC0, 3)]
            PL = 4
            with sec.block() as block:
                @block.tensor
                def _(pe):
                    for k, (sources, _) in enumerate(lots):
                        if k % PL == 0:
                            pe.wait_ge(s_w2, k // PL + 1)
                        if k >= 6:
                            pe.wait_ge(s_t_sb, k - 5)
                        for m, src in enumerate(sources):
                            mm = pe.transpose(banks[k % 6][:, m * P:m * P + P], src, g.ident[:, :])
                        mm.then_inc(s_t_ps, 1)
                    for c in range(DC):
                        mm = pe.matmul(banks[6][:, c * P:c * P + P], sd[:, c:c + 1].to_broadcast([P, P]),
                                       g.ident[:, :], start=True, stop=True)
                    mm.then_inc(s_row_ps, 1)
                    gm1.tensor(pe, g, half_col[:, 0:1], s_col, 1)
                    for t in range(NB // 2):
                        k = len(lots) + t
                        pe.wait_ge(s_xq, t // 2 + 1)
                        pe.wait_ge(s_t_sb, k - 5)
                        for m in range(4):
                            b, c = 2 * t + m // 2, m % 2
                            mm = pe.transpose(banks[k % 6][:, m * P:m * P + P], xn_all[:, b, c * P:c * P + P],
                                              g.ident[:, :])
                        mm.then_inc(s_t_ps, 1)

                @block.scalar
                def _(act):
                    arrived(act, g, "L0_ffn")
                    ln.scalar_start(act)
                    act.activation(act_scale[:, 0:1], w["clip_x"], ACT.Exp, scale=-1.0).then_inc(s_sc, 1)
                    act.activation(act_scale[:, 1:2], w["clip_down"], ACT.Exp, scale=-1.0).then_inc(s_sc, 1)

                    def take_off(k, dst, ps):
                        act.wait_ge(s_t_ps, k + 1)
                        act.activation(dst, ps, ACT.Identity, bias=g.nmagic[:, 0:1]).then_inc(s_t_sb, 1)

                    for n, name in enumerate(("gate", "up", "down")):
                        act.wait_ge(s_iw, n + 1)
                        for f in range(w[name].shape[1]):
                            row = w[name][:, f, :]
                            ins = act.activation(row, row, ACT.Identity, bias=g.magic[:, 0:1],
                                                 scale=iw[n][:, f:f + 1])
                        ins.then_inc(s_w2, 1)
                    for k, (_, dst) in enumerate(lots):
                        ps = banks[k % 6][:, 0:3 * P]
                        take_off(k, dst, ps if k < 2 * PL else ps.rearrange("p (m n) -> p m n", m=3))
                    for t in range(NB // 2):
                        k = len(lots) + t
                        take_off(k, xqT[:, :, 2 * t * P:(2 * t + 2) * P].rearrange("p c (b n) -> p b c n", b=2),
                                 banks[k % 6][:, :].rearrange("p (b c n) -> p b c n", b=2, c=2))

                @block.vector
                def _(dve):
                    arrived(dve, g, "L0_ffn")
                    dve.memset(w["gate"][F0 % P:P, FC0 - 1, :], 0.0)
                    dve.memset(w["up"][F0 % P:P, FC0 - 1, :], 0.0)
                    dve.memset(w["down"][:, :, F0:FC0 * P], 0.0).then_inc(s_w, 1)
                    dve.wait_ge(s_w, 1)
                    ln.vector_start(dve)
                    for n, (name, out) in enumerate((("gate", sg), ("up", su), ("down", sd))):
                        dve.tensor_reduce(iw[n][:, :], w[name], AX.X, ALU.max, apply_absolute_value=True).then_inc(s_w, 1)
                        dve.wait_ge(s_w, 2 * n + 2)
                        dve.tensor_scalar(out[:, :], iw[n][:, :], 1.0 / QMAX, 1e-37, ALU.mult, ALU.max
                                          ).then_inc(s_w, 1)
                        dve.wait_ge(s_w, 2 * n + 3)
                        dve.reciprocal(iw[n][:, :], out[:, :]).then_inc(s_iw, 1)
                    with dve.Fori(1, NG + 1) as i:
                        for m in range(TG):
                            b = TG * i - TG + m
                            xn = dve.tensor_scalar(xn_all[:, b, :], g.x[:, b, :], ln.mv[:, b, 0:1],
                                                   ln.rstd[:, b, :], ALU.subtract, ALU.mult)
                        xn.then_inc(ln.s_xn[0], 1)
                        dve.wait_ge(ln.s_xn[0], i)
                        dve.tensor_reduce(amax[:, i - 1, :], xn_all[:, bass.ts(i - 1, TG), :], AX.XY, ALU.max,
                                          apply_absolute_value=True).then_inc(s_amax, 1)
                    dve.wait_ge(s_amax, NG)
                    dve.tensor_reduce(half_col[:, 0:1], amax[:, :, 0], AX.X, ALU.max).then_inc(s_col, 1)
                    dve.wait_ge(s_sc, 2)
                    dve.tensor_scalar(act_scale[:, 2:4], act_scale[:, 0:2], 1.0, QMAX, ALU.add, ALU.mult).then_inc(s_sc, 1)
                    dve.wait_ge(s_sc, 3)
                    dve.reciprocal(act_scale[:, 2:4], act_scale[:, 2:4]).then_inc(s_sc, 1)
                    dve.wait_ge(s_row_ps, 1)
                    dve.tensor_copy(sd_row[:, :], banks[6][:, 0:D]).then_inc(s_sc, 1)
                    top = gm1.vector(dve)
                    dve.wait_ge(s_sc, 5)
                    dve.tensor_tensor(act_scale[:, 4:5], top, act_scale[:, 2:3], ALU.mult).then_inc(s_sc, 1)
                    dve.wait_ge(s_sc, 6)
                    dve.reciprocal(act_scale[:, 5:6], act_scale[:, 4:5]).then_inc(s_sc, 1)
                    dve.wait_ge(s_iw, 3)
                    dve.tensor_scalar(sg[:, :], sg[:, :], act_scale[:, 4:5], None, ALU.mult)
                    dve.tensor_scalar(su[:, :], su[:, :], act_scale[:, 4:5], None, ALU.mult)
                    dve.wait_ge(s_sc, 7)
                    for q in range(NG):
                        part = xn_all[:, TG * q:TG * q + TG, :]
                        dve.tensor_scalar(part, part, act_scale[:, 5:6], MAGIC, ALU.mult, ALU.add).then_inc(s_dr, 1)
                        dve.wait_ge(s_dr, q + 1)
                        dve.tensor_scalar(part, part, MAGIC + QMAX, MAGIC - QMAX - 1.0, ALU.min, ALU.max
                                          ).then_inc(s_xq, 1)

        h = sec.sb("h", [P, FC0, NB * P])
        ga = sec.sb("silu_gate", [P, 3, BANK])
        s_gu_ps, s_silu, s_h, s_free, s_mx = (sec.sem(n) for n in ("gate_up_ps", "silu", "h", "banks_free", "h_amax"))
        with sec.block() as block:
            @block.tensor
            def _(pe):
                with pe.Fori(1, NG + 1) as i:
                    for f in range(FC0):
                        k = f % 3
                        pe.wait_ge(s_free, FC0 * i - FC0 + f + 1)
                        for m, n in enumerate(("gate", "up")):
                            for c in range(DC):
                                mm = pe.matmul(banks[2 * k + m][:, :], wT[n][:, c, f * P:f * P + P],
                                               xqT[:, c, bass.ts(i - 1, BANK)], start=(c == 0), stop=(c == DC - 1))
                        mm.then_inc(s_gu_ps, 1)
                gm2.tensor(pe, g, half_col[:, 1:2], s_col, 2)

            @block.scalar
            def _(act):
                with act.Fori(1, NG + 1) as i:
                    for f in range(FC0):
                        act.wait_ge(s_free, FC0 * i - FC0 + f + 1)
                        act.wait_ge(s_gu_ps, FC0 * i - FC0 + f + 1)
                        act.activation(ga[:, f % 3, :], banks[2 * (f % 3)][:, :], ACT.Silu,
                                       scale=sg[:, f:f + 1]).then_inc(s_silu, 1)

            @block.vector
            def _(dve):
                dve.memset(g.pad[0:1, 0:1], 0.0).then_inc(s_free, 3)
                with dve.Fori(1, NG + 1) as i:
                    for f in range(FC0):
                        dve.wait_ge(s_silu, FC0 * i - FC0 + f + 1)
                        dve.scalar_tensor_tensor(out=h[:, f, bass.ts(i - 1, BANK)], in0=banks[2 * (f % 3) + 1][:, :],
                                                 scalar=su[:, f:f + 1], in1=ga[:, f % 3, :], op0=ALU.mult,
                                                 op1=ALU.mult).then_inc(s_free, 1)
                        if f % 3 == 2:
                            dve.wait_ge(s_free, FC0 * i - FC0 + f + 4)
                            dve.tensor_reduce(hmax[:, i - 1, f // 3:f // 3 + 1], h[:, f - 2:f + 1, bass.ts(i - 1, BANK)],
                                              AX.XY, ALU.max, apply_absolute_value=True).then_inc(s_mx, 1)
                dve.wait_ge(s_mx, 2 * NG)
                dve.tensor_reduce(half_col[:, 1:2], hmax[:, :, :], AX.XY, ALU.max).then_inc(s_col, 1)
                top = gm2.vector(dve)
                dve.tensor_tensor(act_scale[:, 6:7], top, act_scale[:, 3:4], ALU.mult).then_inc(s_sc, 1)
                dve.wait_ge(s_sc, 8)
                dve.reciprocal(act_scale[:, 7:8], act_scale[:, 6:7])
                dve.tensor_scalar(sd_row[:, :], sd_row[:, :], act_scale[:, 6:7], None, ALU.mult)

        hq = sec.sb("hq", [P, 2, FC0, P], BF16)
        yt = sec.sb("yt", [P, 2, D])
        s_hr, s_hc, s_hq, s_y, s_yt, s_x = (sec.per_stream(n) for n in (
            "h_scaled", "h_clipped", "hq", "y", "y_scaled", "x_done"))
        with sec.block() as block:
            @block.scalar
            def _(act):
                def step(old, cur, nxt):
                    for s in range(NS):
                        if nxt:
                            hb = h[:, :, bass.ts(nxt.b(s), P)]
                            act.activation(hb, hb, ACT.Identity, bias=g.magic[:, 0:1], scale=act_scale[:, 7:8]
                                           ).then_inc(s_hr[s], 1)
                    for s in range(NS):
                        if cur:
                            act.wait_ge(s_hc[s], cur.v)
                            if old:
                                act.wait_ge(s_y[s], old.v)
                            act.activation(hq[:, s, :, :], h[:, :, bass.ts(cur.b(s), P)], ACT.Identity,
                                           bias=g.nmagic[:, 0:1]).then_inc(s_hq[s], 1)
                sweep_pairs(act, step)

            @block.vector
            def _(dve):
                def step(old, cur, nxt):
                    if nxt:
                        for s in range(NS):
                            hb = h[:, :, bass.ts(nxt.b(s), P)]
                            dve.wait_ge(s_hr[s], nxt.v)
                            dve.tensor_scalar(hb, hb, MAGIC + QMAX, MAGIC - QMAX - 1.0, ALU.min, ALU.max
                                              ).then_inc(s_hc[s], 1)
                    if old:
                        for s in range(NS):
                            dve.wait_ge(s_y[s], old.v)
                            dve.tensor_tensor(yt[:, s, :], banks[s][:, 0:D], sd_row[:, :], ALU.mult
                                              ).then_inc(s_yt[s], 1)
                        for s in range(NS):
                            b = old.b(s)
                            dve.wait_ge(s_yt[s], old.v)
                            dve.tensor_tensor(g.x[:, b, :], yt[:, s, :], g.x[:, b, :], ALU.add).then_inc(s_x[s], 1)
                        for s in range(NS):
                            dve.wait_ge(s_x[s], old.v)
                            apart(dve, g)
                            dve.bn_stats(g.stats[:, old.b(s), :], g.x[:, old.b(s), :])
                sweep_pairs(dve, step)

            @block.tensor
            def _(pe):
                def step(old, cur, nxt):
                    if cur:
                        for s in range(NS):
                            pe.wait_ge(s_hq[s], cur.v)
                            if old:
                                pe.wait_ge(s_yt[s], old.v)
                            for f in range(FC0):
                                mm = pe.matmul(banks[s][:, 0:D], hq[:, s, f, :], wdT[:, f, :], start=(f == 0),
                                               stop=(f == FC0 - 1))
                            mm.then_inc(s_y[s], 1)
                sweep_pairs(pe, step)


def bitlinear_ffn(nc, g, w):
    sec = Section(nc, "L1f")
    F = 1024
    FC = F // P
    with sec:
        ln = LayerNorm(sec, g)
        H, T2 = ([[sec.ps(f"{n}{s}_{m}", [P, BANK]) for m in range(2)] for s in range(NS)] for n in (
            "hidden", "h_turned"))
        XT = [H[s][0][:, 0:D] for s in range(NS)]
        sbs = lambda nm, shape, dt=F32: [sec.sb(f"{nm}{s}", shape, dt) for s in range(NS)]
        w1T, w2T = sec.sb("w1T", [P, DC, F], BF16), sec.sb("w2T", [P, FC, D], BF16)
        xs, xqT = sbs("xs", [P, D]), sbs("xqT", [P, DC, P], BF16)
        hh, hs = sbs("h", [P, F]), sbs("hs", [P, F])
        hqT = sbs("hqT", [P, FC, P], BF16)
        hp, junk, deq_old = sbs("hp", [P, F]), sbs("junk", [P, F]), sec.sb("dequant_old", [P, NS])
        s_dq = sec.sem("dequant_old")
        am, fac, deq, tmp = (sec.sb(n, [P, 2, NS]) for n in ("am", "factor", "dequant", "tmp"))
        ss, ms, warm = sec.sb("ss", [P, NS]), sec.sb("ms", [P, NB]), sec.sb("warm", [P, 1])
        rs0, rs1 = Rsqrt(sec, "rs0", NB), Rsqrt(sec, "rs1", NS)
        wsum, wmean, winv = sec.sb("wsum", [P, 2]), sec.sb("wmean", [P, 2]), sec.sb("winv", [P, 2])
        s_f1, s_f2, s_f3, s_fac, s_deq = ([sec.sem(f"{n}{k}") for k in range(2)] for n in (
            "amax_normed", "scale", "inverse", "factor", "dequant"))
        s_am, s_scaled, s_qT_ps, s_qT = ([sec.per_stream(f"{n}{k}_") for k in range(2)] for n in (
            "amax", "scaled", "qT_ps", "qT"))
        s_h_ps, s_h = ([[sec.sem(f"{n}{s}_{m}") for m in range(2)] for s in range(NS)] for n in ("h_ps", "h_pre"))
        s_sq, s_gelu, s_y, s_bo, s_x = (sec.per_stream(n) for n in ("squares", "gelu", "y", "b2_added", "x_done"))
        s_ms = sec.sem("mean_square")
        s_ws, s_wps, s_wst, s_wq = sec.sem("w_sums"), sec.sem("w_mean_ps"), sec.sem("w_steps"), sec.sem("w_rounded")
        with ExitStack() as early:
            wq = [early.enter_context(nc.sbuf_tensor(f"L1f_w{n}q", [P, 8, D] if n == 0 else [P, DC, F], BF16))
                  for n in range(2)]
            flat = T2[0] + T2[1] + H[0]
            lots = [([wq[0][:, f + m, c * P:c * P + P] for m in range(4)],
                     w1T[:, c, f * P:(f + 4) * P].rearrange("p (m n) -> p m n", m=4))
                    for c in range(DC) for f in range(0, FC, 4)]
            lots += [([wq[1][:, c, (f + m) * P:(f + m + 1) * P] for m in range(4)], w2T[:, f:f + 4, c * P:c * P + P])
                     for c in range(DC) for f in range(0, FC, 4)]
            s_t_ps, s_t_sb = sec.sem("turned_ps"), sec.sem("turned_sb")
            with sec.block() as block:
                @block.tensor
                def _(pe):
                    pe.wait_ge(s_ws, 2)
                    pe.matmul(H[1][0][:, 0:2], g.onesP[:, :], wsum[:, :], start=True, stop=True).then_inc(s_wps, 1)
                    pe.wait_ge(s_wq, 2)
                    for k in range(len(lots)):
                        if k >= 6:
                            pe.wait_ge(s_t_sb, k - 5)
                        for m in range(4):
                            mm = pe.transpose(flat[k % 6][:, :].bitcast(BF16)[:, m * P:m * P + P],
                                              lots[k][0][m], g.identb[:, :])
                        mm.then_inc(s_t_ps, 1)

                @block.scalar
                def _(act):
                    for k in range(len(lots)):
                        act.wait_ge(s_t_ps, k + 1)
                        act.copy(lots[k][1], flat[k % 6][:, :].bitcast(BF16)[:, 0:4 * P]
                                 .rearrange("p (m n) -> p m n", m=4)).then_inc(s_t_sb, 1)

                @block.vector
                def _(dve):
                    arrived(dve, g, "L1_ffn")
                    for n in range(2):
                        dve.tensor_reduce(wsum[:, n:n + 1], w[f"w{n + 1}"], AX.XY, ALU.add,
                                          apply_absolute_value=True).then_inc(s_ws, 1)
                    dve.wait_ge(s_wps, 1)
                    dve.tensor_scalar(wmean[:, :], H[1][0][:, 0:2], 1.0 / (F * D), 1e-5, ALU.mult,
                                      ALU.max).then_inc(s_wst, 1)
                    dve.wait_ge(s_wst, 1)
                    dve.reciprocal(winv[:, :], wmean[:, :]).then_inc(s_wst, 1)
                    dve.wait_ge(s_wst, 2)
                    for n in range(2):
                        src = w[f"w{n + 1}"]
                        rounded(dve, wq[n][:, :, :], src, src, winv[:, n:n + 1], s_wst, 2 + 3 * n, (-1.0, 1.0))
                        dve.memset(g.pad[0:1, n:n + 1], 0.0).then_inc(s_wq, 1)

        with sec.block() as block:
            @block.gpsimd
            def _(pool):
                arrived(pool, g, "L1_ffn")

                def step(old, cur, nxt):
                    if nxt:
                        for s in range(NS):
                            b = nxt.b(s)
                            pool.wait_ge(ln.s_xn[s], nxt.v)
                            pool.tensor_tensor(g.x[:, b, :], g.x[:, b, :], w["b2"], ALU.add).then_inc(s_bo[s], 1)
                sweep_pairs(pool, step)

            @block.scalar
            def _(act):
                ln.scalar_start(act)
                act.activation(warm[:, :], g.eps[:, :], ACT.Gelu)

                def step(old, cur, nxt):
                    if old:
                        for s in range(NS):
                            act.wait_ge(s_fac[1], old.v)
                            act.activation(hs[s][:, :], hh[s][:, :], ACT.Identity, bias=g.magic[:, 0:1],
                                           scale=fac[:, 1, s:s + 1]).then_inc(s_scaled[1][s], 1)
                    if cur:
                        for s in range(NS):
                            act.wait_ge(s_h[s][1], cur.v)
                            if old:
                                act.wait_ge(s_scaled[1][s], old.v)
                            act.activation(hh[s][:, :], hp[s][:, :], ACT.Gelu).then_inc(s_gelu[s], 1)
                    if nxt:
                        for s in range(NS):
                            act.wait_ge(s_fac[0], nxt.v)
                            act.activation(xs[s][:, :], ln.xn[s][:, :], ACT.Identity, bias=g.magic[:, 0:1],
                                           scale=fac[:, 0, s:s + 1]).then_inc(s_scaled[0][s], 1)
                    if nxt:
                        for s in range(NS):
                            act.wait_ge(s_qT_ps[0][s], nxt.v)
                            act.activation(xqT[s][:, :, :], XT[s].rearrange("p (c t) -> p c t", c=DC),
                                           ACT.Identity, bias=g.nmagic[:, 0:1]).then_inc(s_qT[0][s], 1)
                    if cur:
                        for s in range(NS):
                            act.wait_ge(s_gelu[s], cur.v)
                            act.activation(junk[s][:, :], hh[s][:, :], ACT.Square, accum_out=ss[:, s:s + 1]
                                           ).then_inc(s_sq[s], 1)
                    if old:
                        for s in range(NS):
                            act.wait_ge(s_qT_ps[1][s], old.v)
                            for m in range(2):
                                cp = act.activation(hqT[s][:, 4 * m:4 * m + 4, :],
                                                    T2[s][m][:, :].rearrange("p (c t) -> p c t", c=4),
                                                    ACT.Identity, bias=g.nmagic[:, 0:1])
                            cp.then_inc(s_qT[1][s], 1)
                sweep_pairs(act, step)

            @block.vector
            def _(dve):
                arrived(dve, g, "L1_ffn")
                ln.vector_start(dve)
                dve.tensor_tensor(ms[:, :], ln.mv[:, :, 1], ln.rstd[:, :, 0], ALU.mult).then_inc(s_ms, 1)
                dve.wait_ge(s_ms, 1)
                dve.tensor_tensor(ms[:, :], ms[:, :], ln.rstd[:, :, 0], ALU.mult).then_inc(s_ms, 1)
                dve.wait_ge(s_ms, 2)
                r0 = rs0.vector(dve, ms[:, :], 1.0, 1e-5, 1)

                def factors(k, r, v):
                    t = tmp[:, k, :]
                    dve.tensor_tensor(t, r, am[:, k, :], ALU.mult).then_inc(s_f1[k], 1)
                    dve.wait_ge(s_f1[k], v)
                    dve.tensor_scalar(t, t, 1e-5, 1.0 / QMAX, ALU.max, ALU.mult).then_inc(s_f2[k], 1)
                    dve.wait_ge(s_f2[k], v)
                    dve.tensor_scalar(deq[:, k, :], t, wmean[:, k:k + 1], None, ALU.mult).then_inc(s_deq[k], 1)
                    dve.reciprocal(fac[:, k, :], t).then_inc(s_f3[k], 1)
                    dve.wait_ge(s_f3[k], v)
                    dve.tensor_tensor(fac[:, k, :], fac[:, k, :], r, ALU.mult).then_inc(s_fac[k], 1)
                    dve.wait_ge(s_deq[k], v)

                def take_h(q, s):
                    for m in range(2):
                        dve.wait_ge(s_h_ps[s][m], q.v)
                        dve.scalar_tensor_tensor(out=hp[s][:, m * BANK:(m + 1) * BANK], in0=H[s][m][:, :],
                                                 scalar=deq[:, 0, s:s + 1], in1=w["b1"][:, m * BANK:(m + 1) * BANK],
                                                 op0=ALU.mult, op1=ALU.add).then_inc(s_h[s][m], 1)

                def step(old, cur, nxt):
                    if nxt:
                        for s in range(NS):
                            ln.vector_norm(dve, s, nxt.b(s))
                        for s in range(NS):
                            dve.wait_ge(ln.s_xn[s], nxt.v)
                            dve.tensor_reduce(am[:, 0, s:s + 1], ln.xn[s][:, :], AX.X, ALU.max,
                                              apply_absolute_value=True).then_inc(s_am[0][s], 1)
                        for s in range(NS):
                            dve.wait_ge(s_am[0][s], nxt.v)
                        if cur:
                            dve.wait_ge(s_h[1][1], cur.v)
                        factors(0, r0[:, nxt.pair], nxt.v)
                    if cur:
                        for s in range(NS):
                            dve.wait_ge(s_gelu[s], cur.v)
                            dve.tensor_reduce(am[:, 1, s:s + 1], hh[s][:, :], AX.X, ALU.max,
                                              apply_absolute_value=True).then_inc(s_am[1][s], 1)
                    if old:
                        dve.tensor_copy(deq_old[:, :], deq[:, 1, :]).then_inc(s_dq, 1)
                        dve.wait_ge(s_dq, old.v)
                    if cur:
                        for s in range(NS):
                            dve.wait_ge(s_am[1][s], cur.v)
                            dve.wait_ge(s_sq[s], cur.v)
                        factors(1, rs1.vector(dve, ss[:, :], 1.0 / F, 1e-5, cur.v), cur.v)
                    if nxt:
                        take_h(nxt, 0)
                        take_h(nxt, 1)
                    if old:
                        for s in range(NS):
                            b = old.b(s)
                            dve.wait_ge(s_y[s], old.v)
                            dve.wait_ge(s_bo[s], old.v)
                            dve.scalar_tensor_tensor(out=g.x[:, b, :], in0=T2[s][0][:, 0:D],
                                                     scalar=deq_old[:, s:s + 1], in1=g.x[:, b, :], op0=ALU.mult,
                                                     op1=ALU.add).then_inc(s_x[s], 1)
                        for s in range(NS):
                            dve.wait_ge(s_x[s], old.v)
                            apart(dve, g)
                            dve.bn_stats(g.stats[:, old.b(s), :], g.x[:, old.b(s), :])
                sweep_pairs(dve, step)

            @block.tensor
            def _(pe):
                def step(old, cur, nxt):
                    if nxt:
                        for s in range(NS):
                            pe.wait_ge(s_scaled[0][s], nxt.v)
                            if cur:
                                pe.wait_ge(s_h[s][0], cur.v)
                            for c in range(DC):
                                mm = pe.transpose(XT[s][:, c * P:c * P + P], xs[s][:, c * P:c * P + P], g.ident[:, :])
                            mm.then_inc(s_qT_ps[0][s], 1)
                    if old:
                        for s in range(NS):
                            pe.wait_ge(s_scaled[1][s], old.v)
                            if not nxt:
                                pe.wait_ge(s_x[s], old.v - 1)
                            for f in range(FC):
                                mm = pe.transpose(T2[s][f // 4][:, f % 4 * P:f % 4 * P + P],
                                                  hs[s][:, f * P:f * P + P], g.ident[:, :])
                            mm.then_inc(s_qT_ps[1][s], 1)
                    if nxt:
                        for s in range(NS):
                            pe.wait_ge(s_qT[0][s], nxt.v)
                            for m in range(2):
                                if cur and m == 1:
                                    pe.wait_ge(s_h[s][m], cur.v)
                                for c in range(DC):
                                    mm = pe.matmul(H[s][m][:, :], xqT[s][:, c, :], w1T[:, c, m * BANK:(m + 1) * BANK],
                                                   start=(c == 0), stop=(c == DC - 1))
                                mm.then_inc(s_h_ps[s][m], 1)
                    if old:
                        for s in range(NS):
                            pe.wait_ge(s_qT[1][s], old.v)
                            for f in range(FC):
                                mm = pe.matmul(T2[s][0][:, 0:D], hqT[s][:, f, :], w2T[:, f, :], start=(f == 0),
                                               stop=(f == FC - 1))
                            mm.then_inc(s_y[s], 1)
                sweep_pairs(pe, step)


class TopTwo:
    STEPS = 11

    def __init__(self, sec, name, rows, groups, n):
        self.shape = [rows, groups, n]
        self.m, self.f = (sec.sb(f"{name}_{k}", [rows, 2, groups]) for k in ("m", "f"))
        self.c, self.d, self.one = (sec.sb(f"{name}_{k}", [rows, 2, groups, n]) for k in ("c", "d", "one"))
        self.rest = sec.sb(f"{name}_rest", self.shape)
        self.s = sec.sem(f"{name}_step")

    def vector(self, dve, g, lg, v):
        n, shape = TopTwo.STEPS * (v - 1), self.shape

        def link(k, ins):
            ins.then_inc(self.s, 1)
            dve.wait_ge(self.s, n + k)
        order = g.order[0:shape[0], 0:shape[2]].unsqueeze(1).to_broadcast(shape)
        src = lg
        for k in range(2):
            m, f, c, d, one = self.m[:, k, :], self.f[:, k, :], self.c[:, k], self.d[:, k], self.one[:, k]
            link(6 * k + 1, dve.tensor_reduce(m, src, AX.X, ALU.max))
            link(6 * k + 2, dve.tensor_tensor(c, src, m.unsqueeze(2).to_broadcast(shape), ALU.is_equal))
            link(6 * k + 3, dve.tensor_tensor(d, c, order, ALU.mult))
            link(6 * k + 4, dve.tensor_reduce(f, d, AX.X, ALU.max))
            link(6 * k + 5, dve.tensor_tensor(one, d, f.unsqueeze(2).to_broadcast(shape), ALU.is_equal))
            if k == 0:
                link(6, dve.scalar_tensor_tensor(out=self.rest[:, :, :], in0=one, scalar=-BIG, in1=lg, op0=ALU.mult,
                                                 op1=ALU.add))
                src = self.rest[:, :, :]


def lora_ffn(nc, g, w):
    sec = Section(nc, "L2f")
    E, R, F = 8, 16, 1024
    FC = F // P
    with sec:
        ln = LayerNorm(sec, g)
        U = [[sec.ps(f"inner{s}_{t}", [P, BANK]) for t in range(2)] for s in range(NS)]
        X, Y = ([sec.ps(f"{n}{s}", [P, BANK]) for s in range(NS)] for n in ("x_turned", "y_ps"))
        sbs = lambda nm, shape, dt=F32: [sec.sb(f"{nm}{s}", shape, dt) for s in range(NS)]
        wiT, woT, bT = sec.sb("wiT", [P, DC, F]), sec.sb("woT", [P, FC, D]), sec.sb("loraBT", [P, F])
        agT = sec.sb("loraA_gateT", [P, DC, P + E])
        bo2 = sec.sb("bo2", [P, D])
        xT, xTb, y = sbs("xT", [P, DC, P]), sbs("xTb", [P, DC, P]), sbs("y", [P, D])
        lg, dl, diff = sec.sb("logits", [P, NS, E]), sec.sb("dl", [P, NS, E + 1]), sec.sb("diff", [P, NS, E])
        den, rden, vs, warm = (sec.sb(n, [P, k]) for n, k in (("den", NS), ("rden", NS), ("vs", NS), ("warm", 1)))
        tk = TopTwo(sec, "top", P, NS, E)
        ta, tb = sbs("ta", [P, 2, P]), sbs("taT", [P, 2, P])
        hs, u = sbs("hs", [P, FC, P]), [sbs(f"u{s}_", [P, 4, P]) for s in range(NS)]
        fours = range(0, FC, 4)
        lots = [([w["wi"][:, f + m, c * P:c * P + P] for m in range(4)],
                 wiT[:, c, f * P:(f + 4) * P].rearrange("p (m n) -> p m n", m=4)) for c in range(DC) for f in fours]
        lots += [([w["wo"][:, c, (f + m) * P:(f + m + 1) * P] for m in range(4)], woT[:, f:f + 4, c * P:c * P + P])
                 for c in range(DC) for f in fours]
        lots += [([w["lora_B"][:, f + m, :] for m in range(4)],
                  bT[:, f * P:(f + 4) * P].rearrange("p (m n) -> p m n", m=4)) for f in fours]
        lots += [([w["lora_A"][:, c * P:c * P + P] for c in range(DC)], agT[:, :, 0:P])]
        lots += [([w["gate_w"][:, c * P:c * P + P] for c in range(DC)], agT[:, :, P:P + E])]
        turn_w = Turned(sec, [U[0][0], U[1][0]], lots)
        (s_xT_ps, s_xT, s_xTb, s_t_ps, s_lg, s_ta, s_taT_ps, s_taT, s_first, s_y_ps, s_y, s_x) = (
            sec.per_stream(n) for n in ("xT_ps", "xT", "xTb", "lora_ps", "logits", "masked", "maskedT_ps",
                                        "maskedT", "first_made", "y_ps", "y", "x_done"))
        s_u1, s_r1, s_u2, s_hs = ([[sec.sem(f"{n}{s}_{t}") for t in range(2)] for s in range(NS)] for n in (
            "first", "first_relu", "second", "hidden"))
        s_u_ps = [[[sec.sem(f"{n}{s}_{t}") for t in range(2)] for s in range(NS)] for n in ("first_ps", "second_ps")]
        s_dl, s_e, s_vs, s_diff, s_den, s_rden = (sec.sem(n) for n in (
            "shifted", "exp", "val_sum", "mask_diff", "den", "inverse_den"))
        s_bo2 = sec.sem("bo2")
        with sec.block() as block:
            @block.tensor
            def _(pe):
                arrived(pe, g, "L2_ffn")
                turn_w.tensor(pe, g.ident)
                turn_w.wait(pe)

                def first(q, s):
                    pe.wait_ge(s_xTb[s], q.v)
                    for f in range(FC):
                        for c in range(DC):
                            mm = pe.matmul(U[s][f // 4][:, f % 4 * P:f % 4 * P + P], wiT[:, c, f * P:f * P + P],
                                           xTb[s][:, c, :], start=(f % 4 == 0 and c == 0), stop=False,
                                           skip_group_check=True)
                    mm.then_inc(s_first[s], 1)

                def expert(q, s, k):
                    pe.wait_ge(s_taT[s], q.v)
                    for f in range(FC):
                        if k == 1 and f % 4 == 0:
                            pe.wait_ge(s_u1[s][f // 4], q.v)
                        mm = pe.matmul(U[s][f // 4][:, f % 4 * P:f % 4 * P + P], bT[:, f * P:f * P + P],
                                       tb[s][:, k, :], start=False, stop=(k == 1), skip_group_check=True)
                        if f % 4 == 3:
                            mm.then_inc(s_u_ps[k][s][f // 4], 1)

                def down(q, s, cur):
                    if cur:
                        pe.wait_ge(s_taT[s], cur.v)
                    elif q.v > 1:
                        pe.wait_ge(s_y[s], q.v - 1)
                    for f in range(FC):
                        if f % 4 == 0:
                            pe.wait_ge(s_hs[s][f // 4], q.v)
                        mm = pe.matmul(Y[s][:, 0:D], hs[s][:, f, :], woT[:, f, :], start=(f == 0), stop=(f == FC - 1))
                    mm.then_inc(s_y_ps[s], 1)

                def step(old, cur, nxt):
                    if old:
                        for s in range(NS):
                            first(old, s)
                        for s in range(NS):
                            expert(old, s, 0)
                    if cur:
                        for s in range(NS):
                            pe.wait_ge(s_ta[s], cur.v)
                            for k in range(2):
                                mm = pe.transpose(Y[s][:, k * P:(k + 1) * P], ta[s][:, k, :], g.ident[:, :])
                            mm.then_inc(s_taT_ps[s], 1)
                    if old:
                        for s in range(NS):
                            expert(old, s, 1)
                    if nxt:
                        for s in range(NS):
                            pe.wait_ge(ln.s_xn[s], nxt.v)
                            for c in range(DC):
                                mm = pe.transpose(X[s][:, c * P:c * P + P], ln.xn[s][:, c * P:c * P + P], g.ident[:, :])
                            mm.then_inc(s_xT_ps[s], 1)
                    if old:
                        down(old, 0, cur)
                    if nxt:
                        for s in range(NS):
                            pe.wait_ge(s_xT[s], nxt.v)
                            for c in range(DC):
                                mm = pe.matmul(X[s][:, D:D + P + E], xT[s][:, c, :], agT[:, c, :], start=(c == 0),
                                               stop=(c == DC - 1))
                            mm.then_inc(s_t_ps[s], 1)
                    if old:
                        down(old, 1, cur)
                sweep_pairs(pe, step)

            @block.scalar
            def _(act):
                ln.scalar_start(act)
                turn_w.scalar(act)
                act.activation(warm[:, :], g.eps[:, :], ACT.Exp)

                def step(old, cur, nxt):
                    if cur:
                        for s in range(NS):
                            act.wait_ge(s_xT[s], cur.v)
                            if old:
                                act.wait_ge(s_first[s], old.v)
                            act.copy(xTb[s][:, :, :], xT[s][:, :, :]).then_inc(s_xTb[s], 1)
                        act.wait_ge(s_dl, cur.v)
                        act.activation(dl[:, :, :], dl[:, :, :], ACT.Exp).then_inc(s_e, 1)
                    if old:
                        for s in range(NS):
                            for t in range(2):
                                act.wait_ge(s_u1[s][t], old.v)
                                act.activation(hs[s][:, 4 * t:4 * t + 4, :], hs[s][:, 4 * t:4 * t + 4, :], ACT.Relu
                                               ).then_inc(s_r1[s][t], 1)
                    if cur:
                        for s in range(NS):
                            act.wait_ge(s_taT_ps[s], cur.v)
                            if old:
                                act.wait_ge(s_u_ps[1][s][1], old.v)
                            act.copy(tb[s][:, :, :], Y[s][:, 0:2 * P].rearrange("p (k t) -> p k t", k=2)
                                     ).then_inc(s_taT[s], 1)
                    if nxt:
                        for s in range(NS):
                            act.wait_ge(s_xT_ps[s], nxt.v)
                            if cur:
                                act.wait_ge(s_xTb[s], cur.v)
                            act.copy(xT[s][:, :, :], X[s][:, 0:D].rearrange("p (c t) -> p c t", c=DC)
                                     ).then_inc(s_xT[s], 1)
                sweep_pairs(act, step)

            @block.gpsimd
            def _(pool):
                arrived(pool, g, "L2_ffn")
                pool.tensor_tensor(bo2[:, :], w["bo"], w["bo"], ALU.add).then_inc(s_bo2, 1)

            @block.vector
            def _(dve):
                arrived(dve, g, "L2_ffn")
                dve.wait_ge(s_bo2, 1)
                ln.vector_start(dve)
                one = tk.one
                bi = lambda t: w["bi"][:, 4 * t:4 * t + 4].unsqueeze(2).to_broadcast([P, 4, P])
                ps = lambda s, t: U[s][t][:, :].rearrange("p (m t) -> p m t", m=4)
                er = lambda ap: ap.rearrange("p (e r) -> p e r", e=E)

                def gate(q):
                    for s in range(NS):
                        dve.wait_ge(s_t_ps[s], q.v)
                        dve.tensor_tensor(lg[:, s, :], X[s][:, D + P:D + P + E], w["gate_b"], ALU.add
                                          ).then_inc(s_lg[s], 1)
                    for s in range(NS):
                        dve.wait_ge(s_lg[s], q.v)
                    tk.vector(dve, g, lg[:, :, :], q.v)
                    top = tk.m[:, 0, :]
                    dve.tensor_tensor(dl[:, :, 0:E], lg[:, :, :], top.unsqueeze(2).to_broadcast([P, NS, E]),
                                      ALU.subtract)
                    dve.tensor_tensor(dl[:, :, E], tk.m[:, 1, :], top, ALU.subtract).then_inc(s_dl, 1)
                    dve.tensor_tensor(diff[:, :, :], one[:, 1, :, :], one[:, 0, :, :], ALU.subtract
                                      ).then_inc(s_diff, 1)
                    dve.wait_ge(s_diff, q.v)
                    for s in range(NS):
                        t_ps = er(X[s][:, D:D + P])
                        dve.tensor_tensor(er(ta[s][:, 0, :]), t_ps, one[:, 0, s, :].unsqueeze(2).to_broadcast([P, E, R]),
                                          ALU.mult)
                        dve.tensor_tensor(er(ta[s][:, 1, :]), t_ps, diff[:, s, :].unsqueeze(2).to_broadcast([P, E, R]),
                                          ALU.mult).then_inc(s_ta[s], 1)

                def step(old, cur, nxt):
                    if cur:
                        gate(cur)
                    if nxt:
                        for s in range(NS):
                            ln.vector_norm(dve, s, nxt.b(s))
                    if old:
                        for s in range(NS):
                            for t in range(2):
                                dve.wait_ge(s_u_ps[0][s][t], old.v)
                                dve.tensor_tensor(hs[s][:, 4 * t:4 * t + 4, :], ps(s, t), bi(t), ALU.add
                                                  ).then_inc(s_u1[s][t], 1)
                        for s in range(NS):
                            for t in range(2):
                                dve.wait_ge(s_u_ps[1][s][t], old.v)
                                dve.tensor_tensor(u[s][t][:, :, :], ps(s, t), bi(t), ALU.add).then_inc(s_u2[s][t], 1)
                            for t in range(2):
                                dve.wait_ge(s_u2[s][t], old.v)
                                dve.wait_ge(s_r1[s][t], old.v)
                                dve.scalar_tensor_tensor(out=hs[s][:, 4 * t:4 * t + 4, :], in0=u[s][t][:, :, :],
                                                         scalar=0.0, in1=hs[s][:, 4 * t:4 * t + 4, :], op0=ALU.max,
                                                         op1=ALU.add).then_inc(s_hs[s][t], 1)
                        for s in range(NS):
                            b = old.b(s)
                            dve.wait_ge(s_y_ps[s], old.v)
                            dve.tensor_tensor(y[s][:, :], Y[s][:, 0:D], bo2[:, :], ALU.add).then_inc(s_y[s], 1)
                            dve.wait_ge(s_y[s], old.v)
                            dve.scalar_tensor_tensor(out=g.x[:, b, :], in0=y[s][:, :], scalar=vs[:, s:s + 1],
                                                     in1=g.x[:, b, :], op0=ALU.mult, op1=ALU.add).then_inc(s_x[s], 1)
                        for s in range(NS):
                            dve.wait_ge(s_x[s], old.v)
                            apart(dve, g)
                            dve.bn_stats(g.stats[:, old.b(s), :], g.x[:, old.b(s), :])
                    if cur:
                        dve.wait_ge(s_e, cur.v)
                        dve.tensor_reduce(den[:, :], dl[:, :, 0:E], AX.X, ALU.add).then_inc(s_den, 1)
                        dve.wait_ge(s_den, cur.v)
                        dve.reciprocal(rden[:, :], den[:, :]).then_inc(s_rden, 1)
                        dve.wait_ge(s_rden, cur.v)
                        dve.scalar_tensor_tensor(out=vs[:, :], in0=dl[:, :, E], scalar=1.0, in1=rden[:, :],
                                                 op0=ALU.add, op1=ALU.mult).then_inc(s_vs, 1)
                        dve.wait_ge(s_vs, cur.v)
                sweep_pairs(dve, step)


def gated_attention(nc, g, w, ctx_dram):
    sec = Section(nc, "L3a")
    SCALE = D ** -0.5
    with sec:
        ln = LayerNorm(sec, g)
        X, Z, L, H = ([sec.ps(f"{n}{s}", [P, BANK]) for s in range(NS)] for n in (
            "turned", "gate_query", "logits_ps", "h_tilde"))
        sbs = lambda nm, shape, dt=F32: [sec.sb(f"{nm}{s}", shape, dt) for s in range(NS)]
        sided = lambda nm, shape: [sbs(f"{nm}{side}_", shape) for side in range(2)]
        qk, gwT = sec.sb("qk", [P, DC, D]), sec.sb("gate_wT", [P, DC, D])
        ms, rs = sec.sb("ms", [P, NB]), Rsqrt(sec, "rs", NB)
        xn, nm, xnT, qT, z, mem = (sided(n, shape) for n, shape in (
            ("xn", [P, D]), ("nm", [P, D]), ("xnT", [P, 2, DC, P]), ("qT", [P, DC, P]), ("z", [P, D]), ("mem", [P, D])))
        lgt, pT, d = sbs("logits", [P, 2, P]), sbs("probsT", [P, 2, P]), sbs("d", [P, D])
        mx, den = sbs("mx", [P, 2]), sbs("den", [P, 2])
        turn_w = Turned(sec, [X[0], X[1]], [square_lot(w["gate_w"], gwT)])
        s_qk_ps, s_qk, s_ms = sec.sem("qk_ps"), sec.sem("qk"), sec.sem("mean_square")
        (s_mem, s_xn, s_nm, s_t_ps, s_t, s_q_ps, s_q, s_z, s_ez, s_ap1, s_al, s_base, s_l_ps, s_lg, s_mx, s_nb, s_p,
         s_pT_ps, s_pT, s_h, s_rd, s_d1, s_d2, s_x) = (
            [sec.per_stream(f"{n}{side}_") for side in range(2)] for n in (
                "mem", "xn", "nm", "turned_ps", "turned", "query_ps", "query", "z", "exp_z", "alpha1", "alpha",
                "xn_added", "logits_ps", "logits", "max", "neg_max", "probs", "probsT_ps", "probsT", "h_tilde",
                "recip", "d1", "d2", "x_done"))

        def run(eng, step):
            sweep(eng, lambda st: step(st.at(0), st.at(1)), ahead=1, behind=0, count=TURNS)

        with sec.block() as block:
            @block.sync
            def _(sp):
                def step(st):
                    prev, nxt = st.at(-1), st.at(1)
                    if nxt:
                        for s in range(NS):
                            if prev:
                                sp.wait_ge(s_h[prev.s][s], prev.v)
                            sp.dma_start(mem[nxt.s][s][:, :], ctx_dram[NS * nxt.b + s, :, :]
                                         ).then_inc(s_mem[nxt.s][s], 16)
                sweep(sp, step, ahead=1, behind=0, count=TURNS)

            @block.tensor
            def _(pe):
                arrived(pe, g, "L3_xattn")
                turn_w.tensor(pe, g.ident)
                for m in range(DC):
                    for c in range(DC):
                        mm = pe.matmul(Z[0][:, m * D:m * D + D], w["q_w"][:, c, m * P:m * P + P], w["k_w"][:, c, :],
                                       start=(c == 0), stop=(c == DC - 1))
                mm.then_inc(s_qk_ps, 1)
                turn_w.wait(pe)
                pe.wait_ge(s_qk, 1)

                def step(cur, nxt):
                    if cur:
                        k = cur.s
                        for s in range(NS):
                            pe.wait_ge(s_q[k][s], cur.v)
                            keys = [xnT[k][s][:, 1], g.ctxT[:, NS * cur.b + s]]
                            for n in range(2):
                                for c in range(DC):
                                    mm = pe.matmul(L[s][:, n * P:n * P + P], qT[k][s][:, c, :], keys[n][:, c, :],
                                                   start=(c == 0), stop=(c == DC - 1))
                            mm.then_inc(s_l_ps[k][s], 1)
                    if nxt:
                        j = nxt.s
                        for s in range(NS):
                            pe.wait_ge(s_xn[j][s], nxt.v)
                            pe.wait_ge(s_nm[j][s], nxt.v)
                            for n, src in enumerate((xn, nm)):
                                for c in range(DC):
                                    mm = pe.transpose(X[s][:, n * D + c * P:n * D + c * P + P],
                                                      src[j][s][:, c * P:c * P + P], g.ident[:, :])
                            mm.then_inc(s_t_ps[j][s], 1)
                    for s in range(NS):
                        if nxt:
                            pe.wait_ge(s_t[j][s], nxt.v)
                            if cur:
                                pe.wait_ge(s_z[k][s], cur.v)
                            for c in range(DC):
                                pe.matmul(Z[s][:, 0:D], xnT[j][s][:, 0, c, :], gwT[:, c, :], start=(c == 0),
                                          stop=(c == DC - 1))
                            for m in range(DC):
                                for c in range(DC):
                                    mm = pe.matmul(Z[s][:, D + m * P:D + m * P + P], qk[:, c, m * P:m * P + P],
                                                   xnT[j][s][:, 1, c, :], start=(c == 0), stop=(c == DC - 1))
                            mm.then_inc(s_q_ps[j][s], 1)
                        if cur:
                            pe.wait_ge(s_p[k][s], cur.v)
                            for n in range(2):
                                mm = pe.transpose(L[s][:, D + n * P:D + n * P + P], lgt[s][:, n, :], g.ident[:, :])
                            mm.then_inc(s_pT_ps[k][s], 1)
                    if cur:
                        for s in range(NS):
                            pe.wait_ge(s_pT[k][s], cur.v)
                            pe.wait_ge(s_mem[k][s], 16 * cur.v)
                            pe.matmul(H[s][:, 0:D], pT[s][:, 0, :], nm[k][s][:, :], start=True, stop=False)
                            pe.matmul(H[s][:, 0:D], pT[s][:, 1, :], mem[k][s][:, :], start=False, stop=True
                                      ).then_inc(s_h[k][s], 1)
                run(pe, step)

            @block.scalar
            def _(act):
                ln.scalar_start(act)
                turn_w.scalar(act)
                act.wait_ge(s_qk_ps, 1)
                act.copy(qk[:, :, :], Z[0][:, :].rearrange("p (c n) -> p c n", c=DC)).then_inc(s_qk, 1)
                two = lambda ap: ap.rearrange("p (c t) -> p c t", c=DC)

                def step(cur, nxt):
                    if nxt:
                        j = nxt.s
                        for s in range(NS):
                            act.wait_ge(s_t_ps[j][s], nxt.v)
                            act.copy(xnT[j][s][:, :, :, :], X[s][:, :].rearrange("p (n c t) -> p n c t", n=2, c=DC)
                                     ).then_inc(s_t[j][s], 1)
                    if cur:
                        k = cur.s
                        for s in range(NS):
                            act.wait_ge(s_nb[k][s], cur.v)
                            act.activation(lgt[s][:, :, :], lgt[s][:, :, :], ACT.Exp, bias=mx[s][:, 1:2], scale=SCALE,
                                           accum_out=den[s][:, 0:1]).then_inc(s_p[k][s], 1)
                    for s in range(NS):
                        if nxt:
                            act.wait_ge(s_q_ps[j][s], nxt.v)
                            act.copy(qT[j][s][:, :, :], two(Z[s][:, D:2 * D])).then_inc(s_q[j][s], 1)
                        if cur:
                            act.wait_ge(s_pT_ps[k][s], cur.v)
                            act.copy(pT[s][:, :, :], two(L[s][:, D:2 * D])).then_inc(s_pT[k][s], 1)
                    if nxt:
                        for s in range(NS):
                            act.wait_ge(s_z[j][s], nxt.v)
                            act.activation(z[j][s][:, :], z[j][s][:, :], ACT.Exp, scale=-1.0).then_inc(s_ez[j][s], 1)
                run(act, step)

            @block.gpsimd
            def _(pool):
                def step(cur, nxt):
                    if nxt:
                        j = nxt.s
                        for s in range(NS):
                            b = NS * nxt.b + s
                            pool.wait_ge(s_xn[j][s], nxt.v)
                            pool.tensor_tensor(g.x[:, b, :], g.x[:, b, :], xn[j][s][:, :], ALU.add
                                               ).then_inc(s_base[j][s], 1)
                        for s in range(NS):
                            pool.wait_ge(s_ez[j][s], nxt.v)
                            pool.tensor_tensor(z[j][s][:, :], z[j][s][:, :], g.onesP[:, 0:1].to_broadcast([P, D]),
                                               ALU.add).then_inc(s_ap1[j][s], 1)
                run(pool, step)

            @block.vector
            def _(dve):
                arrived(dve, g, "L3_xattn")
                ln.vector_start(dve)
                dve.tensor_tensor(ms[:, :], ln.mv[:, :, 1], ln.rstd[:, :, 0], ALU.mult).then_inc(s_ms, 1)
                dve.wait_ge(s_ms, 1)
                dve.tensor_tensor(ms[:, :], ms[:, :], ln.rstd[:, :, 0], ALU.mult).then_inc(s_ms, 1)
                dve.wait_ge(s_ms, 2)
                r = rs.vector(dve, ms[:, :], 1.0, 1e-6, 1)

                def step(cur, nxt):
                    if nxt:
                        j = nxt.s
                        for s in range(NS):
                            b = NS * nxt.b + s
                            dve.tensor_scalar(xn[j][s][:, :], g.x[:, b, :], ln.mv[:, b, 0:1], ln.rstd[:, b, :],
                                              ALU.subtract, ALU.mult).then_inc(s_xn[j][s], 1)
                        for s in range(NS):
                            b = NS * nxt.b + s
                            dve.wait_ge(s_xn[j][s], nxt.v)
                            dve.scalar_tensor_tensor(out=nm[j][s][:, :], in0=xn[j][s][:, :], scalar=r[:, bass.ds(b, 1)],
                                                     in1=w["norm_w"], op0=ALU.mult, op1=ALU.mult
                                                     ).then_inc(s_nm[j][s], 1)
                    if cur:
                        k = cur.s
                        for s in range(NS):
                            dve.wait_ge(s_l_ps[k][s], cur.v)
                            dve.tensor_tensor(lgt[s][:, :, :], L[s][:, 0:D].rearrange("p (k t) -> p k t", k=2),
                                              g.causal[:, :, :], ALU.add).then_inc(s_lg[k][s], 1)
                            dve.wait_ge(s_lg[k][s], cur.v)
                            dve.tensor_reduce(mx[s][:, 0:1], lgt[s][:, :, :], AX.XY, ALU.max).then_inc(s_mx[k][s], 1)
                            dve.wait_ge(s_mx[k][s], cur.v)
                            dve.tensor_scalar(mx[s][:, 1:2], mx[s][:, 0:1], -SCALE, None, ALU.mult
                                              ).then_inc(s_nb[k][s], 1)
                        for s in range(NS):
                            dve.wait_ge(s_ap1[k][s], cur.v)
                            dve.reciprocal(z[k][s][:, :], z[k][s][:, :]).then_inc(s_al[k][s], 1)
                    if nxt:
                        for s in range(NS):
                            dve.wait_ge(s_q[j][s], nxt.v)
                            dve.tensor_tensor(z[j][s][:, :], Z[s][:, 0:D], w["gate_b"], ALU.add).then_inc(s_z[j][s], 1)
                    if cur:
                        for s in range(NS):
                            dve.wait_ge(s_p[k][s], cur.v)
                            dve.reciprocal(den[s][:, 1:2], den[s][:, 0:1]).then_inc(s_rd[k][s], 1)
                        for s in range(NS):
                            b = NS * cur.b + s
                            dve.wait_ge(s_rd[k][s], cur.v)
                            dve.wait_ge(s_h[k][s], cur.v)
                            dve.scalar_tensor_tensor(out=d[s][:, :], in0=H[s][:, 0:D], scalar=den[s][:, 1:2],
                                                     in1=xn[k][s][:, :], op0=ALU.mult, op1=ALU.subtract
                                                     ).then_inc(s_d1[k][s], 1)
                            dve.wait_ge(s_d1[k][s], cur.v)
                            dve.wait_ge(s_al[k][s], cur.v)
                            dve.tensor_tensor(d[s][:, :], d[s][:, :], z[k][s][:, :], ALU.mult).then_inc(s_d2[k][s], 1)
                            dve.wait_ge(s_d2[k][s], cur.v)
                            dve.wait_ge(s_base[k][s], cur.v)
                            dve.tensor_tensor(g.x[:, b, :], d[s][:, :], g.x[:, b, :], ALU.add).then_inc(s_x[k][s], 1)
                        for s in range(NS):
                            dve.wait_ge(s_x[k][s], cur.v)
                            apart(dve, g)
                            dve.bn_stats(g.stats[:, NS * cur.b + s, :], g.x[:, NS * cur.b + s, :])
                run(dve, step)


def expert_gates(nc, g, w):
    sec = Section(nc, "L3g")
    E, HID = 4, 128
    with sec:
        ln = LayerNorm(sec, g)
        bank = banks_of(sec)
        r, mr = sec.sb("r", [P, NB, 1]), sec.sb("mr", [P, NB])
        pooled, hid = sec.sb("pooled", [P, DC, NB]), sec.sb("hid", [HID, NB])
        lg, dg = sec.sb("logits", [NB, E]), sec.sb("spread", [NB, NB, E])
        sw = sec.sb("shares", [NB, 4])
        wt = sec.sb("weights", [NB, 2, E])
        tk = TopTwo(sec, "top", NB, 1, E)
        s_mr, s_ps, s_pool, s_hid_ps, s_hid, s_lg_ps, s_lg, s_e, s_st, s_g_ps = (sec.sem(n) for n in (
            "mean_factors", "pooled_ps", "pooled", "hidden_ps", "hidden", "logits_ps", "logits", "exp", "steps",
            "gates_ps"))
        corr = sec.sb("correction", [P, NB])
        s_corr = sec.sem("correction")
        with sec.block() as block:
            @block.tensor
            def _(pe):
                arrived(pe, g, "L3_ffn")
                pe.wait_ge(s_mr, 2)
                pe.matmul(bank[0][0][:, 0:NB], g.onesP[:, :], mr[:, :], start=True, stop=True)
                for b in range(NB):
                    for c in range(DC):
                        n = NB * (c + 1) + b
                        mm = pe.matmul(bank[0][0][:, n:n + 1], g.x[:, b, c * P:c * P + P], r[:, b, :], start=True,
                                       stop=True)
                mm.then_inc(s_ps, 1)
                pe.wait_ge(s_pool, 1)
                for c in range(DC):
                    mm = pe.matmul(bank[0][1][0:HID, 0:NB], w["Wg1"][:, c, :], pooled[:, c, :], start=(c == 0),
                                   stop=(c == DC - 1))
                mm.then_inc(s_hid_ps, 1)
                pe.wait_ge(s_hid, 1)
                pe.matmul(bank[0][2][0:NB, 0:E], hid[:, :], w["Wg2"][:, 0, :], start=True, stop=True).then_inc(s_lg_ps, 1)
                pe.wait_ge(s_st, 6)
                pe.matmul(bank[0][3][:, 0:NB * E], g.onesP[0:NB, :], dg[:, :, :], start=True, stop=True).then_inc(s_g_ps, 1)

            @block.scalar
            def _(act):
                arrived(act, g, "L3_ffn")
                ln.scalar_start(act)
                act.wait_ge(s_hid_ps, 1)
                act.activation(hid[:, :], bank[0][1][0:HID, 0:NB], ACT.Relu, bias=w["bg1"][:, 0:1]).then_inc(s_hid, 1)
                act.wait_ge(s_st, 1)
                act.activation(sw[:, 1:2], sw[:, 0:1], ACT.Exp).then_inc(s_e, 1)

            @block.vector
            def _(dve):
                arrived(dve, g, "L3_ffn")
                ln.vector_start(dve)
                dve.tensor_scalar(r[:, :, 0], ln.rstd[:, :, 0], 1.0 / P, None, ALU.mult).then_inc(s_mr, 1)
                dve.wait_ge(s_mr, 1)
                dve.tensor_tensor(mr[:, :], r[:, :, 0], ln.mv[:, :, 0], ALU.mult).then_inc(s_mr, 1)
                dve.wait_ge(s_ps, 1)
                dve.tensor_copy(corr[:, :], bank[0][0][:, 0:NB]).then_inc(s_corr, 1)
                dve.wait_ge(s_corr, 1)
                dve.tensor_tensor(pooled[:, :, :],
                                  bank[0][0][:, NB:3 * NB].rearrange("p (c b) -> p c b", c=DC),
                                  corr[:, :].unsqueeze(1).to_broadcast([P, DC, NB]), ALU.subtract).then_inc(s_pool, 1)
                dve.wait_ge(s_lg_ps, 1)
                dve.tensor_tensor(lg[:, :], bank[0][2][0:NB, 0:E], w["bg2"][0:NB, :], ALU.add).then_inc(s_lg, 1)
                dve.wait_ge(s_lg, 1)
                tk.vector(dve, g, lg[:, :].unsqueeze(1), 1)
                dve.tensor_scalar(sw[:, 0:1], tk.m[:, 1:2], tk.m[:, 0:1], None, ALU.subtract).then_inc(s_st, 1)
                dve.wait_ge(s_e, 1)
                dve.tensor_scalar(sw[:, 2:3], sw[:, 1:2], 1.0, None, ALU.add).then_inc(s_st, 1)
                dve.wait_ge(s_st, 2)
                dve.reciprocal(sw[:, 2:3], sw[:, 2:3]).then_inc(s_st, 1)
                dve.wait_ge(s_st, 3)
                dve.tensor_tensor(sw[:, 3:4], sw[:, 2:3], sw[:, 1:2], ALU.mult)
                dve.tensor_scalar(wt[:, 0, :], tk.one[:, 0, 0, :], sw[:, 2:3], None, ALU.mult).then_inc(s_st, 1)
                dve.wait_ge(s_st, 4)
                dve.scalar_tensor_tensor(out=wt[:, 1, :], in0=tk.one[:, 1, 0, :], scalar=sw[:, 3:4], in1=wt[:, 0, :],
                                         op0=ALU.mult, op1=ALU.add).then_inc(s_st, 1)
                dve.wait_ge(s_st, 5)
                dve.tensor_tensor(dg[:, :, :], g.ident[0:NB, 0:NB].unsqueeze(2).to_broadcast([NB, NB, E]),
                                  wt[:, 1, :].unsqueeze(1).to_broadcast([NB, NB, E]), ALU.mult).then_inc(s_st, 1)
                dve.wait_ge(s_g_ps, 1)
                dve.tensor_copy(g.gates[:, :, :, 0], bank[0][3][:, 0:NB * E].rearrange("p (b e) -> p b e", e=E))


def finish(nc, g, out):
    sec = Section(nc, "finish")
    with sec:
        s_out = sec.sem("out")
        with sec.block() as block:
            @block.sync
            def _(sp):
                sp.dma_start(out.rearrange("b p d -> p b d"), g.x[:, :, :]).then_inc(s_out, 16)
                sp.wait_ge(s_out, 16)


def program(nc, a, out):
    g = Globals()
    with ExitStack() as whole:
        scope = [whole]

        def sb(name, shape, dt=F32):
            return scope[-1].enter_context(nc.sbuf_tensor(name, shape, dt))

        g.loads, g.counts = [], {"x": 1}
        g.loaded = {"x": nc.alloc_semaphore("x_loaded")}

        def loading(what, dst, src):
            if what not in g.loaded:
                g.loaded[what] = nc.alloc_semaphore(f"{what}_loaded")
                g.counts[what] = 0
            g.counts[what] += 1
            g.loads.append((dst, src, what))

        def load(what, name, shape, src, dt=F32):
            t = sb(name, shape, dt)
            t = t[tuple(slice(None) for _ in shape)]
            loading(what, t, src)
            return t

        def matrix(what, name):
            r, n = a[name].shape
            return load(what, name, [P, r // P, n], a[name].rearrange("(c p) n -> p c n", p=P))

        def column(what, name):
            return load(what, name, [P, a[name].shape[0] // P], a[name].rearrange("(c p) -> p c", p=P))

        def row(what, name):
            return load(what, name, [P, a[name].shape[0]], a[name].partition_broadcast(P))

        g.x = sb("x_all", [P, NB, D])
        g.stats = sb("stats", [P, NB, 6])
        g.ctxT = sb("ctxT_all", [P, NB, DC, P])
        g.ident, g.hmask, g.causal = sb("ident", [P, P]), sb("hmask", [P, HC]), sb("causal", [P, 2, P])
        g.pad, g.pads = sb("pad", [1, PADS]), 0
        g.order, g.hidden, g.identb = sb("order", [P, 8]), sb("hidden", [P, P], BF16), sb("identb", [P, P], BF16)
        g.gates = sb("gates", [P, NB, 4, 1])
        g.mask = load("mask", "mask", [P, P], a["mask_1x1xSxS2_bk0"].rearrange("a b q k -> (a b q) k"), U8)
        g.eps, g.magic, g.nmagic, g.onesP = (sb(n, [P, k]) for n, k in (
            ("eps", 1), ("magic", 1), ("minus_magic", 1), ("onesP", P)))

        def xattn(n):
            what = f"L{n}_xattn"
            w = {k: matrix(what, f"{what}_{k}") for k in ("Wq", "Wk", "Wv", "Wo")}
            w.update({k: column(what, f"{what}_{k}") for k in ("bq", "bk")})
            w.update({k: row(what, f"{what}_{k}") for k in ("bv", "bo")})
            return w

        w2 = xattn(2)
        scope.append(whole.enter_context(ExitStack()))
        w0, f0 = xattn(0), {}
        for k in ("gate", "up"):
            f0[k] = sb(f"L0_ffn_{k}", [P, FC0, D])[:, :, :]
            src, full = a[f"L0_ffn_w_{k}"], F0 // P * P
            loading("L0_ffn", f0[k][:, 0:F0 // P, :], src[0:full, :].rearrange("(c p) n -> p c n", p=P))
            loading("L0_ffn", f0[k][0:F0 - full, F0 // P, :], src[full:F0, :])
        f0["down"] = sb("L0_ffn_down", [P, DC, FC0 * P])[:, :, :]
        loading("L0_ffn", f0["down"][:, :, 0:F0], a["L0_ffn_w_down"].rearrange("(c p) n -> p c n", p=P))
        f0.update({k: row("L0_ffn", f"L0_ffn_{k}") for k in ("clip_x", "clip_down")})
        w1 = xattn(1)
        f1 = {k: matrix("L1_ffn", f"L1_ffn_{k}") for k in ("w1", "w2")}
        f1.update({k: row("L1_ffn", f"L1_ffn_{k}") for k in ("b1", "b2")})
        first = [load for load in g.loads if load[2] in ("L0_xattn", "mask")]
        later = [load for load in g.loads if load[2] not in ("L0_xattn", "mask")]
        later.sort(key=lambda load: load[2][:2] == "L2")
        setup(nc, g, a, first)
        attention(nc, g, "L0a", PLAIN, w0, None, ["L0_xattn"], later)
        fake_quant_ffn(nc, g, f0)
        turned_attention(nc, g, "L1a", PRUNED, w1, ["L1_xattn"])
        bitlinear_ffn(nc, g, f1)
        scope.pop().close()

        scope.append(whole.enter_context(ExitStack()))
        g.loads = []
        f2 = {k: matrix("L2_ffn", f"L2_ffn_{k}") for k in ("wi", "wo")}
        f2["lora_A"] = load("L2_ffn", "L2_ffn_lora_A", [P, D], a["L2_ffn_lora_A"].rearrange("e r d -> (e r) d"))
        f2["gate_w"] = load("L2_ffn", "L2_ffn_gate_w", [8, D], a["L2_ffn_gate_w"])
        f2["lora_B"] = sb("L2_ffn_lora_B", [P, 8, P])[:, :, :]
        for f in range(8):
            loading("L2_ffn", f2["lora_B"][:, f, :].rearrange("p (e r) -> p e r", e=8),
                    a["L2_ffn_lora_B"][:, f * P:f * P + P, :].rearrange("e p r -> p e r"))
        f2["bi"] = column("L2_ffn", "L2_ffn_bi")
        f2.update({k: row("L2_ffn", f"L2_ffn_{k}") for k in ("bo", "gate_b")})
        a3 = {k: matrix("L3_xattn", f"L3_xattn_{k}") for k in ("q_w", "k_w", "gate_w")}
        a3.update({k: row("L3_xattn", f"L3_xattn_{k}") for k in ("norm_w", "gate_b")})
        E3, g.mixed_at, g.mixw = 4, {}, 0
        for k in ("Wk", "bk", "bq", "Wq", "Wv", "bv"):
            g.mixed_at[k] = g.mixw
            g.mixw += DC * D if k[0] == "W" else D if k == "bv" else DC
        g.mixk = g.mixed_at["Wq"]
        g.experts = sb("experts", [P, E3, g.mixw])
        for e in range(E3):
            for k, at in g.mixed_at.items():
                src = a[f"L3_ffn_{k}"][e]
                if k[0] == "W":
                    loading("L3_ffn", g.experts[:, e, at:at + DC * D].rearrange("p (c n) -> p c n", c=DC),
                            src.rearrange("(c p) n -> p c n", p=P))
                elif k == "bv":
                    loading("L3_ffn", g.experts[:, e, at:at + D], src.partition_broadcast(P))
                else:
                    loading("L3_ffn", g.experts[:, e, at:at + DC], src.rearrange("(c p) -> p c", p=P))
        f3 = {k: matrix("L3_ffn", f"L3_ffn_{k}") for k in ("Wo", "Wg1", "Wg2")}
        f3.update({k: row("L3_ffn", f"L3_ffn_{k}") for k in ("bo", "bg2")})
        f3["bg1"] = column("L3_ffn", "L3_ffn_bg1")
        turned_attention(nc, g, "L2a", MASKED, w2, ["L2_xattn"], g.loads)
        lora_ffn(nc, g, f2)
        gated_attention(nc, g, a3, a["ctx_1024"])
        expert_gates(nc, g, f3)
        attention(nc, g, "L3f", MIXED, f3, None, ["L3_ffn"])
        finish(nc, g, out)


def turned_attention(nc, g, name, kind, w, needs, later=()):
    with ExitStack() as ctx:
        t, lots = dict(w), []
        for k in ("Wq", "Wk", "Wv", "Wo"):
            t[k] = ctx.enter_context(nc.sbuf_tensor(f"{name}_{k}T", [P, DC, D], F32))[:, :, :]
            lots.append(square_lot(w[k], t[k]))
        attention(nc, g, name, kind, t, lots, needs, later)


_INS = ['x', 'ctx_1024', 'mask_1x1xSxS2_bk0'] + [f'L{n}_xattn_{k}' for n in range(3) for k in (
    'Wq', 'bq', 'Wk', 'bk', 'Wv', 'bv', 'Wo', 'bo')] + [f'L0_ffn_{k}' for k in (
        'clip_x', 'clip_down', 'w_gate', 'w_up', 'w_down')] + [f'L1_ffn_{k}' for k in ('w1', 'b1', 'w2', 'b2')] + [
    f'L2_ffn_{k}' for k in ('wi', 'bi', 'wo', 'bo', 'lora_A', 'lora_B', 'gate_w', 'gate_b')] + [
    f'L3_xattn_{k}' for k in ('q_w', 'k_w', 'norm_w', 'gate_w', 'gate_b')] + [f'L3_ffn_{k}' for k in (
        'Wq', 'bq', 'Wk', 'bk', 'Wv', 'bv', 'Wg1', 'bg1', 'Wg2', 'bg2', 'Wo', 'bo')]


def kernel(**inputs):
    import numpy as np
    import concourse.bacc as bacc
    from concourse.bass_utils import run_bass_kernel_spmd

    nc = bacc.Bacc("TRN2", target_bir_lowering=False, num_devices=1)
    arrays, aps = {}, {}
    for name in _INS:
        x = np.ascontiguousarray(inputs[name])
        arrays[f"in_{name}"] = x
        aps[name] = nc.dram_tensor(f"in_{name}", x.shape, mybir.dt.from_np(x.dtype), kind="ExternalInput").ap()
    out = nc.dram_tensor("out", (NB, P, D), F32, kind="ExternalOutput").ap()
    program(nc, aps, out)
    r = run_bass_kernel_spmd(nc, [arrays], core_ids=[0])
    return r.results[0]["out"]
```
